# Optimizing a Trainium2 kernel written in Bass

```python
import numpy as np
import jax
import jax.numpy as jnp

def _softmax(x, axis=-1):
    return jax.nn.softmax(x, axis=axis)

def _gelu(x):
    return jax.nn.gelu(x, approximate=True)

def _silu(x):
    return jax.nn.silu(x)

def _sigmoid(x):
    return jax.nn.sigmoid(x)

def _layernorm(x, axis=-1, eps=1e-05):
    m = jnp.mean(x, axis=axis, keepdims=True)
    v = jnp.var(x, axis=axis, keepdims=True)
    return (x - m) / jnp.sqrt(v + eps)

def _scatter_add(tgt, idx, src, axis=0):
    return tgt.at[idx].add(src)

def _segment_sum(src, seg, n):
    return jax.ops.segment_sum(src, seg, n)
kernel_name = 'mk_macaron_d2_jaxref_r8_e247c4'

def setup_inputs(seed: int=0):
    np.random.seed(seed)
    _w = jnp.asarray

    def _L0_attn_setup():
        import jax, jax.numpy as jnp
        import numpy as np
        D_MODEL = 128
        E = 4
        D_STATE = 128
        HEADDIM = 64
        EXPAND = 2
        D_CONV = 4
        CHUNK = 64
        D_INNER = EXPAND * D_MODEL
        NHEADS = D_INNER // HEADDIM
        CONV_DIM = D_INNER + 2 * D_STATE
        D_IN_PROJ = 2 * D_INNER + 2 * D_STATE + NHEADS

        def _segsum(a):
            l = a.shape[-1]
            cs = jnp.cumsum(a, -1)
            S = cs[..., :, None] - cs[..., None, :]
            return jnp.where(jnp.tril(jnp.ones((l, l), bool)), S, -jnp.inf)

        def _ssd(xdt, a, Bm, Cm):
            b, t, h, p = xdt.shape
            n = Bm.shape[-1]
            c, l = (t // CHUNK, CHUNK)
            xdt = xdt.reshape(b, c, l, h, p)
            a = a.reshape(b, c, l, h).transpose(0, 3, 1, 2)
            Bm = Bm.reshape(b, c, l, n)
            Cm = Cm.reshape(b, c, l, n)
            acs = jnp.cumsum(a, -1)
            L = jnp.exp(_segsum(a))
            Yd = jnp.einsum('bcln,bcsn,bhcls,bcshp->bclhp', Cm, Bm, L, xdt)
            decay_states = jnp.exp(acs[..., -1:] - acs)
            states = jnp.einsum('bcln,bhcl,bclhp->bchpn', Bm, decay_states, xdt)
            chunk_decay = jnp.exp(acs[..., -1])

            def step(hprev, inp):
                st, dec = inp
                return (st + dec[..., None, None] * hprev, hprev)
            _, prev = jax.lax.scan(step, jnp.zeros((b, h, p, n), xdt.dtype), (states.transpose(1, 0, 2, 3, 4), chunk_decay.transpose(2, 0, 1)))
            Yoff = jnp.einsum('bcln,cbhpn,bhcl->bclhp', Cm, prev, jnp.exp(acs))
            return (Yd + Yoff).reshape(b, t, h, p)

        def _expert(x, in_w, conv_w, conv_b, dt_bias, A_log, D_skip, norm_w, out_w):
            B, T, _ = x.shape
            zxbcdt = x @ in_w
            z = zxbcdt[..., :D_INNER]
            xBC = zxbcdt[..., D_INNER:D_INNER + CONV_DIM]
            dt = jax.nn.softplus(zxbcdt[..., -NHEADS:] + dt_bias)
            xp = jnp.pad(xBC, ((0, 0), (D_CONV - 1, 0), (0, 0)))
            xBC = sum((xp[:, k:k + T, :] * conv_w[:, k] for k in range(D_CONV))) + conv_b
            xBC = jax.nn.silu(xBC)
            xs = xBC[..., :D_INNER].reshape(B, T, NHEADS, HEADDIM)
            Bm = xBC[..., D_INNER:D_INNER + D_STATE]
            Cm = xBC[..., D_INNER + D_STATE:]
            A = -jnp.exp(A_log)
            y = _ssd(xs * dt[..., None], dt * A, Bm, Cm)
            y = y + D_skip[None, None, :, None] * xs
            y = y.reshape(B, T, D_INNER)
            y = y * jax.nn.silu(z)
            y = y * jax.lax.rsqrt(jnp.mean(y * y, -1, keepdims=True) + 1e-05) * norm_w
            return y @ out_w
        key = jax.random.key(seed)
        ks = jax.random.split(key, 8)
        B, T = (2, 256)
        x = jax.random.normal(ks[0], (B, T, D_MODEL), jnp.float32)
        s = lambda k, shape, fan: jax.random.normal(k, shape, jnp.float32) / np.sqrt(fan).astype(np.float32)
        in_w = s(ks[1], (E, D_MODEL, D_IN_PROJ), D_MODEL)
        conv_w = s(ks[2], (E, CONV_DIM, D_CONV), D_CONV)
        conv_b = jnp.zeros((E, CONV_DIM), jnp.float32)
        dt0 = jax.random.uniform(ks[3], (E, NHEADS), jnp.float32, 0.001, 0.1)
        dt_bias = jnp.log(jnp.expm1(dt0))
        A_log = jnp.log(jax.random.uniform(ks[4], (E, NHEADS), jnp.float32, 1.0, 16.0))
        D_skip = jnp.ones((E, NHEADS), jnp.float32)
        norm_w = jnp.ones((E, D_INNER), jnp.float32)
        out_w = s(ks[5], (E, D_INNER, D_MODEL), D_INNER)
        router_w = s(ks[6], (D_MODEL, E), D_MODEL)
        return dict(x=x, router_w=router_w, in_w=in_w, conv_w=conv_w, conv_b=conv_b, dt_bias=dt_bias, A_log=A_log, D_skip=D_skip, norm_w=norm_w, out_w=out_w)
    _L0_attn_in = _L0_attn_setup()

    def _L0_ffn_setup():
        import jax, jax.numpy as jnp
        import numpy as np
        HIDDEN = 128
        INTER = 512
        N_EXPERTS = 8

        def geglu(x, w1, w2, w3):
            return jax.nn.gelu(x @ w1, approximate=False) * (x @ w2) @ w3
        key = jax.random.key(seed)
        ks = jax.random.split(key, 8)
        s = 0.02
        x = jax.random.normal(ks[0], (2, 256, HIDDEN), dtype=jnp.float32)
        w1s = jax.random.normal(ks[1], (HIDDEN, INTER), dtype=jnp.float32) * s
        w2s = jax.random.normal(ks[2], (HIDDEN, INTER), dtype=jnp.float32) * s
        w3s = jax.random.normal(ks[3], (INTER, HIDDEN), dtype=jnp.float32) * s
        W1 = jax.random.normal(ks[4], (N_EXPERTS, HIDDEN, INTER), dtype=jnp.float32) * s
        W2 = jax.random.normal(ks[5], (N_EXPERTS, HIDDEN, INTER), dtype=jnp.float32) * s
        W3 = jax.random.normal(ks[6], (N_EXPERTS, INTER, HIDDEN), dtype=jnp.float32) * s
        Wg = jax.random.normal(ks[7], (HIDDEN, N_EXPERTS), dtype=jnp.float32) * s
        return {'x': x, 'w1s': w1s, 'w2s': w2s, 'w3s': w3s, 'W1': W1, 'W2': W2, 'W3': W3, 'Wg': Wg}
    _L0_ffn_in = _L0_ffn_setup()

    def _L1_attn_setup():
        import jax, jax.numpy as jnp
        import numpy as np
        N_EMBD = 128
        QK_DIM = 16
        key = jax.random.key(seed)
        k1, k2, k3, k4, k5 = jax.random.split(key, 5)
        b, s = (8, 256)
        lim = 1.0 / np.sqrt(N_EMBD)
        return {'x': jax.random.normal(k1, (b, s, N_EMBD), dtype=jnp.float32), 'w_q': jax.random.uniform(k2, (QK_DIM, N_EMBD), minval=-lim, maxval=lim, dtype=jnp.float32), 'b_q': jax.random.uniform(k3, (QK_DIM,), minval=-lim, maxval=lim, dtype=jnp.float32), 'w_k': jax.random.uniform(k4, (QK_DIM, N_EMBD), minval=-lim, maxval=lim, dtype=jnp.float32), 'b_k': jax.random.uniform(k5, (QK_DIM,), minval=-lim, maxval=lim, dtype=jnp.float32)}
    _L1_attn_in = _L1_attn_setup()

    def _L1_ffn_setup():
        import jax, jax.numpy as jnp
        import numpy as np
        D_MODEL, D_FF, N_EXPERTS, TOP_K = (128, 512, 8, 2)
        B, S = (2, 256)
        key = jax.random.key(seed)
        ks = jax.random.split(key, 7)
        scale = 0.02
        return {'x': jax.random.normal(ks[0], (B, S, D_MODEL), dtype=jnp.float32), 'W1': jax.random.normal(ks[1], (N_EXPERTS, D_MODEL, D_FF), dtype=jnp.float32) * scale, 'b1': jnp.zeros((N_EXPERTS, D_FF), dtype=jnp.float32), 'W2': jax.random.normal(ks[2], (N_EXPERTS, D_FF, D_MODEL), dtype=jnp.float32) * scale, 'b2': jnp.zeros((N_EXPERTS, D_MODEL), dtype=jnp.float32), 'Wg': jax.random.normal(ks[3], (D_MODEL, N_EXPERTS), dtype=jnp.float32) * scale, 'bg': jnp.zeros((N_EXPERTS,), dtype=jnp.float32)}
    _L1_ffn_in = _L1_ffn_setup()
    _d = {'L0_attn_x': _L0_attn_in['x'], 'L0_attn_router_w': _L0_attn_in['router_w'], 'L0_attn_in_w': _L0_attn_in['in_w'], 'L0_attn_conv_w': _L0_attn_in['conv_w'], 'L0_attn_conv_b': _L0_attn_in['conv_b'], 'L0_attn_dt_bias': _L0_attn_in['dt_bias'], 'L0_attn_A_log': _L0_attn_in['A_log'], 'L0_attn_D_skip': _L0_attn_in['D_skip'], 'L0_attn_norm_w': _L0_attn_in['norm_w'], 'L0_attn_out_w': _L0_attn_in['out_w'], 'L0_ffn_w1s': _L0_ffn_in['w1s'], 'L0_ffn_w2s': _L0_ffn_in['w2s'], 'L0_ffn_w3s': _L0_ffn_in['w3s'], 'L0_ffn_W1': _L0_ffn_in['W1'], 'L0_ffn_W2': _L0_ffn_in['W2'], 'L0_ffn_W3': _L0_ffn_in['W3'], 'L0_ffn_Wg': _L0_ffn_in['Wg'], 'L1_attn_w_q': _L1_attn_in['w_q'], 'L1_attn_b_q': _L1_attn_in['b_q'], 'L1_attn_w_k': _L1_attn_in['w_k'], 'L1_attn_b_k': _L1_attn_in['b_k'], 'L1_ffn_W1': _L1_ffn_in['W1'], 'L1_ffn_b1': _L1_ffn_in['b1'], 'L1_ffn_W2': _L1_ffn_in['W2'], 'L1_ffn_b2': _L1_ffn_in['b2'], 'L1_ffn_Wg': _L1_ffn_in['Wg'], 'L1_ffn_bg': _L1_ffn_in['bg']}
    _x0 = _d['L0_attn_x']
    _d['L0_attn_x'] = jax.random.normal(jax.random.fold_in(jax.random.key(seed), 1), (4, 1024, 128), dtype=_x0.dtype)
    del _x0
    return _d

def reference(L0_attn_x, L0_attn_router_w, L0_attn_in_w, L0_attn_conv_w, L0_attn_conv_b, L0_attn_dt_bias, L0_attn_A_log, L0_attn_D_skip, L0_attn_norm_w, L0_attn_out_w, L0_ffn_w1s, L0_ffn_w2s, L0_ffn_w3s, L0_ffn_W1, L0_ffn_W2, L0_ffn_W3, L0_ffn_Wg, L1_attn_w_q, L1_attn_b_q, L1_attn_w_k, L1_attn_b_k, L1_ffn_W1, L1_ffn_b1, L1_ffn_W2, L1_ffn_b2, L1_ffn_Wg, L1_ffn_bg):

    def _L0_attn_ref(x, router_w, in_w, conv_w, conv_b, dt_bias, A_log, D_skip, norm_w, out_w):
        import jax, jax.numpy as jnp
        import numpy as np
        D_MODEL = 128
        E = 4
        D_STATE = 128
        HEADDIM = 64
        EXPAND = 2
        D_CONV = 4
        CHUNK = 64
        D_INNER = EXPAND * D_MODEL
        NHEADS = D_INNER // HEADDIM
        CONV_DIM = D_INNER + 2 * D_STATE
        D_IN_PROJ = 2 * D_INNER + 2 * D_STATE + NHEADS

        def _segsum(a):
            l = a.shape[-1]
            cs = jnp.cumsum(a, -1)
            S = cs[..., :, None] - cs[..., None, :]
            return jnp.where(jnp.tril(jnp.ones((l, l), bool)), S, -jnp.inf)

        def _ssd(xdt, a, Bm, Cm):
            b, t, h, p = xdt.shape
            n = Bm.shape[-1]
            c, l = (t // CHUNK, CHUNK)
            xdt = xdt.reshape(b, c, l, h, p)
            a = a.reshape(b, c, l, h).transpose(0, 3, 1, 2)
            Bm = Bm.reshape(b, c, l, n)
            Cm = Cm.reshape(b, c, l, n)
            acs = jnp.cumsum(a, -1)
            L = jnp.exp(_segsum(a))
            Yd = jnp.einsum('bcln,bcsn,bhcls,bcshp->bclhp', Cm, Bm, L, xdt)
            decay_states = jnp.exp(acs[..., -1:] - acs)
            states = jnp.einsum('bcln,bhcl,bclhp->bchpn', Bm, decay_states, xdt)
            chunk_decay = jnp.exp(acs[..., -1])

            def step(hprev, inp):
                st, dec = inp
                return (st + dec[..., None, None] * hprev, hprev)
            _, prev = jax.lax.scan(step, jnp.zeros((b, h, p, n), xdt.dtype), (states.transpose(1, 0, 2, 3, 4), chunk_decay.transpose(2, 0, 1)))
            Yoff = jnp.einsum('bcln,cbhpn,bhcl->bclhp', Cm, prev, jnp.exp(acs))
            return (Yd + Yoff).reshape(b, t, h, p)

        def _expert(x, in_w, conv_w, conv_b, dt_bias, A_log, D_skip, norm_w, out_w):
            B, T, _ = x.shape
            zxbcdt = x @ in_w
            z = zxbcdt[..., :D_INNER]
            xBC = zxbcdt[..., D_INNER:D_INNER + CONV_DIM]
            dt = jax.nn.softplus(zxbcdt[..., -NHEADS:] + dt_bias)
            xp = jnp.pad(xBC, ((0, 0), (D_CONV - 1, 0), (0, 0)))
            xBC = sum((xp[:, k:k + T, :] * conv_w[:, k] for k in range(D_CONV))) + conv_b
            xBC = jax.nn.silu(xBC)
            xs = xBC[..., :D_INNER].reshape(B, T, NHEADS, HEADDIM)
            Bm = xBC[..., D_INNER:D_INNER + D_STATE]
            Cm = xBC[..., D_INNER + D_STATE:]
            A = -jnp.exp(A_log)
            y = _ssd(xs * dt[..., None], dt * A, Bm, Cm)
            y = y + D_skip[None, None, :, None] * xs
            y = y.reshape(B, T, D_INNER)
            y = y * jax.nn.silu(z)
            y = y * jax.lax.rsqrt(jnp.mean(y * y, -1, keepdims=True) + 1e-05) * norm_w
            return y @ out_w
        routing = jax.nn.softmax(x @ router_w, axis=-1)
        outs = jax.vmap(_expert, in_axes=(None, 0, 0, 0, 0, 0, 0, 0, 0))(x, in_w, conv_w, conv_b, dt_bias, A_log, D_skip, norm_w, out_w)
        return jnp.einsum('ebtd,bte->btd', outs, routing)

    def _L0_ffn_ref(x, w1s, w2s, w3s, W1, W2, W3, Wg):
        import jax, jax.numpy as jnp
        import numpy as np
        HIDDEN = 128
        INTER = 512
        N_EXPERTS = 8

        def geglu(x, w1, w2, w3):
            return jax.nn.gelu(x @ w1, approximate=False) * (x @ w2) @ w3
        B, T, C = x.shape
        xf = x.reshape(-1, C)
        shared = geglu(xf, w1s, w2s, w3s)
        logits = xf @ Wg
        idx = jnp.argmax(logits, axis=-1)
        final = jnp.zeros_like(xf)
        for e in range(N_EXPERTS):
            y = geglu(xf, W1[e], W2[e], W3[e])
            final = final + jnp.where((idx == e)[:, None], y, 0.0)
        return (shared + final).reshape(B, T, C)

    def _L1_attn_ref(x, w_q, b_q, w_k, b_k):
        import jax, jax.numpy as jnp
        import numpy as np
        N_EMBD = 128
        QK_DIM = 16
        s = x.shape[-2]
        q = jnp.einsum('bsd,ed->bse', x, w_q) + b_q
        k = jnp.einsum('bsd,ed->bse', x, w_k) + b_k
        scale = 1.0 / jnp.sqrt(jnp.asarray(QK_DIM, dtype=x.dtype))
        mask = jnp.arange(s)[:, None] >= jnp.arange(s)[None, :]
        scores = jnp.einsum('bqe,bke->bqk', q, k) * scale
        scores = jnp.where(mask[None], scores, jnp.asarray(-10000.0, dtype=x.dtype))
        probs = jax.nn.softmax(scores, axis=-1)
        return jnp.einsum('bqk,bkv->bqv', probs, x)

    def _L1_ffn_ref(x, W1, b1, W2, b2, Wg, bg):
        import jax, jax.numpy as jnp
        import numpy as np
        D_MODEL, D_FF, N_EXPERTS, TOP_K = (128, 512, 8, 2)
        B, S = (2, 256)
        Bx, Sx, d = x.shape
        E = W1.shape[0]
        logits = jnp.einsum('bsd,de->bse', x, Wg) + bg
        topk_scores, topk_idx = jax.lax.top_k(logits, TOP_K)
        topk_scores = jax.nn.softmax(topk_scores, axis=-1)
        tokens = x.reshape(-1, d)
        idx_flat = topk_idx.reshape(-1, TOP_K)
        sc_flat = topk_scores.reshape(-1, TOP_K)
        comb = (jax.nn.one_hot(idx_flat, E, dtype=x.dtype) * sc_flat[..., None]).sum(axis=1)
        h = jnp.einsum('td,edf->etf', tokens, W1) + b1[:, None, :]
        even = (jnp.arange(E) % 2 == 0)[:, None, None]
        a = jnp.where(even, jax.nn.gelu(h, approximate=False), jax.nn.silu(h))
        y = jnp.einsum('etf,efd->etd', a, W2) + b2[:, None, :]
        out = jnp.einsum('te,etd->td', comb, y)
        return out.reshape(Bx, Sx, d)
    x = L0_attn_x
    x = x + 0.5 * _L0_ffn_ref(_layernorm(x, axis=-1), L0_ffn_w1s, L0_ffn_w2s, L0_ffn_w3s, L0_ffn_W1, L0_ffn_W2, L0_ffn_W3, L0_ffn_Wg)
    x = x + _L0_attn_ref(_layernorm(x, axis=-1), L0_attn_router_w, L0_attn_in_w, L0_attn_conv_w, L0_attn_conv_b, L0_attn_dt_bias, L0_attn_A_log, L0_attn_D_skip, L0_attn_norm_w, L0_attn_out_w)
    x = x + 0.5 * _L0_ffn_ref(_layernorm(x, axis=-1), L0_ffn_w1s, L0_ffn_w2s, L0_ffn_w3s, L0_ffn_W1, L0_ffn_W2, L0_ffn_W3, L0_ffn_Wg)
    x = x + 0.5 * _L1_ffn_ref(_layernorm(x, axis=-1), L1_ffn_W1, L1_ffn_b1, L1_ffn_W2, L1_ffn_b2, L1_ffn_Wg, L1_ffn_bg)
    x = x + _L1_attn_ref(_layernorm(x, axis=-1), L1_attn_w_q, L1_attn_b_q, L1_attn_w_k, L1_attn_b_k)
    x = x + 0.5 * _L1_ffn_ref(_layernorm(x, axis=-1), L1_ffn_W1, L1_ffn_b1, L1_ffn_W2, L1_ffn_b2, L1_ffn_Wg, L1_ffn_bg)
    return x

_drawn_inputs = setup_inputs


def setup_inputs(seed=0):
    import zlib

    import numpy as np

    out = dict(_drawn_inputs(seed))
    spreads = {'L0_attn_conv_b': (0.0, 0.1),
     'L0_attn_D_skip': (1.0, 0.2),
     'L0_attn_norm_w': (1.0, 0.2),
     'L1_ffn_b1': (0.0, 0.494),
     'L1_ffn_b2': (0.0, 0.1),
     'L1_ffn_bg': (0.0, 0.1)}
    factors = {'L0_ffn_w1s': 4.843,
     'L0_ffn_w2s': 4.718,
     'L0_ffn_w3s': 4.748,
     'L0_ffn_W1': 5.196,
     'L0_ffn_W2': 5.109,
     'L0_ffn_W3': 5.119,
     'L0_ffn_Wg': 5.503,
     'L1_attn_b_q': 36.939,
     'L1_attn_b_k': 64.0,
     'L1_attn_w_q': 3.114,
     'L1_ffn_W1': 3.255}
    for name, (base, spread) in spreads.items():
        noise = np.random.default_rng([zlib.crc32(name.encode()), seed]).standard_normal(out[name].shape)
        drawn = base * np.exp(spread * noise) if base else spread * noise
        out[name] = jnp.asarray(drawn.astype(out[name].dtype))
    for name, factor in factors.items():
        out[name] = (out[name] * factor).astype(out[name].dtype)
    return out
```

```python
import numpy as np
import concourse.bass as bass
from concourse import mybir
from contextlib import ExitStack

F32 = mybir.dt.float32
BF16 = mybir.dt.bfloat16
I32 = mybir.dt.int32
U32 = mybir.dt.uint32
ALU = mybir.AluOpType
ACT = mybir.ActivationFunctionType
AX = mybir.AxisListType
ds = bass.ds

STAGES = ("ffn0", "mamba", "ffn0", "ffn1", "attn", "ffn1")

P = 128
D = 128
BATCH, SEQ = 4, 1024
TOK = BATCH * SEQ
NT = TOK // P
GRP = 4
NG = NT // GRP
NE = 8
FF = 512
FB = FF // P
EPS = 1e-5
ME, MH = 4, 4
ZW, CW = 256, 512
HD = ZW // MH
MEH = ME * MH
NM = ME + MEH
TAPS = 4
QK = 16
LEAD = 4


class Signal:

    def __init__(self, nc, ctx, name, unit=1, lead=LEAD):
        self.sem = ctx.enter_context(nc.semaphore(name))
        self.unit = unit
        self.base = self.lead = lead * unit

    def at(self, n):
        return n * self.unit + self.base

    def close(self, total):
        self.base += total * self.unit


class Bench:

    def __init__(self, nc, ctx):
        self.nc, self.ctx, self.counters, self.new, self.stages = nc, ctx, {}, [], 0

    def sb(self, name, shape, dt=F32):
        return self.ctx.enter_context(self.nc.sbuf_tensor(name, shape, dt))

    def scope(self, stack):
        self.stages += 1
        tag = self.stages
        return lambda name, shape, dt=F32: stack.enter_context(self.nc.sbuf_tensor(f"{name}_{tag}", shape, dt))

    def counter(self, name, unit=1, lead=LEAD):
        if name not in self.counters:
            self.counters[name] = Signal(self.nc, self.ctx, name, unit, lead)
            self.new.append(self.counters[name])
        return self.counters[name]

    def settle(self, eng):
        eng.sem_inc(self.counters["settled"].sem, 1)

    def start(self):
        if self.new:
            with self.nc.Block() as block:
                @block.sync
                def _(sp):
                    for s in self.new:
                        if s.lead:
                            sp.sem_inc(s.sem, s.lead)
            self.new = []


def bcast(ap, axis, n):
    shape = list(ap.shape)
    return ap.unsqueeze(axis).to_broadcast(shape[:axis] + [n] + shape[axis:])


class Chain:

    def __init__(self, eng, signal, start=0):
        self.eng, self.count, self.n = eng, signal, start

    def __call__(self, ins):
        self.n += 1
        ins.then_inc(self.count.sem, 1)
        self.eng.wait_ge(self.count.sem, self.count.at(self.n))


def prepare(k, router, nr, loads):
    weights_in = k.counter("weights_in", 16)
    nc = k.nc
    var_ready, rstd_ready, xn_ready = (k.counter(n) for n in ("prep_var_ready", "prep_rstd_ready", "prep_xn_ready"))
    own, pool_own = k.counter("prep_vector_step"), k.counter("prep_pool_step")
    transposed, xt_copied, routed, logits_kept = (
        k.counter(n) for n in ("prep_transposed", "prep_xt_copied", "prep_routed", "prep_logits_kept"))
    stored = [k.counter(f"prep_stored{r}", 16) for r in range(2)]
    x, xn4, xt4, xnT, stat, mv, rstd = k.x, k.xn4, k.xt4, k.xnT, k.stat, k.mv, k.rstd
    rows = k.xn_rows.rearrange("(g j p) d -> p g j d", p=P, j=GRP)
    ps_t, ps_r = k.ps[:, 0:2, :], k.ps[:, 2:4, :]

    k.start()
    with nc.Block() as block:
        @block.vector
        def _(dve):
            with dve.Fori(0, NG // 2) as i:
                for r in range(2):
                    g = i * 2 + r
                    for j in range(GRP):
                        ins = nc.vector.bn_stats(stat[:, r, j, :], x[:, ds((g * GRP + j) * D, D)])
                    ins.then_inc(own.sem, 1)
                    dve.wait_ge(own.sem, own.at(g + 1))
                    k.settle(dve)
                    for j in range(GRP):
                        ins = nc.vector.bn_aggr(mv[:, r, j, :], stat[:, r, j, :])
                    ins.then_inc(var_ready.sem, 1)
                    dve.wait_ge(rstd_ready.sem, rstd_ready.at(g + 1))
                    dve.wait_ge(transposed.sem, transposed.at(g - 1))
                    dve.wait_ge(stored[r].sem, stored[r].at(i))
                    for j in range(GRP):
                        ins = nc.vector.tensor_scalar(xn4[:, r, j, :], x[:, ds((g * GRP + j) * D, D)],
                                                      mv[:, r, j, 0:1], rstd[:, r, j:j + 1],
                                                      ALU.subtract, ALU.mult)
                    ins.then_inc(xn_ready.sem, 1)
                    if nr:
                        dve.wait_ge(routed.sem, routed.at(g + 1))
                        nc.vector.tensor_copy(k.logits[:, ds(g * GRP * nr, GRP * nr)], ps_r[:, r, 0:GRP * nr]
                                              ).then_inc(logits_kept.sem, 1)
            if nr:
                dve.wait_ge(logits_kept.sem, logits_kept.at(NG))

        @block.gpsimd
        def _(pool):
            with pool.Fori(0, NG // 2) as i:
                for r in range(2):
                    g = i * 2 + r
                    pool.wait_ge(var_ready.sem, var_ready.at(g + 1))
                    pool.wait_ge(xn_ready.sem, xn_ready.at(g - 1))
                    nc.gpsimd.tensor_tensor(rstd[:, r, :], mv[:, r, :, 1], k.eps[:, 0:GRP], ALU.add).then_inc(pool_own.sem, 1)
                    pool.wait_ge(pool_own.sem, pool_own.at(g + 1))
                    nc.gpsimd.tensor_tensor(rstd[:, r, :], rstd[:, r, :], k.minus_half[:, 0:GRP],
                                            ALU.pow).then_inc(rstd_ready.sem, 1)

        @block.sync
        def _(sp):
            for dst, src in loads:
                sp.dma_start(dst, src, allow_slow_non_contiguous=True).then_inc(weights_in.sem, 16)
            with sp.Fori(0, NG // 2) as i:
                for r in range(2):
                    g = i * 2 + r
                    sp.wait_ge(xn_ready.sem, xn_ready.at(g + 1))
                    sp.wait_ge(stored[r].sem, stored[r].at(i))
                    sp.dma_start(rows[:, ds(g, 1)].rearrange("p g j d -> p (g j) d"), xn4[:, r, :, :]).then_inc(stored[r].sem, 16)
            for r in range(2):
                sp.wait_ge(stored[r].sem, stored[r].at(NG // 2))
            sp.wait_ge(weights_in.sem, weights_in.at(len(loads)))

        @block.tensor
        def _(pe):
            with pe.Fori(0, NG // 2) as i:
                for r in range(2):
                    g = i * 2 + r
                    pe.wait_ge(xn_ready.sem, xn_ready.at(g + 1))
                    pe.wait_ge(xt_copied.sem, xt_copied.at(g - 1))
                    for j in range(GRP):
                        ins = nc.tensor.transpose(ps_t[:, r, j * P:(j + 1) * P], xn4[:, r, j, :], k.ident[:, :])
                    ins.then_inc(transposed.sem, 1)
                    if nr:
                        pe.wait_ge(xt_copied.sem, xt_copied.at(g + 1))
                        pe.wait_ge(logits_kept.sem, logits_kept.at(g - 1))
                        for j in range(GRP):
                            ins = nc.tensor.matmul(ps_r[:, r, j * nr:(j + 1) * nr], xt4[:, r, j * P:(j + 1) * P],
                                                   router, start=True, stop=True)
                        ins.then_inc(routed.sem, 1)

        @block.scalar
        def _(act):
            with act.Fori(0, NG // 2) as i:
                for r in range(2):
                    g = i * 2 + r
                    act.wait_ge(transposed.sem, transposed.at(g + 1))
                    if nr:
                        act.wait_ge(routed.sem, routed.at(g - 1))
                        nc.scalar.copy(xt4[:, r, :], ps_t[:, r, :])
                    nc.scalar.copy(xnT[:, ds(g * GRP * P, GRP * P)], ps_t[:, r, :]).then_inc(xt_copied.sem, 1)
            act.wait_ge(xt_copied.sem, xt_copied.at(NG))

    weights_in.close(len(loads))
    for s in (var_ready, rstd_ready, xn_ready, pool_own, transposed, xt_copied):
        s.close(NG)
    own.close(NG)
    if nr:
        routed.close(NG)
        logits_kept.close(NG)
    for s in stored:
        s.close(NG // 2)


def route(k, top, slots):
    nc = k.nc
    own = k.counter("route_vector_step")
    marks, counted = k.counter("route_marks_ready"), k.counter("route_counted")
    weights, expd = k.counter("route_difference_ready"), k.counter("route_exp_done")
    onehot, placed = k.counter("route_onehot_ready"), k.counter("route_placed")
    opened = k.counter("route_table_opened")
    L3 = k.logits[:, 0:NT * NE].rearrange("p (t e) -> p t e", e=NE)
    r3 = [k.rt[i][:, :].rearrange("p (t e) -> p t e", e=NE) for i in range(5)]
    e3 = [k.rt[i][:, :].rearrange("p (e t) -> p e t", e=NE) for i in range(5)]
    NP = top * NT
    ps_rank, ps_cnt = k.ps[:, 0, 0:NE * NT], k.ps[:, 1, 0:NE * NT]
    table = k.ps[:, 2, 0:2 * slots]
    V = nc.vector

    k.start()
    with nc.Block() as block:
        @block.vector
        def _(dve):
            do = Chain(dve, own)
            logit, eq, sel = L3, r3[4], [r3[0], r3[1]]
            for c in range(top):
                do(V.tensor_reduce(k.best[:, c, :], logit, AX.X, ALU.max))
                do(V.tensor_tensor(eq, logit, bcast(k.best[:, c, :], 2, NE), ALU.is_equal))
                do(V.tensor_tensor(eq, eq, bcast(k.falling[:, :], 1, NT), ALU.mult))
                do(V.tensor_reduce(k.small[:, 0:NT], eq, AX.X, ALU.max))
                do(V.tensor_tensor(sel[c], eq, bcast(k.small[:, 0:NT], 2, NE), ALU.is_equal))
                if c + 1 < top:
                    do(V.scalar_tensor_tensor(r3[3], sel[c], -1e30, L3, ALU.mult, ALU.add))
                    logit = r3[3]
            if top == 2:
                V.tensor_sub(k.small[:, 0:NT], k.best[:, 1, :], k.best[:, 0, :]).then_inc(weights.sem, 1)
                dve.wait_ge(expd.sem, expd.at(1))
                do(V.tensor_scalar(k.small[:, NT:2 * NT], k.small[:, 0:NT], 1.0, None, ALU.add))
                do(V.reciprocal(k.gate[:, 0, :], k.small[:, NT:2 * NT]))
                do(V.tensor_scalar(k.gate[:, 0, :], k.gate[:, 0, :], 0.5, None, ALU.mult))
                do(V.tensor_mul(k.gate[:, 1, :], k.small[:, 0:NT], k.gate[:, 0, :]))
                do(V.tensor_add(r3[4], sel[0], sel[1]))
                V.tensor_copy(k.marks[:, :].rearrange("p (e t) -> p t e", e=NE), r3[4]).then_inc(marks.sem, 1)
            else:
                V.tensor_copy(k.marks[:, :].rearrange("p (e t) -> p t e", e=NE), sel[0]).then_inc(marks.sem, 1)
            dve.wait_ge(counted.sem, counted.at(1))
            cnt, incl = k.rt[2], k.rt[3]
            do(V.tensor_copy(cnt[:, :], ps_cnt))
            do(V.tensor_tensor_scan(incl[:, :], k.carry[:, :], cnt[:, :], 0.0, ALU.mult, ALU.add))
            do(V.tensor_sub(cnt[:, :], incl[:, :], cnt[:, :]))
            do(V.tensor_tensor(cnt[:, :], cnt[:, :], ps_rank, ALU.add))
            do(V.tensor_scalar(k.n_int[:, :], e3[3][:, :, NT - 1], float(P - 1), None, ALU.add))
            do(V.tensor_single_scalar(k.n_int[:, :], k.n_int[:, :], 7, ALU.arith_shift_right))
            do(V.tensor_copy(k.e8[:, 0, :], k.n_int[:, :]))
            do(V.tensor_tensor_scan(k.e8[:, 1, :], k.ones[:, 0:NE], k.e8[:, 0, :], 0.0, ALU.mult, ALU.add))
            do(V.tensor_sub(k.e8[:, 1, :], k.e8[:, 1, :], k.e8[:, 0, :]))
            do(V.tensor_scalar(k.e8[:, 2, :], k.e8[:, 1, :], float(P), None, ALU.mult))
            do(V.tensor_tensor(e3[3], e3[2], bcast(k.e8[:, 2, :], 2, NT), ALU.add))
            for c in range(top):
                cols = slice(c * NT, (c + 1) * NT)
                do(V.tensor_tensor(r3[4], sel[c], k.rt[3][:, :].rearrange("p (e t) -> p t e", e=NE), ALU.mult))
                do(V.tensor_reduce(k.posf[:, cols], r3[4], AX.X, ALU.add))
            do(V.tensor_copy(k.pos[:, 0:NP], k.posf[:, 0:NP]))
            do(V.tensor_single_scalar(k.hi_int[:, 0:NP], k.pos[:, 0:NP].bitcast(I32), 7, ALU.arith_shift_right))
            do(V.tensor_copy(k.hi[:, 0:NP], k.hi_int[:, 0:NP]))
            do(V.scalar_tensor_tensor(k.lo[:, 0:NP], k.hi[:, 0:NP], -float(P), k.posf[:, 0:NP], ALU.mult, ALU.add))
            do(V.tensor_scalar(k.erow[:, 0:slots], k.iota[:, 0:slots], k.e8[:, 1, 1:2], None, ALU.is_ge))
            for e in range(2, NE):
                do(V.scalar_tensor_tensor(k.erow[:, 0:slots], k.iota[:, 0:slots], k.e8[:, 1, e:e + 1],
                                          k.erow[:, 0:slots], ALU.is_ge, ALU.add))
            do(V.tensor_copy(k.slot_expert[:, 0:slots], k.erow[:, 0:slots]))
            with dve.Fori(0, NP // 2) as i:
                for r in range(2):
                    t = i * 2 + r
                    dve.wait_ge(placed.sem, placed.at(t - 1))
                    V.tensor_scalar(k.oh_lane[:, r, :], k.iota[:, 0:P], k.lo[:, ds(t, 1)], None, ALU.is_equal)
                    V.tensor_scalar(k.oh_slot[:, r, 0:slots], k.iota[:, 0:slots], k.hi[:, ds(t, 1)],
                                    k.lane[:, 0:1], ALU.is_equal, ALU.mult)
                    V.tensor_scalar(k.oh_slot[:, r, slots:2 * slots], k.iota[:, 0:slots], k.hi[:, ds(t, 1)],
                                    k.tile_of[:, ds(t, 1)], ALU.is_equal, ALU.mult).then_inc(onehot.sem, 1)
            dve.wait_ge(placed.sem, placed.at(NP))
            do(V.tensor_copy(k.erow[:, 0:slots], table[:, 0:slots]))
            do(V.scalar_tensor_tensor(k.slot_token[:, 0:slots], table[:, slots:2 * slots], float(P),
                                      k.erow[:, 0:slots], ALU.mult, ALU.add))
            k.route_steps = do.n

        @block.scalar
        def _(act):
            if top == 2:
                act.wait_ge(weights.sem, weights.at(1))
                nc.scalar.activation(k.small[:, 0:NT], k.small[:, 0:NT], ACT.Exp).then_inc(expd.sem, 1)

        @block.tensor
        def _(pe):
            pe.wait_ge(marks.sem, marks.at(1))
            nc.tensor.matmul(ps_rank, k.before[:, :], k.marks[:, :], start=True, stop=True)
            nc.tensor.matmul(ps_cnt, k.ones_bf[:, :], k.marks[:, :], start=True, stop=True).then_inc(counted.sem, 1)
            nc.tensor.matmul(table, k.ones_bf[:, :], k.zeros_bf[:, 0:2 * slots], start=True, stop=False,
                             skip_group_check=True)
            with pe.Fori(0, NP // 2) as i:
                for r in range(2):
                    t = i * 2 + r
                    pe.wait_ge(onehot.sem, onehot.at(t + 1))
                    nc.tensor.matmul(table, k.oh_lane[:, r, :], k.oh_slot[:, r, 0:2 * slots], start=False,
                                     stop=False, skip_group_check=True).then_inc(placed.sem, 1)

    own.close(k.route_steps)
    marks.close(1)
    counted.close(1)
    if top == 2:
        weights.close(1)
        expd.close(1)
    onehot.close(NP)
    placed.close(NP)


def shared(k):
    nc = k.nc
    up, acted, ready, down, added = (k.counter(f"shared_{n}") for n in ("up", "acted", "inner_ready", "down", "added"))
    w12, w3 = k.w12[:, NE, :], k.w3[:, NE]
    h1, h2, py = k.ps[:, 0:2, :], k.ps[:, 2:4, :], k.ps[:, 4:6, :]
    NU = NG * FB

    k.start()
    with nc.Block() as block:
        @block.tensor
        def _(pe):
            def up_block(g, b):
                u, r = g * FB + b, b % 2
                pe.wait_ge(ready.sem, ready.at(u - 1))
                nc.tensor.matmul(h1[:, r, :], w12[:, b * P:(b + 1) * P], k.xnT[:, ds(g * GRP * P, GRP * P)],
                                 start=True, stop=True)
                nc.tensor.matmul(h2[:, r, :], w12[:, FF + b * P:FF + (b + 1) * P],
                                 k.xnT[:, ds(g * GRP * P, GRP * P)], start=True, stop=True).then_inc(up.sem, 1)

            def down_group(g, r):
                pe.wait_ge(ready.sem, ready.at((g + 1) * FB))
                pe.wait_ge(added.sem, added.at(g - 1))
                for j in range(GRP):
                    for b in range(FB):
                        ins = nc.tensor.matmul(py[:, r, j * P:(j + 1) * P], k.inner[:, r, b, j * P:(j + 1) * P],
                                               w3[:, b, :], start=(b == 0), stop=(b == FB - 1))
                ins.then_inc(down.sem, 1)

            for b in range(FB):
                up_block(0, b)
            with pe.Fori(0, NG // 2 - 1) as i:
                for r in range(2):
                    for b in range(FB):
                        up_block(i * 2 + r + 1, b)
                    down_group(i * 2 + r, r)
            for b in range(FB):
                up_block(NG - 1, b)
            down_group(NG - 2, 0)
            down_group(NG - 1, 1)

        @block.scalar
        def _(act):
            with act.Fori(0, NG) as g:
                for b in range(FB):
                    u = g * FB + b
                    act.wait_ge(up.sem, up.at(u + 1))
                    act.wait_ge(ready.sem, ready.at(u - 1))
                    nc.scalar.activation(k.gl[:, b % 2, :], h1[:, b % 2, :], ACT.Gelu).then_inc(acted.sem, 1)

        @block.vector
        def _(dve):
            def inner(g, r):
                dve.wait_ge(down.sem, down.at(g - 1))
                for b in range(FB):
                    u = g * FB + b
                    dve.wait_ge(acted.sem, acted.at(u + 1))
                    nc.vector.tensor_tensor(k.inner[:, r, b, :], k.gl[:, b % 2, :], h2[:, b % 2, :],
                                            ALU.mult).then_inc(ready.sem, 1)

            def add(g, r):
                dve.wait_ge(down.sem, down.at(g + 1))
                xg = k.x[:, ds(g * GRP * D, GRP * D)]
                nc.vector.scalar_tensor_tensor(xg, py[:, r, :], 0.5, xg, ALU.mult, ALU.add).then_inc(added.sem, 1)

            inner(0, 0)
            with dve.Fori(0, NG // 2 - 1) as i:
                inner(i * 2 + 1, 1)
                add(i * 2, 0)
                inner(i * 2 + 2, 0)
                add(i * 2 + 1, 1)
            inner(NG - 1, 1)
            add(NG - 2, 0)
            add(NG - 1, 1)
            dve.wait_ge(added.sem, added.at(NG))

    for s in (up, acted, ready):
        s.close(NU)
    down.close(NG)
    added.close(NG)


def experts(k, top, slots):
    nc = k.nc
    gathered = [k.counter(f"slot_gathered{r}", 16, lead=0) for r in range(2)]
    stored = [k.counter(f"slot_stored{r}", 16) for r in range(2)]
    index_ready, weights_ready, transposed, gT_ready, up_done, act_done, inner_ready, down_done, y_ready = (
        k.counter(f"slot_{n}") for n in ("index_ready", "weights_ready", "transposed", "gT_ready", "up_done",
                                        "act_done", "inner_ready", "down_done", "y_ready"))
    biased = k.counter("slot_biased")
    ps_t, h1, h2, py = k.ps[:, 0:2, 0:P], k.ps[:, 2:4, :], k.ps[:, 4:6, :], k.ps[:, 6:8, 0:D]
    wide = 2 * FF if top == 1 else FF
    w_up = k.w12[:, :, :].rearrange("p e n -> p (e n)") if top == 1 else k.w1[:, :, :].rearrange("p e n -> p (e n)")
    w_dn = (k.w3 if top == 1 else k.w2)[:, :, :, :].rearrange("p e b d -> p (e b d)")
    y_rows = k.y_rows.rearrange("(s p) d -> s p d", p=P)
    half = (slots - 1) // 2

    def every_slot(eng, body):
        body(0, 0)
        with eng.Fori(0, half) as i:
            body(i * 2 + 1, 1)
            body(i * 2 + 2, 0)

    def uses(s, r):
        return (s + 1) // 2 if r == 0 else s // 2

    k.start()
    with nc.Block() as block:
        @block.gpsimd
        def _(pool):
            def body(s, r):
                pool.wait_ge(transposed.sem, transposed.at(s - 1))
                nc.gpsimd.tensor_copy(k.index[:, r:r + 1], k.slot_token[:, ds(s, 1)]).then_inc(index_ready.sem, 1)
                pool.wait_ge(index_ready.sem, index_ready.at(s + 1))
                k.settle(pool)
                nc.gpsimd.indirect_dma_start(k.rows_in[:, r, :], None, k.xn_rows[:, :],
                                             bass.IndirectOffsetOnAxis(ap=k.index[:, r:r + 1], axis=0)
                                             ).then_inc(gathered[r].sem, 16)
            every_slot(pool, body)

        @block.tensor
        def _(pe):
            def up(s, r):
                pe.wait_ge(gathered[r].sem, gathered[r].at(uses(s, r) + 1))
                pe.wait_ge(gT_ready.sem, gT_ready.at(s - 1))
                nc.tensor.transpose(ps_t[:, r, :], k.rows_in[:, r, :], k.ident[:, :]).then_inc(transposed.sem, 1)
                pe.wait_ge(gT_ready.sem, gT_ready.at(s + 1))
                pe.wait_ge(weights_ready.sem, weights_ready.at(s + 1))
                pe.wait_ge(inner_ready.sem, inner_ready.at(s - 1))
                for b in range(FB):
                    ins = nc.tensor.matmul(h1[:, r, b * P:(b + 1) * P], k.w_slot[:, r, b * P:(b + 1) * P],
                                           k.gT[:, r, :], start=True, stop=True)
                if top == 1:
                    for b in range(FB):
                        ins = nc.tensor.matmul(h2[:, r, b * P:(b + 1) * P], k.w_slot[:, r, FF + b * P:FF + (b + 1) * P],
                                               k.gT[:, r, :], start=True, stop=True)
                ins.then_inc(up_done.sem, 1)

            def down(s, r):
                e = pe.value_load(k.slot_expert[0:1, ds(s, 1)], min_val=0, max_val=NE - 1)
                pe.wait_ge(inner_ready.sem, inner_ready.at(s + 1))
                pe.wait_ge(y_ready.sem, y_ready.at(s - 1))
                for b in range(FB):
                    ins = nc.tensor.matmul(py[:, r, :], k.inner_slot[:, r, b * P:(b + 1) * P],
                                           w_dn[:, ds(e * (FB * D) + b * D, D)], start=(b == 0), stop=(b == FB - 1))
                ins.then_inc(down_done.sem, 1)

            up(0, 0)
            with pe.Fori(0, half) as i:
                up(i * 2 + 1, 1)
                down(i * 2, 0)
                up(i * 2 + 2, 0)
                down(i * 2 + 1, 1)
            down(slots - 1, 0)

        @block.scalar
        def _(act):
            def body(s, r):
                if top == 2:
                    e = act.value_load(k.slot_expert[0:1, ds(s, 1)], min_val=0, max_val=NE - 1)
                act.wait_ge(transposed.sem, transposed.at(s + 1))
                act.wait_ge(up_done.sem, up_done.at(s - 1))
                nc.scalar.copy(k.gT[:, r, :], ps_t[:, r, :]).then_inc(gT_ready.sem, 1)
                if top == 1:
                    act.wait_ge(up_done.sem, up_done.at(s + 1))
                    act.wait_ge(inner_ready.sem, inner_ready.at(s - 1))
                    nc.scalar.activation(k.gl[:, r, :], h1[:, r, :], ACT.Gelu).then_inc(act_done.sem, 1)
                else:
                    act.wait_ge(biased.sem, biased.at(s + 1))
                    act.wait_ge(down_done.sem, down_done.at(s - 1))
                    with act.If(e % 2 == 0):
                        nc.scalar.activation(k.inner_slot[:, r, :], k.hb[:, r, :], ACT.Gelu).then_inc(act_done.sem, 1)
                    with act.Else():
                        nc.scalar.activation(k.inner_slot[:, r, :], k.hb[:, r, :], ACT.Tanh, scale=0.5).then_inc(act_done.sem, 1)
            if top == 2:
                nc.scalar.activation(k.spare[:, 1:2], k.zero[:, 0:1], ACT.Gelu)
            every_slot(act, body)

        @block.vector
        def _(dve):
            def output(s, r):
                if top == 2:
                    e = dve.value_load(k.slot_expert[0:1, ds(s, 1)], min_val=0, max_val=NE - 1)
                dve.wait_ge(down_done.sem, down_done.at(s + 1))
                dve.wait_ge(stored[r].sem, stored[r].at(uses(s, r)))
                if top == 1:
                    nc.vector.tensor_copy(k.y[:, r, :], py[:, r, :]).then_inc(y_ready.sem, 1)
                else:
                    nc.vector.tensor_tensor(k.y[:, r, :], py[:, r, :], k.b2[:, ds(e * D, D)], ALU.add
                                            ).then_inc(y_ready.sem, 1)

            def inner(s, r):
                if top == 1:
                    dve.wait_ge(act_done.sem, act_done.at(s + 1))
                    dve.wait_ge(down_done.sem, down_done.at(s - 1))
                    nc.vector.tensor_tensor(k.inner_slot[:, r, :], k.gl[:, r, :], h2[:, r, :], ALU.mult
                                            ).then_inc(inner_ready.sem, 1)
                else:
                    e = dve.value_load(k.slot_expert[0:1, ds(s, 1)], min_val=0, max_val=NE - 1)
                    dve.wait_ge(up_done.sem, up_done.at(s + 1))
                    nc.vector.tensor_tensor(k.hb[:, r, :].rearrange("p (b t) -> p b t", b=FB),
                                            h1[:, r, :].rearrange("p (b t) -> p b t", b=FB),
                                            bcast(k.b1[:, ds(e * FB, FB)], 2, P), ALU.add).then_inc(biased.sem, 1)
                    dve.wait_ge(act_done.sem, act_done.at(s + 1))
                    with dve.If(e % 2 == 0):
                        nc.vector.tensor_copy(k.spare[:, 2:3], k.zero[:, 0:1]).then_inc(inner_ready.sem, 1)
                    with dve.Else():
                        nc.vector.scalar_tensor_tensor(k.inner_slot[:, r, :], k.inner_slot[:, r, :], 1.0,
                                                       k.hb[:, r, :], ALU.add, ALU.mult).then_inc(inner_ready.sem, 1)

            def weights(s, r):
                e = dve.value_load(k.slot_expert[0:1, ds(s, 1)], min_val=0, max_val=NE - 1)
                dve.wait_ge(up_done.sem, up_done.at(s - 1))
                nc.vector.tensor_copy(k.w_slot[:, r, 0:wide], w_up[:, ds(e * wide, wide)]).then_inc(weights_ready.sem, 1)

            weights(0, 0)
            weights(1, 1)
            inner(0, 0)
            with dve.Fori(0, half - 1) as i:
                weights(i * 2 + 2, 0)
                inner(i * 2 + 1, 1)
                output(i * 2, 0)
                weights(i * 2 + 3, 1)
                inner(i * 2 + 2, 0)
                output(i * 2 + 1, 1)
            weights(slots - 1, 0)
            inner(slots - 2, 1)
            output(slots - 3, 0)
            inner(slots - 1, 0)
            output(slots - 2, 1)
            output(slots - 1, 0)

        @block.sync
        def _(sp):
            def body(s, r):
                sp.wait_ge(y_ready.sem, y_ready.at(s + 1))
                sp.dma_start(y_rows[ds(s, 1)].rearrange("s p d -> (s p) d"),
                             k.y[:, r, :]).then_inc(stored[r].sem, 16)
            every_slot(sp, body)
            for r in range(2):
                sp.wait_ge(stored[r].sem, stored[r].at(half + 1 - r))

    for s in (index_ready, weights_ready, transposed, gT_ready, up_done, act_done, inner_ready, down_done, y_ready):
        s.close(slots)
    if top == 2:
        biased.close(slots)
    for r in range(2):
        gathered[r].close(half + 1 - r)
        stored[r].close(half + 1 - r)

    fetched = [k.counter(f"back_fetched{r}", 16, lead=0) for r in range(4)]
    picked, added = k.counter("back_index_ready"), k.counter("back_added")
    NP = top * NT
    RING = 4
    k.start()
    with nc.Block() as block:
        @block.gpsimd
        def _(pool):
            def fetch(n, r):
                nc.gpsimd.tensor_copy(k.index[:, r:r + 1], k.pos[:, ds(n, 1)]).then_inc(picked.sem, 1)
                pool.wait_ge(picked.sem, picked.at(n + 1))
                k.settle(pool)
                nc.gpsimd.indirect_dma_start(k.back[:, r, :], None, k.y_rows[0:slots * P, :],
                                             bass.IndirectOffsetOnAxis(ap=k.index[:, r:r + 1], axis=0)
                                             ).then_inc(fetched[r].sem, 16)
            for r in range(RING):
                fetch(r, r)
            with pool.Fori(1, NP // RING) as i:
                for r in range(RING):
                    pool.wait_ge(added.sem, added.at(i * RING + (r - RING + 1)))
                    fetch(i * RING + r, r)

        @block.vector
        def _(dve):
            for c in range(top):
                with dve.Fori(0, NT // RING) as i:
                    for r in range(RING):
                        t = i * RING
                        n = t + (r + c * NT)
                        dve.wait_ge(fetched[r].sem, fetched[r].at(i + (c * NT // RING + 1)))
                        if c:
                            dve.wait_ge(added.sem, added.at(n - NT + 1))
                        xt = k.x[:, ds((t + r) * D, D)]
                        if top == 1:
                            nc.vector.scalar_tensor_tensor(xt, k.back[:, r, :], 0.5, xt, ALU.mult, ALU.add
                                                           ).then_inc(added.sem, 1)
                        else:
                            nc.vector.scalar_tensor_tensor(xt, k.back[:, r, :], k.gate[:, c, ds(t + r, 1)], xt,
                                                           ALU.mult, ALU.add).then_inc(added.sem, 1)
            dve.wait_ge(added.sem, added.at(NP))
    for r in range(RING):
        fetched[r].close(NP // RING)
    picked.close(NP)
    added.close(NP)




def attend(k, w):
    nc = k.nc
    QB = SEQ // P
    SCALE = float(QK) ** -0.5
    w_turned, w_ready = k.counter("attn_w_turned"), k.counter("attn_w_ready")
    projected, qk_ready = k.counter("attn_projected"), k.counter("attn_qk_ready")
    v_in = k.counter("attn_v_in", 16)
    scored, masked, maxed, expd, turned, pt_ready, mixed, added = (
        k.counter(f"attn_{n}") for n in ("scored", "masked", "max_ready", "exp_done", "probs_turned",
                                        "probsT_ready", "mixed", "added"))
    own = k.counter("attn_vector_step")
    with ExitStack() as stack:
        S = k.scope(stack)
        wqk, wT, bqk = S("wqk", [QK, 2, D]), S("wT", [P, 2, QK]), S("bqk", [QK, 2])
        qT, kT = S("qT", [QK, SEQ]), S("kT", [QK, SEQ])
        v = S("v", [P, QB, D])
        probs, pT = S("probs", [P, 2, SEQ]), S("pT", [P, 2, SEQ])
        keep, fill = S("keep", [P, P]), S("fill", [P, P])
        top, nmax, total, inv = (S(n, [P, 2]) for n in ("top", "nmax", "total", "inv"))
        loads = [(wqk[:, 0, :], w["L1_attn_w_q"]), (wqk[:, 1, :], w["L1_attn_w_k"]),
                 (bqk[:, 0:1], w["L1_attn_b_q"].unsqueeze(1)), (bqk[:, 1:2], w["L1_attn_b_k"].unsqueeze(1))]
        prepare(k, None, 0, loads)
        xn_h = k.xn_rows.rearrange("(b t p) d -> p b t d", p=P, b=BATCH)
        ps_s = [k.ps[:, 2 * r:2 * r + 2, :].rearrange("p b n -> p (b n)") for r in range(2)]
        ps_t = k.ps[:, 4:6, :].rearrange("p b n -> p (b n)")
        ps_o, ps_q = k.ps[:, 6:8, 0:D], k.ps[:, 7, :]
        k.start()
        with nc.Block() as block:
            @block.gpsimd
            def _(pool):
                nc.gpsimd.affine_select(out=keep[:, :], in_=k.ones[:, :], compare_op=ALU.is_ge, fill=0.0, base=0,
                                        pattern=[[-1, P]], channel_multiplier=1).then_inc(w_turned.sem, 1)
                pool.wait_ge(w_turned.sem, w_turned.at(1))
                nc.gpsimd.tensor_scalar(fill[:, :], keep[:, :], -1.0, 10000.0 / SCALE, ALU.add, ALU.mult
                                        ).then_inc(w_turned.sem, 1)

            @block.sync
            def _(sp):
                with sp.Fori(0, BATCH) as b:
                    sp.wait_ge(mixed.sem, mixed.at(b * QB))
                    sp.dma_start(v[:, :, :], xn_h[:, ds(b, 1)].rearrange("p b t d -> p (b t) d")).then_inc(v_in.sem, 16)

            @block.tensor
            def _(pe):
                for i in range(2):
                    ins = nc.tensor.transpose(ps_q[:, i * QK:(i + 1) * QK], wqk[:, i, :], k.ident[0:QK, 0:QK])
                ins.then_inc(w_ready.sem, 1)
                pe.wait_ge(w_ready.sem, w_ready.at(2))

                def score(b, q):
                    n, r = b * QB + q, q % 2
                    pe.wait_ge(expd.sem, expd.at(n - 1))
                    for c in range(0, (q + 1) * P, 512):
                        width = min(512, (q + 1) * P - c)
                        ins = nc.tensor.matmul(ps_s[r][:, c:c + width], qT[:, q * P:(q + 1) * P], kT[:, c:c + width],
                                               start=True, stop=True)
                    ins.then_inc(scored.sem, 1)

                def mix(b, q):
                    n, r = b * QB + q, q % 2
                    pe.wait_ge(expd.sem, expd.at(n + 1))
                    pe.wait_ge(pt_ready.sem, pt_ready.at(n))
                    for c in range(q + 1):
                        ins = nc.tensor.transpose(ps_t[:, c * P:(c + 1) * P], probs[:, r, c * P:(c + 1) * P], k.ident[:, :])
                    ins.then_inc(turned.sem, 1)
                    pe.wait_ge(pt_ready.sem, pt_ready.at(n + 1))
                    pe.wait_ge(added.sem, added.at(n - 1))
                    for c in range(q + 1):
                        ins = nc.tensor.matmul(ps_o[:, r, :], pT[:, r, c * P:(c + 1) * P], v[:, c, :],
                                               start=(c == 0), stop=(c == q))
                    ins.then_inc(mixed.sem, 1)

                with pe.Fori(0, BATCH) as b:
                    pe.wait_ge(added.sem, added.at(b * QB))
                    for i in range(4):
                        m = b * 4 + i
                        pe.wait_ge(qk_ready.sem, qk_ready.at(m))
                        k.settle(pe)
                        nc.tensor.matmul(ps_q[0:QK, :], wT[:, i // 2, :], k.xnT[:, ds(b * SEQ + (i % 2) * 512, 512)],
                                         start=True, stop=True).then_inc(projected.sem, 1)
                    pe.wait_ge(qk_ready.sem, qk_ready.at(b * 4 + 4))
                    pe.wait_ge(v_in.sem, v_in.at(b + 1))
                    score(b, 0)
                    for q in range(1, QB):
                        score(b, q)
                        mix(b, q - 1)
                    mix(b, QB - 1)

            @block.scalar
            def _(act):
                act.wait_ge(w_ready.sem, w_ready.at(1))
                nc.scalar.copy(wT[:, :, :].rearrange("p a n -> p (a n)"), ps_q[:, 0:2 * QK]).then_inc(w_ready.sem, 1)
                with act.Fori(0, BATCH) as b:
                    for i in range(4):
                        m = b * 4 + i
                        act.wait_ge(projected.sem, projected.at(m + 1))
                        dst = (qT, kT)[i // 2]
                        nc.scalar.activation(dst[:, (i % 2) * 512:(i % 2) * 512 + 512], ps_q[0:QK, :], ACT.Identity,
                                             bias=bqk[:, i // 2:i // 2 + 1]).then_inc(qk_ready.sem, 1)
                    for q in range(QB):
                        n, r, width = b * QB + q, q % 2, (q + 1) * P
                        act.wait_ge(maxed.sem, maxed.at(n + 1))
                        act.wait_ge(turned.sem, turned.at(n - 1))
                        act.wait_ge(added.sem, added.at(n - 1))
                        nc.scalar.activation(probs[:, r, 0:width], ps_s[r][:, 0:width], ACT.Exp, scale=SCALE,
                                             bias=nmax[:, r:r + 1], accum_out=total[:, r:r + 1]).then_inc(expd.sem, 1)
                        act.wait_ge(turned.sem, turned.at(n + 1))
                        act.wait_ge(mixed.sem, mixed.at(n - 1))
                        nc.scalar.copy(pT[:, r, 0:width], ps_t[:, 0:width]).then_inc(pt_ready.sem, 1)

            @block.vector
            def _(dve):
                V = nc.vector
                dve.wait_ge(w_turned.sem, w_turned.at(2))

                def maximum(b, q):
                    n, r = b * QB + q, q % 2
                    last = ps_s[r][:, q * P:(q + 1) * P]
                    dve.wait_ge(scored.sem, scored.at(n + 1))
                    V.tensor_tensor(last, last, keep[:, :], ALU.mult).then_inc(own.sem, 1)
                    dve.wait_ge(own.sem, own.at(n * 3 + 1))
                    V.tensor_tensor(last, last, fill[:, :], ALU.add).then_inc(own.sem, 1)
                    dve.wait_ge(own.sem, own.at(n * 3 + 2))
                    V.tensor_reduce(top[:, r:r + 1], ps_s[r][:, 0:(q + 1) * P], AX.X, ALU.max).then_inc(own.sem, 1)
                    dve.wait_ge(own.sem, own.at(n * 3 + 3))
                    dve.wait_ge(expd.sem, expd.at(n - 1))
                    V.tensor_scalar(nmax[:, r:r + 1], top[:, r:r + 1], -SCALE, None, ALU.mult).then_inc(maxed.sem, 1)

                def add(b, q):
                    n, r = b * QB + q, q % 2
                    dve.wait_ge(mixed.sem, mixed.at(n + 1))
                    V.reciprocal(inv[:, r:r + 1], total[:, r:r + 1]).then_inc(masked.sem, 1)
                    dve.wait_ge(masked.sem, masked.at(n + 1))
                    xt = k.x[:, ds(n * D, D)]
                    V.scalar_tensor_tensor(xt, ps_o[:, r, :], inv[:, r:r + 1], xt, ALU.mult, ALU.add
                                           ).then_inc(added.sem, 1)

                with dve.Fori(0, BATCH) as b:
                    maximum(b, 0)
                    for q in range(1, QB):
                        maximum(b, q)
                        add(b, q - 1)
                    add(b, QB - 1)
        n = BATCH * QB
        for s in (scored, masked, maxed, expd, turned, pt_ready, mixed, added):
            s.close(n)
        own.close(3 * n)
        w_turned.close(2)
        w_ready.close(2)
        projected.close(4 * BATCH)
        qk_ready.close(4 * BATCH)
        v_in.close(BATCH)


def mamba(k, w):
    nc = k.nc
    with ExitStack() as stack:
        S = k.scope(stack)
        m = Weights()
        m.win, m.wout, m.nw = S("win", [P, ME, ZW + CW + MH]), S("wout", [P, ME, 2, D]), S("nw", [P, ME * 2])
        m.cw, m.cb = S("cw", [P, ME * 4, TAPS]), S("cb", [P, ME * 4])
        m.dtb, m.aneg, m.dsk = (S(n, [P, MEH]) for n in ("dtb", "aneg", "dsk"))
        m.diagD = S("diagD", [P, MEH, P])
        m.tri, m.identb = S("tri", [P, P]), S("identb", [P, P], BF16)
        m.future = S("future", [P, MH, P], BF16)
        m.pickA, m.pickQ = S("pickA", [P, MEH, P], BF16), S("pickQ", [P, ME, MH * P], BF16)
        m.keep = S("keepg", [P, NG])
        m.rout = S("rout", [P, NT * ME])
        m.wst, m.ea, m.cd = (S(n, [P, NT * MEH]) for n in ("wst", "ea", "cd"))
        m.parts = S("parts", [P, NT, P], BF16)
        in_w = w["L0_attn_in_w"]
        loads = [
            (m.win[:, :, :], in_w.rearrange("e d n -> d e n")),
            (m.wout[:, :].rearrange("p e b d -> p (e b) d"), w["L0_attn_out_w"].rearrange("e (b p) d -> p (e b) d", p=P)),
            (m.nw[:, :], w["L0_attn_norm_w"].rearrange("e (b p) -> p (e b)", p=P)),
            (m.cw[:, :, :], w["L0_attn_conv_w"].rearrange("e (b p) k -> p (e b) k", p=P)),
            (m.cb[:, :], w["L0_attn_conv_b"].rearrange("e (b p) -> p (e b)", p=P)),
            (m.dtb[:, :], w["L0_attn_dt_bias"].rearrange("e h -> (e h)").unsqueeze(0).to_broadcast([P, MEH])),
            (m.aneg[:, :], w["L0_attn_A_log"].rearrange("e h -> (e h)").unsqueeze(0).to_broadcast([P, MEH])),
            (m.dsk[:, :], w["L0_attn_D_skip"].rearrange("e h -> (e h)").unsqueeze(0).to_broadcast([P, MEH])),
        ]
        prepare(k, k.mw[:, :], NM, loads)
        with ExitStack() as inner:
            mamba_scalars(k, m, k.scope(inner))
        with ExitStack() as inner:
            mamba_groups(k, m, k.scope(inner))


class Weights:
    pass


def mamba_scalars(k, m, S):
    nc = k.nc
    N = NT * MEH
    v, av, u, dt, q, z0 = (S(n, [P, N]) for n in ("v", "av", "u", "dt", "q", "z0"))
    mx, sm = S("mx", [P, NT]), S("sm", [P, NT])
    consts, own, to_act, acted, a_ready, summed = (
        k.counter(f"scalars_{n}") for n in ("constants", "vector_step", "to_scalar", "scalar_step", "a_ready", "summed"))
    lg = k.logits[:, 0:NT * NM].rearrange("p (t n) -> p t n", n=NM)
    by_head = lambda t: t[:, :].rearrange("p (t n) -> p t n", n=MEH)
    ps_acs, ps_tot = k.ps[:, 0, :], k.ps[:, 1, :]

    k.start()
    with nc.Block() as block:
        @block.gpsimd
        def _(pool):
            G = nc.gpsimd
            do = Chain(pool, consts)
            do(G.affine_select(out=m.tri[:, :], in_=k.ones[:, :], compare_op=ALU.is_ge, fill=0.0, base=0,
                               pattern=[[1, P]], channel_multiplier=-1))
            do(G.tensor_copy(m.identb[:, :], k.ident[:, :]))
            do(G.memset(m.future[:, :, :], 0.0))
            do(G.affine_select(out=m.future[:, :, :], in_=m.future[:, :, :], compare_op=ALU.is_ge, fill=-1e30,
                               base=0, pattern=[[0, MH], [1, P]], channel_multiplier=-1))
            do(G.memset(m.pickA[:, :, :], 0.0))
            do(G.memset(m.pickQ[:, :, :], 0.0))
            for part in range(3):
                do(G.affine_select(out=m.pickA[:, :, :], in_=m.pickA[:, :, :], compare_op=ALU.not_equal, fill=1.0,
                                   base=-MEH * part, pattern=[[-1, MEH], [0, P]], channel_multiplier=1))
                pq = m.pickQ[:, :, :].rearrange("p e (h l) -> p e h l", h=MH)
                do(G.affine_select(out=pq, in_=pq, compare_op=ALU.not_equal, fill=1.0, base=-MEH * (3 + part),
                                   pattern=[[-MH, ME], [-1, MH], [0, P]], channel_multiplier=1))
            do(G.memset(m.keep[:, :], 1.0))
            do(G.memset(m.keep[:, :].rearrange("p (b g) -> p b g", b=BATCH)[:, :, 0:1], 0.0))

        @block.vector
        def _(dve):
            V = nc.vector
            do = Chain(dve, own)

            def on_scalar(step):
                dve.sem_inc(to_act.sem, 1)
                dve.wait_ge(acted.sem, acted.at(step))

            rout = m.rout[:, :].rearrange("p (t e) -> p t e", e=ME)
            do(V.memset(m.parts[:, :, :], 0.0))
            do(V.tensor_reduce(mx[:, :], lg[:, :, 0:ME], AX.X, ALU.max))
            do(V.tensor_tensor(rout, lg[:, :, 0:ME], bcast(mx[:, :], 2, ME), ALU.subtract))
            do(V.tensor_tensor(by_head(v), lg[:, :, ME:NM], bcast(m.dtb[:, :], 1, NT), ALU.add))
            do(V.scalar_tensor_tensor(av[:, :], v[:, :], -1.0, v[:, :], ALU.mult, ALU.max))
            on_scalar(3)
            do(V.tensor_reduce(sm[:, :], rout, AX.X, ALU.add))
            do(V.reciprocal(sm[:, :], sm[:, :]))
            do(V.tensor_tensor(rout, rout, bcast(sm[:, :], 2, ME), ALU.mult))
            do(V.tensor_scalar(av[:, :], u[:, :], 1.0, None, ALU.add))
            on_scalar(4)
            do(V.tensor_scalar(av[:, :], av[:, :], -1.0, None, ALU.add))
            do(V.tensor_scalar(z0[:, :], av[:, :], 0.0, None, ALU.is_equal))
            do(V.tensor_add(av[:, :], av[:, :], z0[:, :]))
            do(V.reciprocal(av[:, :], av[:, :]))
            do(V.tensor_mul(dt[:, :], dt[:, :], av[:, :]))
            do(V.tensor_add(dt[:, :], dt[:, :], z0[:, :]))
            do(V.tensor_mul(dt[:, :], dt[:, :], u[:, :]))
            do(V.scalar_tensor_tensor(dt[:, :], v[:, :], 0.0, dt[:, :], ALU.max, ALU.add))
            do(V.tensor_scalar(u[:, :], dt[:, :], 1e-19, None, ALU.max))
            V.scalar_tensor_tensor(by_head(v), by_head(dt), -1.0, bcast(m.aneg[:, :], 1, NT), ALU.mult, ALU.mult
                                   ).then_inc(a_ready.sem, 1)
            on_scalar(5)
            dve.wait_ge(summed.sem, summed.at(1))
            acs = dt
            do(V.tensor_copy(acs[:, :], ps_acs))
            do(V.tensor_sub(q[:, :], q[:, :], acs[:, :]))
            do(V.tensor_tensor(av[:, :], q[:, :], ps_tot, ALU.add))
            on_scalar(8)
            for t in (m.ea, m.cd):
                first = t[:, :].rearrange("p (b c n) -> p b c n", b=BATCH, n=MEH)[:, :, 0, :]
                do(V.memset(first, 0.0))
            for src, first in ((acs, 0), (q, 3)):
                for part in range(3):
                    out = m.parts[:, :, (first + part) * MEH:(first + part + 1) * MEH]
                    do(V.tensor_copy(out, by_head(src)))
                    if part < 2:
                        do(V.tensor_tensor(by_head(src), by_head(src), out, ALU.subtract))
            for e in range(ME):
                for b in range(2):
                    do(V.tensor_scalar(m.wout[:, e, b, :], m.wout[:, e, b, :], m.nw[:, e * 2 + b:e * 2 + b + 1],
                                       None, ALU.mult))
            for n in range(MEH):
                do(V.tensor_scalar(m.diagD[:, n, :], k.ident[:, :], m.dsk[:, n:n + 1], None, ALU.mult))
            k.scalar_steps = do.n
            dve.wait_ge(consts.sem, consts.at(14))

        @block.scalar
        def _(act):
            do = Chain(act, acted)
            act.wait_ge(to_act.sem, to_act.at(1))
            do(nc.scalar.activation(m.rout[:, :], m.rout[:, :], ACT.Exp))
            do(nc.scalar.activation(u[:, :], av[:, :], ACT.Exp, scale=-1.0))
            do(nc.scalar.activation(m.aneg[:, :], m.aneg[:, :], ACT.Exp))
            act.wait_ge(to_act.sem, to_act.at(2))
            do(nc.scalar.activation(dt[:, :], av[:, :], ACT.Ln))
            act.wait_ge(to_act.sem, to_act.at(3))
            do(nc.scalar.activation(q[:, :], u[:, :], ACT.Ln))
            act.wait_ge(to_act.sem, to_act.at(4))
            do(nc.scalar.activation(m.wst[:, :], av[:, :], ACT.Exp))
            do(nc.scalar.activation(m.ea[:, :], dt[:, :], ACT.Exp))
            do(nc.scalar.activation(m.cd[:, :], ps_tot, ACT.Exp))

        @block.tensor
        def _(pe):
            pe.wait_ge(consts.sem, consts.at(1))
            pe.wait_ge(a_ready.sem, a_ready.at(1))
            nc.tensor.matmul(ps_acs, m.tri[:, :], v[:, :], start=True, stop=True)
            nc.tensor.matmul(ps_tot, k.ones[:, :], v[:, :], start=True, stop=True).then_inc(summed.sem, 1)
    own.close(k.scalar_steps)
    consts.close(14)
    to_act.close(4)
    acted.close(8)
    a_ready.close(1)
    summed.close(1)


def mamba_groups(k, m, S):
    nc = k.nc
    NU = GRP * ME
    NB = CW // P
    GT = GRP * P
    xc = S("xc", [P, GT])
    xb, cv, tails = S("xb", [P, 2, TAPS - 1 + GT]), S("cv", [P, 2, GT]), S("tails", [P, ME * NB, TAPS - 1])
    xbc, sz = S("xbc", [P, ME, NB, GT]), S("sz", [P, ME, GRP, ZW])
    rows = S("rows", [P, GRP, P], BF16)
    state, carried = S("state", [P, ME, ZW]), S("carried", [P, 2, ZW])
    XB, L, M, Xw = S("XB", [P, 2, ZW + P]), S("L", [P, 2, MH * P]), S("M", [P, 2, MH * P]), S("Xw", [P, 2, ZW])
    t1, t2, y2, yT, sq = S("t1", [P, ZW]), S("t2", [P, ZW]), S("y2", [P, 2, ZW]), S("yT", [P, 2, ZW]), S("sq", [P, ZW])
    ss, rs, gain = S("ss", [P, 2]), S("rs", [P, 2]), S("gain", [P, 2])

    names = ("xc", "rows_turned", "rows", "proj", "copied", "conv", "conv_silu", "z", "z_silu", "tail")
    a = {n: k.counter(f"group_{n}") for n in names}
    own = k.counter("group_vector_step")
    names = ("x_turned", "cb", "exponent", "XB", "L", "M", "Xw", "y", "s", "carried", "state", "y2", "squared",
             "yT_turned", "yT", "out", "gain", "added")
    b = {n: k.counter(f"unit_{n}") for n in names}
    yown, gown, init = k.counter("unit_y_step"), k.counter("unit_gain_step"), k.counter("group_init")

    bankX, bankL, bankCB, bankY, bankS, bankYT, bankO = (k.ps[:, i, :] for i in range(7))

    def inc(ins, sig):
        ins.then_inc(sig.sem, 1)

    def wait(eng, sig, n):
        eng.wait_ge(sig.sem, sig.at(n))

    k.start()
    with nc.Block() as block:
        @block.tensor
        def _(pe):
            def project(g):
                wait(pe, b["added"], g * NU)
                wait(pe, a["xc"], g + 1)
                for j in range(GRP):
                    ins = nc.tensor.matmul(k.ps[:, 7, j * P:(j + 1) * P], m.parts[:, ds(g * GRP + j, 1), :].rearrange("p a n -> p (a n)"),
                                           m.identb[:, :], start=True, stop=True)
                inc(ins, a["rows_turned"])
                for e in range(ME):
                    for blk in range(NB):
                        i = (g * ME + e) * NB + blk
                        wait(pe, a["copied"], i - 3)
                        inc(nc.tensor.matmul(k.ps[:, blk, :], m.win[:, e, ZW + blk * P:ZW + (blk + 1) * P], xc[:, :],
                                             start=True, stop=True), a["proj"])
                    if e == 0:
                        wait(pe, a["rows"], g + 1)
                    wait(pe, a["z_silu"], g * ME + e)
                    for j in range(GRP):
                        ins = nc.tensor.matmul(k.ps[:, 4 + j, 0:ZW], xc[:, j * P:(j + 1) * P], m.win[:, e, 0:ZW],
                                               start=True, stop=True)
                    inc(ins, a["z"])

            def open_unit(g, u):
                j, e = u // ME, u % ME
                n = g * NU + u
                cols = slice(j * P, (j + 1) * P)
                if u < ME:
                    wait(pe, a["conv_silu"], (g * ME + ME) * NB)
                    wait(pe, a["z_silu"], (g + 1) * ME)
                wait(pe, b["XB"], n)
                for blk in range(3):
                    ins = nc.tensor.transpose(bankX[:, blk * P:(blk + 1) * P], xbc[:, e, blk, cols], k.ident[:, :])
                inc(ins, b["x_turned"])
                wait(pe, b["L"], n)
                nc.tensor.matmul(bankL, m.identb[:, :], m.future[:, :, :].rearrange("p h l -> p (h l)"),
                                 start=True, stop=False, skip_group_check=True)
                nc.tensor.matmul(bankL, rows[:, j, :], m.pickQ[:, e, :], start=False, stop=False, skip_group_check=True)
                for h in range(MH):
                    ins = nc.tensor.matmul(bankL[:, h * P:(h + 1) * P], m.pickA[:, e * MH + h, :], rows[:, j, :],
                                           start=False, stop=(h == MH - 1), skip_group_check=True)
                inc(ins, b["exponent"])
                wait(pe, b["M"], n)
                inc(nc.tensor.matmul(bankCB[:, 0:P], xbc[:, e, 2, cols], xbc[:, e, 3, cols], start=True, stop=True), b["cb"])

            def mix_unit(g, u):
                j, e = u // ME, u % ME
                n = g * NU + u
                r = u % 2
                wait(pe, b["M"], n + 1)
                wait(pe, b["XB"], n + 1)
                wait(pe, b["y2"], n)
                for h in range(MH):
                    cols = slice(h * HD, (h + 1) * HD)
                    nc.tensor.matmul(bankY[:, cols], M[:, r, h * P:(h + 1) * P], XB[:, r, cols], start=True, stop=False)
                    nc.tensor.matmul(bankY[:, cols], m.diagD[:, e * MH + h, :], XB[:, r, cols], start=False, stop=True)
                wait(pe, b["state"], n - 3)
                inc(nc.tensor.matmul(bankY[:, ZW:2 * ZW], xbc[:, e, 3, j * P:(j + 1) * P], state[:, e, :],
                                     start=True, stop=True), b["y"])
                wait(pe, b["Xw"], n + 1)
                wait(pe, b["state"], n)
                inc(nc.tensor.matmul(bankS[:, 0:ZW], XB[:, r, ZW:ZW + P], Xw[:, r, :], start=True, stop=True), b["s"])

            def turn_unit(g, u):
                n, r = g * NU + u, u % 2
                wait(pe, b["y2"], n + 1)
                wait(pe, b["yT"], n)
                for blk in range(2):
                    ins = nc.tensor.transpose(bankYT[:, blk * P:(blk + 1) * P], y2[:, r, blk * P:(blk + 1) * P], k.ident[:, :])
                inc(ins, b["yT_turned"])

            def out_unit(g, u):
                n, r, e = g * NU + u, u % 2, u % ME
                wait(pe, b["yT"], n + 1)
                wait(pe, b["added"], n)
                for blk in range(2):
                    ins = nc.tensor.matmul(bankO[:, 0:D], yT[:, r, blk * P:(blk + 1) * P], m.wout[:, e, blk, :],
                                           start=(blk == 0), stop=(blk == 1))
                inc(ins, b["out"])

            wait(pe, init, 1)
            with pe.Fori(0, NG) as g:
                project(g)
                open_unit(g, 0)
                for u in range(NU + 1):
                    if u + 1 < NU:
                        open_unit(g, u + 1)
                    if u >= 1:
                        turn_unit(g, u - 1)
                    if u < NU:
                        mix_unit(g, u)
                    if u >= 1:
                        out_unit(g, u - 1)

        @block.scalar
        def _(act):
            def copy(i, blk):
                wait(act, a["proj"], i + 1)
                wait(act, a["conv"], i - 1)
                inc(nc.scalar.copy(xb[:, blk % 2, TAPS - 1:TAPS - 1 + GT], k.ps[:, blk, :]), a["copied"])

            def silu(i, e, blk):
                wait(act, a["conv"], i + 1)
                inc(nc.scalar.activation(xbc[:, e, blk, :], cv[:, blk % 2, :], ACT.Silu,
                                         bias=m.cb[:, e * NB + blk:e * NB + blk + 1]), a["conv_silu"])

            def open_unit(g, u):
                n, r = g * NU + u, u % 2
                wait(act, b["x_turned"], n + 1)
                wait(act, b["s"], n - 1)
                inc(nc.scalar.copy(XB[:, r, :], bankX[:, 0:ZW + P]), b["XB"])
                wait(act, b["exponent"], n + 1)
                wait(act, b["M"], n - 1)
                inc(nc.scalar.activation(L[:, r, :], bankL, ACT.Exp), b["L"])

            def close_unit(g, u):
                n, r = g * NU + u, u % 2
                wait(act, b["yT_turned"], n + 1)
                wait(act, b["out"], n - 1)
                inc(nc.scalar.copy(yT[:, r, :], bankYT[:, 0:ZW]), b["yT"])
                wait(act, b["gain"], n - 1)
                wait(act, b["squared"], n)
                inc(nc.scalar.activation(sq[:, :], y2[:, r, :], ACT.Square, scale=float(ZW) ** -0.5,
                                         accum_out=ss[:, r:r + 1]), b["squared"])

            with act.Fori(0, NG) as g:
                wait(act, a["z"], g * ME)
                wait(act, b["out"], g * NU)
                inc(nc.scalar.copy(xc[:, :], k.xnT[:, ds(g * GT, GT)]), a["xc"])
                wait(act, a["rows_turned"], g + 1)
                inc(nc.scalar.copy(rows[:, :, :].rearrange("p j n -> p (j n)"), k.ps[:, 7, :]), a["rows"])
                for e in range(ME):
                    i = (g * ME + e) * NB
                    copy(i, 0)
                    for blk in range(1, NB):
                        copy(i + blk, blk)
                        silu(i + blk - 1, e, blk - 1)
                    wait(act, a["z"], g * ME + e + 1)
                    inc(nc.scalar.activation(sz[:, e, :, :], k.ps[:, 4:8, 0:ZW], ACT.Silu), a["z_silu"])
                    silu(i + NB - 1, e, NB - 1)
                open_unit(g, 0)
                for u in range(NU + 1):
                    if u + 1 < NU:
                        open_unit(g, u + 1)
                    if u >= 1:
                        close_unit(g, u - 1)

        @block.vector
        def _(dve):
            V = nc.vector

            def convolve(g, e, blk):
                i = (g * ME + e) * NB + blk
                r, c = blk % 2, e * NB + blk
                k5 = i * 5
                wait(dve, own, k5)
                inc(V.tensor_scalar(xb[:, r, 0:TAPS - 1], tails[:, c, :], m.keep[:, ds(g, 1)], None, ALU.mult), own)
                wait(dve, a["copied"], i + 1)
                wait(dve, own, k5 + 1)
                wait(dve, a["conv_silu"], i - 1)
                inc(V.tensor_scalar(cv[:, r, :], xb[:, r, 0:GT], m.cw[:, c, 0:1], None, ALU.mult), own)
                for tap in range(1, TAPS):
                    wait(dve, own, k5 + 1 + tap)
                    ins = V.scalar_tensor_tensor(cv[:, r, :], xb[:, r, tap:tap + GT], m.cw[:, c, tap:tap + 1],
                                                 cv[:, r, :], ALU.mult, ALU.add)
                    if tap < TAPS - 1:
                        inc(ins, own)
                inc(V.tensor_copy(tails[:, c, :], xb[:, r, GT:GT + TAPS - 1]), own)
                wait(dve, own, k5 + 5)
                inc(V.tensor_copy(k.spare[:, 0:1], k.zero[:, 0:1]), a["conv"])

            def matrices(g, u):
                n, r = g * NU + u, u % 2
                wait(dve, b["L"], n + 1)
                wait(dve, b["cb"], n + 1)
                wait(dve, b["y"], n - 1)
                inc(V.tensor_tensor(M[:, r, :].rearrange("p (h l) -> p h l", h=MH), L[:, r, :].rearrange(
                    "p (h l) -> p h l", h=MH), bcast(bankCB[:, 0:P], 1, MH), ALU.mult), b["M"])

            def gated(g, u):
                j, e = u // ME, u % ME
                n, r = g * NU + u, u % 2
                heads = lambda t: t.rearrange("p (h d) -> p h d", h=MH)
                wait(dve, b["y"], n + 1)
                wait(dve, b["y2"], n)
                inc(V.tensor_tensor(heads(t1[:, :]), heads(bankY[:, ZW:2 * ZW]),
                                    bcast(m.ea[:, ds((g * GRP + j) * MEH + e * MH, MH)], 2, HD), ALU.mult), yown)
                wait(dve, yown, n * 2 + 1)
                inc(V.tensor_tensor(t2[:, :], t1[:, :], bankY[:, 0:ZW], ALU.add), yown)
                wait(dve, yown, n * 2 + 2)
                wait(dve, b["squared"], n - 1)
                wait(dve, b["yT_turned"], n - 1)
                inc(V.tensor_tensor(y2[:, r, :], t2[:, :], sz[:, e, j, :], ALU.mult), b["y2"])
                wait(dve, b["s"], n + 1)
                wait(dve, b["carried"], n + 1)
                inc(V.tensor_tensor(state[:, e, :], bankS[:, 0:ZW], carried[:, r, :], ALU.add), b["state"])

            def add(g, u):
                j = u // ME
                n, r = g * NU + u, u % 2
                wait(dve, b["out"], n + 1)
                wait(dve, b["gain"], n + 1)
                wait(dve, b["added"], n)
                xt = k.x[:, ds((g * GRP + j) * D, D)]
                inc(V.scalar_tensor_tensor(xt, bankO[:, 0:D], gain[:, r:r + 1], xt, ALU.mult, ALU.add), b["added"])

            V.memset(tails[:, :, :], 0.0)
            inc(V.memset(state[:, :, :], 0.0), init)
            wait(dve, init, 1)
            with dve.Fori(0, NG) as g:
                for e in range(ME):
                    for blk in range(NB):
                        convolve(g, e, blk)
                matrices(g, 0)
                for u in range(NU + 1):
                    if u + 1 < NU:
                        matrices(g, u + 1)
                    if u < NU:
                        gated(g, u)
                    if u >= 1:
                        add(g, u - 1)

        @block.gpsimd
        def _(pool):
            G = nc.gpsimd
            heads = lambda t: t.rearrange("p (h d) -> p h d", h=MH)

            def weigh(g, u):
                j, e = u // ME, u % ME
                n, r = g * NU + u, u % 2
                wait(pool, b["XB"], n + 1)
                wait(pool, b["s"], n - 1)
                k.settle(pool)
                inc(G.tensor_tensor(heads(Xw[:, r, :]), heads(XB[:, r, 0:ZW]),
                                    bcast(m.wst[:, ds((g * GRP + j) * MEH + e * MH, MH)], 2, HD), ALU.mult), b["Xw"])

            def carry(g, u):
                j, e = u // ME, u % ME
                n, r = g * NU + u, u % 2
                wait(pool, b["state"], n - 1)
                k.settle(pool)
                inc(G.tensor_tensor(heads(carried[:, r, :]), heads(state[:, e, :]),
                                    bcast(m.cd[:, ds((g * GRP + j) * MEH + e * MH, MH)], 2, HD), ALU.mult), b["carried"])

            def normalise(g, u):
                j, e = u // ME, u % ME
                n, r = g * NU + u, u % 2
                wait(pool, b["squared"], n + 1)
                wait(pool, b["added"], n - 1)
                inc(G.tensor_tensor(rs[:, r:r + 1], ss[:, r:r + 1], k.eps[:, 0:1], ALU.add), gown)
                wait(pool, gown, n * 2 + 1)
                inc(G.tensor_tensor(rs[:, r:r + 1], rs[:, r:r + 1], k.minus_half[:, 0:1], ALU.pow), gown)
                wait(pool, gown, n * 2 + 2)
                k.settle(pool)
                inc(G.tensor_tensor(gain[:, r:r + 1], rs[:, r:r + 1], m.rout[:, ds((g * GRP + j) * ME + e, 1)],
                                    ALU.mult), b["gain"])

            wait(pool, init, 1)
            with pool.Fori(0, NG) as g:
                weigh(g, 0)
                for u in range(NU + 1):
                    if u < NU:
                        carry(g, u)
                    if u + 1 < NU:
                        weigh(g, u + 1)
                    if u >= 1:
                        normalise(g, u - 1)

    for n in ("xc", "rows_turned", "rows"):
        a[n].close(NG)
    for n in ("proj", "copied", "conv", "conv_silu"):
        a[n].close(NG * ME * NB)
    for n in ("z", "z_silu"):
        a[n].close(NG * ME)
    own.close(NG * ME * NB * 5)
    for s in b.values():
        s.close(NG * NU)
    yown.close(NG * NU * 2)
    gown.close(NG * NU * 2)
    init.close(1)

def setup(k, w):
    nc = k.nc
    k.counter("settled")
    loads, made, own = k.counter("setup_loads", 16), k.counter("setup_made"), k.counter("setup_step")
    S = k.sb
    k.x, k.xnT = S("x", [P, NT * D]), S("xnT", [P, TOK])
    k.xn4, k.xt4 = S("xn4", [P, 2, GRP, D]), S("xt4", [P, 2, GRP * P])
    k.stat, k.mv, k.rstd = S("stat", [P, 2, GRP, 6]), S("mv", [P, 2, GRP, 2]), S("rstd", [P, 2, GRP])
    k.logits = S("logits", [P, NT * NM])
    k.ident, k.ones, k.zero = S("ident", [P, P]), S("ones", [P, P]), S("zero", [P, 1])
    k.ones_bf, k.zeros_bf, k.before = S("ones_bf", [P, P], BF16), S("zeros_bf", [P, 2 * SLOTS2], BF16), S("before", [P, P], BF16)
    k.iota, k.lane, k.tile_of = S("iota", [P, P]), S("lane", [P, 1]), S("tile_of", [P, 2 * NT])
    k.falling, k.carry, k.minus_half = S("falling", [P, NE]), S("carry", [P, NE * NT]), S("minus_half", [P, GRP])
    k.mw = S("mw", [P, NM])
    k.spare, k.eps = S("spare", [P, 4]), S("eps", [P, GRP])
    k.rt = [S(f"rt{i}", [P, NE * NT]) for i in range(5)]
    k.best, k.small, k.gate = S("best", [P, 2, NT]), S("small", [P, 2 * NT]), S("gate", [P, 2, NT])
    k.marks = S("marks", [P, NE * NT], BF16)
    k.n_int, k.e8 = S("n_int", [P, NE], I32), S("e8", [P, 3, NE])
    k.posf, k.pos, k.hi_int = S("posf", [P, 2 * NT]), S("pos", [P, 2 * NT], U32), S("hi_int", [P, 2 * NT], I32)
    k.hi, k.lo, k.erow = S("hi", [P, 2 * NT]), S("lo", [P, 2 * NT]), S("erow", [P, SLOTS2])
    k.slot_expert, k.slot_token = S("slot_expert", [P, SLOTS2], I32), S("slot_token", [P, SLOTS2], U32)
    k.oh_lane, k.oh_slot = S("oh_lane", [P, 2, P], BF16), S("oh_slot", [P, 2, 2 * SLOTS2], BF16)
    k.wg0, k.wg1, k.bg = S("wg0", [P, NE]), S("wg1", [P, NE]), S("bg", [P, NE])
    k.index = S("index", [P, 4], U32)
    k.ps = k.ctx.enter_context(nc.psum_tensor("ps", [P, 8, 512], F32))
    k.xn_rows = nc.dram_tensor("xn_rows", [TOK, D], F32, kind="Internal").ap()
    k.y_rows = nc.dram_tensor("y_rows", [SLOTS2 * P, D], F32, kind="Internal").ap()

    copies = [
        (k.x[:, :].rearrange("p (t d) -> p t d", t=NT), w["L0_attn_x"].rearrange("b (t p) d -> p (b t) d", p=P)),
        (k.wg0[:, :], w["L0_ffn_Wg"]),
        (k.wg1[:, :], w["L1_ffn_Wg"]),
        (k.bg[:, :], w["L1_ffn_bg"].unsqueeze(0).to_broadcast([P, NE])),
        (k.mw[:, 0:ME], w["L0_attn_router_w"]),
        (k.mw[:, ME:NM].rearrange("p (e h) -> p e h", e=ME), w["L0_attn_in_w"].rearrange("e d n -> d e n")[:, :, ZW + CW:]),
    ]

    k.start()
    with nc.Block() as block:
        @block.sync
        def _(sp):
            for dst, src in copies:
                sp.dma_start(dst, src, allow_slow_non_contiguous=True).then_inc(loads.sem, 16)
            sp.wait_ge(loads.sem, loads.at(len(copies)))

        @block.gpsimd
        def _(pool):
            G = nc.gpsimd
            do = Chain(pool, made)
            do(G.memset(k.ones[:, :], 1.0))
            do(G.affine_select(out=k.ident[:, :], in_=k.ones[:, :], compare_op=ALU.is_equal, fill=0.0, base=0,
                               pattern=[[1, P]], channel_multiplier=-1))
            do(G.affine_select(out=k.before[:, :], in_=k.ones[:, :], compare_op=ALU.is_gt, fill=0.0, base=0,
                               pattern=[[1, P]], channel_multiplier=-1))
            do(G.memset(k.zero[:, :], 0.0))
            do(G.memset(k.minus_half[:, :], -0.5))
            do(G.memset(k.eps[:, :], EPS))
            do(G.iota(k.iota[:, :], pattern=[[1, P]], base=0, channel_multiplier=0, allow_small_or_imprecise_dtypes=True))
            do(G.iota(k.lane[:, :], pattern=[[1, 1]], base=0, channel_multiplier=1, allow_small_or_imprecise_dtypes=True))
            do(G.iota(k.tile_of[:, :], pattern=[[0, 2], [1, NT]], base=0, channel_multiplier=0, allow_small_or_imprecise_dtypes=True))
            do(G.iota(k.falling[:, :], pattern=[[-1, NE]], base=NE, channel_multiplier=0, allow_small_or_imprecise_dtypes=True))

        @block.vector
        def _(dve):
            V = nc.vector
            do = Chain(dve, own)
            do(V.memset(k.ones_bf[:, :], 1.0))
            do(V.memset(k.zeros_bf[:, :], 0.0))
            do(V.memset(k.carry[:, :], 1.0))
            do(V.memset(k.carry[:, :].rearrange("p (e t) -> p e t", e=NE)[:, :, 0:1], 0.0))


def store(k, out):
    nc = k.nc
    done = k.counter("output_stored", 16)
    k.start()
    with nc.Block() as block:
        @block.sync
        def _(sp):
            sp.dma_start(out.rearrange("b (t p) d -> p (b t) d", p=P), k.x[:, :].rearrange("p (t d) -> p t d", t=NT)
                         ).then_inc(done.sem, 16)
            sp.wait_ge(done.sem, done.at(1))


SLOTS1 = (TOK + NE * (P - 1)) // P
SLOTS2 = (2 * TOK + NE * (P - 1)) // P


def macaron(nc, w, out):
    with ExitStack() as ctx:
        k = Bench(nc, ctx)
        setup(k, w)
        for stage in STAGES:
            {"ffn0": ffn0, "ffn1": ffn1, "attn": attend, "mamba": mamba}[stage](k, w)
        store(k, out)


def ffn0(k, w):
    with ExitStack() as stack:
        S = k.scope(stack)
        k.w12, k.w3 = S("w12", [P, NE + 1, 2 * FF]), S("w3", [P, NE + 1, FB, D])
        k.gl, k.inner = S("gl", [P, 2, GRP * P]), S("inner", [P, 2, FB, GRP * P])
        k.rows_in, k.gT, k.w_slot = S("rows_in", [P, 2, D]), S("gT", [P, 2, P]), S("w_slot", [P, 2, 2 * FF])
        k.inner_slot, k.y, k.back = S("inner_slot", [P, 2, FF]), S("y", [P, 2, D]), S("back", [P, 4, D])
        loads = [
            (k.w12[:, NE, 0:FF], w["L0_ffn_w1s"]),
            (k.w12[:, NE, FF:2 * FF], w["L0_ffn_w2s"]),
            (k.w3[:, NE], w["L0_ffn_w3s"].rearrange("(b p) d -> p b d", p=P)),
            (k.w12[:, 0:NE, 0:FF], w["L0_ffn_W1"].rearrange("e d f -> d e f")),
            (k.w12[:, 0:NE, FF:2 * FF], w["L0_ffn_W2"].rearrange("e d f -> d e f")),
            (k.w3[:, 0:NE].rearrange("p e b d -> p (e b) d"), w["L0_ffn_W3"].rearrange("e (b p) d -> p (e b) d", p=P)),
        ]
        prepare(k, k.wg0[:, :], NE, loads)
        route(k, 1, SLOTS1)
        shared(k)
        experts(k, 1, SLOTS1)


def ffn1(k, w):
    nc = k.nc
    done = k.counter("router_biased")
    with ExitStack() as stack:
        S = k.scope(stack)
        k.w1, k.w2 = S("w1", [P, NE, FF]), S("w2", [P, NE, FB, D])
        k.b1, k.b2 = S("b1", [P, NE * FB]), S("b2", [P, NE * D])
        k.rows_in, k.gT, k.w_slot = S("rows_in", [P, 2, D]), S("gT", [P, 2, P]), S("w_slot", [P, 2, FF])
        k.inner_slot, k.hb, k.y = S("inner_slot", [P, 2, FF]), S("hb", [P, 2, FF]), S("y", [P, 2, D])
        k.back = S("back", [P, 4, D])
        loads = [
            (k.w1[:, :, :], w["L1_ffn_W1"].rearrange("e d f -> d e f")),
            (k.b2[:, :], w["L1_ffn_b2"].rearrange("e d -> (e d)").unsqueeze(0).to_broadcast([P, NE * D])),
            (k.w2[:, :].rearrange("p e b d -> p (e b) d"), w["L1_ffn_W2"].rearrange("e (b p) d -> p (e b) d", p=P)),
            (k.b1[:, :], w["L1_ffn_b1"].rearrange("e (b p) -> p (e b)", p=P)),
        ]
        prepare(k, k.wg1[:, :], NE, loads)
        k.start()
        with nc.Block() as block:
            @block.vector
            def _(dve):
                l3 = k.logits[:, 0:NT * NE].rearrange("p (t e) -> p t e", e=NE)
                nc.vector.tensor_tensor(l3, l3, bcast(k.bg[:, :], 1, NT), ALU.add).then_inc(done.sem, 1)
                for e in range(1, NE, 2):
                    nc.vector.tensor_scalar(k.w2[:, e], k.w2[:, e], 0.5, None, ALU.mult).then_inc(done.sem, 1)
                dve.wait_ge(done.sem, done.at(1 + NE // 2))
        done.close(1 + NE // 2)
        route(k, 2, SLOTS2)
        experts(k, 2, SLOTS2)


_INS = ['L0_attn_x', 'L0_attn_router_w', 'L0_attn_in_w', 'L0_attn_conv_w', 'L0_attn_conv_b', 'L0_attn_dt_bias',
        'L0_attn_A_log', 'L0_attn_D_skip', 'L0_attn_norm_w', 'L0_attn_out_w', 'L0_ffn_w1s', 'L0_ffn_w2s', 'L0_ffn_w3s',
        'L0_ffn_W1', 'L0_ffn_W2', 'L0_ffn_W3', 'L0_ffn_Wg', 'L1_attn_w_q', 'L1_attn_b_q', 'L1_attn_w_k', 'L1_attn_b_k',
        'L1_ffn_W1', 'L1_ffn_b1', 'L1_ffn_W2', 'L1_ffn_b2', 'L1_ffn_Wg', 'L1_ffn_bg']


def kernel(**inputs):
    import numpy as _np
    import concourse.bacc as _bacc
    from concourse import mybir as _mybir
    from concourse.bass_utils import run_bass_kernel_spmd as _run

    nc = _bacc.Bacc("TRN2", target_bir_lowering=False, num_devices=1)
    arrays, w = {}, {}
    for name in _INS:
        a = _np.ascontiguousarray(inputs[name])
        arrays[f"in_{name}"] = a
        w[name] = nc.dram_tensor(f"in_{name}", a.shape, _mybir.dt.from_np(a.dtype), kind="ExternalInput").ap()
    out = nc.dram_tensor("out_x", (BATCH, SEQ, D), _mybir.dt.float32, kind="ExternalOutput").ap()
    macaron(nc, w, out)
    r = _run(nc, [arrays], core_ids=[0])
    return r.results[0]["out_x"]
```

```python
import numpy as np
import concourse.bass as bass
from concourse import mybir
from contextlib import ExitStack

F32 = mybir.dt.float32
BF16 = mybir.dt.bfloat16
I32 = mybir.dt.int32
U32 = mybir.dt.uint32
ALU = mybir.AluOpType
ACT = mybir.ActivationFunctionType
AX = mybir.AxisListType
ds = bass.ds

STAGES = ("ffn0", "mamba", "ffn0", "ffn1", "attn", "ffn1")

P = 128
D = 128
BATCH, SEQ = 4, 1024
TOK = BATCH * SEQ
NT = TOK // P
GRP = 4
NG = NT // GRP
NE = 8
FF = 512
FB = FF // P
EPS = 1e-5
ME, MH = 4, 4
ZW, CW = 256, 512
HD = ZW // MH
MEH = ME * MH
NM = ME + MEH
TAPS = 4
QK = 16
LEAD = 4


class Signal:

    def __init__(self, nc, ctx, name, unit=1, lead=LEAD):
        self.sem = ctx.enter_context(nc.semaphore(name))
        self.unit = unit
        self.base = self.lead = lead * unit

    def at(self, n):
        return n * self.unit + self.base

    def close(self, total):
        self.base += total * self.unit


class Bench:

    def __init__(self, nc, ctx):
        self.nc, self.ctx, self.counters, self.new, self.stages = nc, ctx, {}, [], 0
        self.pending = (0, 0)

    def sb(self, name, shape, dt=F32):
        return self.ctx.enter_context(self.nc.sbuf_tensor(name, shape, dt))

    def scope(self, stack):
        self.stages += 1
        tag = self.stages
        return lambda name, shape, dt=F32: stack.enter_context(self.nc.sbuf_tensor(f"{name}_{tag}", shape, dt))

    def counter(self, name, unit=1, lead=LEAD):
        if name not in self.counters:
            self.counters[name] = Signal(self.nc, self.ctx, name, unit, lead)
            self.new.append(self.counters[name])
        return self.counters[name]

    def settle(self, eng):
        eng.sem_inc(self.counters["settled"].sem, 1)

    def start(self):
        if self.new:
            with self.nc.Block() as block:
                @block.sync
                def _(sp):
                    for s in self.new:
                        if s.lead:
                            sp.sem_inc(s.sem, s.lead)
            self.new = []


def bcast(ap, axis, n):
    shape = list(ap.shape)
    return ap.unsqueeze(axis).to_broadcast(shape[:axis] + [n] + shape[axis:])


class Chain:

    def __init__(self, eng, signal, start=0):
        self.eng, self.count, self.n = eng, signal, start

    def __call__(self, ins):
        self.n += 1
        ins.then_inc(self.count.sem, 1)
        self.eng.wait_ge(self.count.sem, self.count.at(self.n))


def in_turn(eng, n, ahead, behind):
    ahead(0, 0, 0)
    with eng.Fori(0, n // 2 - 1) as i:
        ahead(i * 2 + 1, 1, i)
        behind(i * 2, 0, i)
        ahead(i * 2 + 2, 0, i + 1)
        behind(i * 2 + 1, 1, i)
    ahead(n - 1, 1, n // 2 - 1)
    behind(n - 2, 0, n // 2 - 1)
    behind(n - 1, 1, n // 2 - 1)


def rounds(eng, n, lag, ring, step):
    def fixed(t):
        return lambda behind: (t - behind, (t - behind) % ring, (t - behind) // ring) if 0 <= t - behind < n else None

    full = (n - lag) // ring
    for t in range(lag):
        step(fixed(t))
    with eng.Fori(0, full) as i:
        for q in range(ring):
            step(lambda behind: (i * ring + (lag + q - behind), (lag + q - behind) % ring,
                                 i + (lag + q - behind) // ring))
    for t in range(lag + full * ring, n + lag):
        step(fixed(t))


def prepare(k, S, router, nr, loads):
    nc = k.nc
    top, slots, x = k.pending[0], k.pending[1], k.x
    k.pending = (0, 0)
    weights_in = k.counter("weights_in", 16)
    var_ready, rstd_ready, xn_ready = (k.counter(n) for n in ("prep_var_ready", "prep_rstd_ready", "prep_xn_ready"))
    own, pool_own = k.counter("prep_vector_step"), k.counter("prep_pool_step")
    transposed, xt_copied, routed, logits_kept = (
        k.counter(n) for n in ("prep_transposed", "prep_xt_copied", "prep_routed", "prep_logits_kept"))
    stored = [k.counter(f"prep_stored{r}", 16) for r in range(2)]
    index_ready, added, k.first_added = (k.counter(f"back_{n}") for n in ("index_ready", "added", "first_added"))
    NR = GRP * top
    fetched = [k.counter(f"back_fetched{n}", 16, lead=0) for n in range(2 * NR)]
    xn4, xt4, xnT, stat, mv, rstd = k.xn4, k.xt4, k.xnT, k.stat, k.mv, k.rstd
    back = S("back", [P, 2 * NR, D]) if top else None
    rows = k.xn_rows.rearrange("(g j p) d -> p g j d", p=P, j=GRP)
    ps_t, ps_r = k.ps[:, 0:2, :], k.ps[:, 2:4, :]

    k.start()
    with nc.Block() as block:
        @block.vector
        def _(dve):
            V = nc.vector

            def statistics(g, r, i):
                take_back(k, dve, g, r, i, top, back, fetched, added)
                for j in range(GRP):
                    ins = V.bn_stats(stat[:, r, j, :], x[:, ds((g * GRP + j) * D, D)])
                ins.then_inc(own.sem, 1)
                dve.wait_ge(own.sem, own.at(g + 1))
                k.settle(dve)
                for j in range(GRP):
                    ins = V.bn_aggr(mv[:, r, j, :], stat[:, r, j, :])
                ins.then_inc(var_ready.sem, 1)

            def normalise(g, r, i):
                dve.wait_ge(rstd_ready.sem, rstd_ready.at(g + 1))
                dve.wait_ge(transposed.sem, transposed.at(g - 1))
                dve.wait_ge(stored[r].sem, stored[r].at(i))
                for j in range(GRP):
                    ins = V.tensor_scalar(xn4[:, r, j, :], x[:, ds((g * GRP + j) * D, D)],
                                          mv[:, r, j, 0:1], rstd[:, r, j:j + 1], ALU.subtract, ALU.mult)
                ins.then_inc(xn_ready.sem, 1)

            in_turn(dve, NG, statistics, normalise)

        @block.gpsimd
        def _(pool):
            def fetch(g, r, i):
                fetch_back(k, pool, g, r, top, slots, back, index_ready, fetched, added)

            def root(g, r, i):
                pool.wait_ge(var_ready.sem, var_ready.at(g + 1))
                pool.wait_ge(xn_ready.sem, xn_ready.at(g - 1))
                nc.gpsimd.tensor_tensor(rstd[:, r, :], mv[:, r, :, 1], k.eps[:, 0:GRP], ALU.add).then_inc(pool_own.sem, 1)
                pool.wait_ge(pool_own.sem, pool_own.at(g + 1))
                nc.gpsimd.tensor_tensor(rstd[:, r, :], rstd[:, r, :], k.minus_half[:, 0:GRP],
                                        ALU.pow).then_inc(rstd_ready.sem, 1)

            in_turn(pool, NG, fetch, root)

        @block.sync
        def _(sp):
            for dst, src in loads:
                sp.dma_start(dst, src, allow_slow_non_contiguous=True).then_inc(weights_in.sem, 16)
            with sp.Fori(0, NG // 2) as i:
                for r in range(2):
                    g = i * 2 + r
                    sp.wait_ge(xn_ready.sem, xn_ready.at(g + 1))
                    sp.wait_ge(stored[r].sem, stored[r].at(i))
                    sp.dma_start(rows[:, ds(g, 1)].rearrange("p g j d -> p (g j) d"), xn4[:, r, :, :]).then_inc(stored[r].sem, 16)
            for r in range(2):
                sp.wait_ge(stored[r].sem, stored[r].at(NG // 2))
            sp.wait_ge(weights_in.sem, weights_in.at(len(loads)))

        @block.tensor
        def _(pe):
            def transpose(g, r, i):
                pe.wait_ge(xn_ready.sem, xn_ready.at(g + 1))
                pe.wait_ge(xt_copied.sem, xt_copied.at(g - 1))
                for j in range(GRP):
                    ins = nc.tensor.transpose(ps_t[:, r, j * P:(j + 1) * P], xn4[:, r, j, :], k.ident[:, :])
                ins.then_inc(transposed.sem, 1)

            def score(g, r, i):
                if nr:
                    pe.wait_ge(xt_copied.sem, xt_copied.at(g + 1))
                    pe.wait_ge(logits_kept.sem, logits_kept.at(g - 1))
                    for j in range(GRP):
                        ins = nc.tensor.matmul(ps_r[:, r, j * nr:(j + 1) * nr], xt4[:, r, j * P:(j + 1) * P],
                                               router, start=True, stop=True)
                    ins.then_inc(routed.sem, 1)

            in_turn(pe, NG, transpose, score)

        @block.scalar
        def _(act):
            def copy(g, r, i):
                act.wait_ge(transposed.sem, transposed.at(g + 1))
                if nr:
                    act.wait_ge(routed.sem, routed.at(g - 1))
                    nc.scalar.copy(xt4[:, r, :], ps_t[:, r, :])
                nc.scalar.copy(xnT[:, ds(g * GRP * P, GRP * P)], ps_t[:, r, :]).then_inc(xt_copied.sem, 1)

            def keep(g, r, i):
                if nr:
                    act.wait_ge(routed.sem, routed.at(g + 1))
                    nc.scalar.copy(k.logits[:, ds(g * GRP * nr, GRP * nr)], ps_r[:, r, 0:GRP * nr]
                                   ).then_inc(logits_kept.sem, 1)

            in_turn(act, NG, copy, keep)

    weights_in.close(len(loads))
    for s in (var_ready, rstd_ready, xn_ready, own, pool_own, transposed, xt_copied):
        s.close(NG)
    if nr:
        routed.close(NG)
        logits_kept.close(NG)
    for s in stored:
        s.close(NG // 2)
    close_back(k, top, index_ready, fetched, added)


def fetch_back(k, pool, g, r, top, slots, back, index_ready, fetched, added):
    if not top:
        return
    NR = GRP * top
    pool.wait_ge(added.sem, added.at(g - 1))
    k.settle(pool)
    for c in range(top):
        ins = k.nc.gpsimd.tensor_copy(k.index[:, r * NR + c * GRP:r * NR + (c + 1) * GRP],
                                      k.pos[:, ds(g * GRP + c * NT, GRP)])
    ins.then_inc(index_ready.sem, 1)
    pool.wait_ge(index_ready.sem, index_ready.at(g + 1))
    k.settle(pool)
    for n in range(r * NR, (r + 1) * NR):
        k.nc.gpsimd.indirect_dma_start(back[:, n, :], None, k.y_rows[0:slots * P, :],
                                       bass.IndirectOffsetOnAxis(ap=k.index[:, n:n + 1], axis=0)
                                       ).then_inc(fetched[n].sem, 16)


def take_back(k, dve, g, r, i, top, back, fetched, added):
    if not top:
        return
    NR = GRP * top
    V = k.nc.vector
    for n in range(r * NR, r * NR + GRP):
        dve.wait_ge(fetched[n].sem, fetched[n].at(i + 1))
    if top == 1:
        xg = k.x[:, ds(g * GRP * D, GRP * D)]
        V.scalar_tensor_tensor(xg, back[:, r * NR:(r + 1) * NR, :].rearrange("p j d -> p (j d)"), 0.5, xg,
                               ALU.mult, ALU.add).then_inc(added.sem, 1)
        dve.wait_ge(added.sem, added.at(g + 1))
        k.settle(dve)
        return
    for c in range(top):
        for j in range(GRP):
            n = r * NR + c * GRP + j
            if c:
                dve.wait_ge(fetched[n].sem, fetched[n].at(i + 1))
            xt = k.x[:, ds((g * GRP + j) * D, D)]
            ins = V.scalar_tensor_tensor(xt, back[:, n, :], k.gate[:, c, ds(g * GRP + j, 1)], xt, ALU.mult, ALU.add)
        if c == 0:
            ins.then_inc(k.first_added.sem, 1)
            dve.wait_ge(k.first_added.sem, k.first_added.at(g + 1))
    ins.then_inc(added.sem, 1)
    dve.wait_ge(added.sem, added.at(g + 1))
    k.settle(dve)


def close_back(k, top, index_ready, fetched, added):
    if top == 2:
        k.first_added.close(NG)
    if top:
        index_ready.close(NG)
        added.close(NG)
        for s in fetched:
            s.close(NG // 2)


def route(k, top, slots, alone):
    nc = k.nc
    own = k.counter("route_vector_step")
    marks, counted = k.counter("route_marks_ready"), k.counter("route_counted")
    weights, expd = k.counter("route_difference_ready"), k.counter("route_exp_done")
    place_counters(k)
    NB = top * NG
    L3 = k.logits[:, 0:NT * NE].rearrange("p (t e) -> p t e", e=NE)
    r3 = [k.rt[i][:, :].rearrange("p (t e) -> p t e", e=NE) for i in range(5)]
    e3 = [k.rt[i][:, :].rearrange("p (e t) -> p e t", e=NE) for i in range(5)]
    NP = top * NT
    ps_rank, ps_cnt = k.ps[:, 0, 0:NE * NT], k.ps[:, 1, 0:NE * NT]
    V = nc.vector

    k.start()
    with nc.Block() as block:
        @block.vector
        def _(dve):
            do = Chain(dve, own)
            logit, eq, sel = L3, r3[4], [r3[0], r3[1]]
            for c in range(top):
                do(V.tensor_reduce(k.best[:, c, :], logit, AX.X, ALU.max))
                do(V.tensor_tensor(eq, logit, bcast(k.best[:, c, :], 2, NE), ALU.is_equal))
                do(V.tensor_tensor(eq, eq, bcast(k.falling[:, :], 1, NT), ALU.mult))
                do(V.tensor_reduce(k.small[:, 0:NT], eq, AX.X, ALU.max))
                do(V.tensor_tensor(sel[c], eq, bcast(k.small[:, 0:NT], 2, NE), ALU.is_equal))
                if c + 1 < top:
                    do(V.scalar_tensor_tensor(r3[3], sel[c], -1e30, L3, ALU.mult, ALU.add))
                    logit = r3[3]
            if top == 2:
                V.tensor_sub(k.small[:, 0:NT], k.best[:, 1, :], k.best[:, 0, :]).then_inc(weights.sem, 1)
                dve.wait_ge(expd.sem, expd.at(1))
                do(V.tensor_scalar(k.small[:, NT:2 * NT], k.small[:, 0:NT], 1.0, None, ALU.add))
                do(V.reciprocal(k.gate[:, 0, :], k.small[:, NT:2 * NT]))
                do(V.tensor_scalar(k.gate[:, 0, :], k.gate[:, 0, :], 0.5, None, ALU.mult))
                do(V.tensor_mul(k.gate[:, 1, :], k.small[:, 0:NT], k.gate[:, 0, :]))
                do(V.tensor_add(r3[4], sel[0], sel[1]))
                V.tensor_copy(k.marks[:, :].rearrange("p (e t) -> p t e", e=NE), r3[4]).then_inc(marks.sem, 1)
            else:
                V.tensor_copy(k.marks[:, :].rearrange("p (e t) -> p t e", e=NE), sel[0]).then_inc(marks.sem, 1)
            dve.wait_ge(counted.sem, counted.at(1))
            cnt, incl = k.rt[2], k.rt[3]
            do(V.tensor_copy(cnt[:, :], ps_cnt))
            do(V.tensor_tensor_scan(incl[:, :], k.carry[:, :], cnt[:, :], 0.0, ALU.mult, ALU.add))
            do(V.tensor_sub(cnt[:, :], incl[:, :], cnt[:, :]))
            do(V.tensor_tensor(cnt[:, :], cnt[:, :], ps_rank, ALU.add))
            do(V.tensor_scalar(k.n_int[:, :], e3[3][:, :, NT - 1], float(P - 1), None, ALU.add))
            do(V.tensor_single_scalar(k.n_int[:, :], k.n_int[:, :], 7, ALU.arith_shift_right))
            do(V.tensor_copy(k.e8[:, 0, :], k.n_int[:, :]))
            do(V.tensor_tensor_scan(k.e8[:, 1, :], k.ones[:, 0:NE], k.e8[:, 0, :], 0.0, ALU.mult, ALU.add))
            do(V.tensor_sub(k.e8[:, 1, :], k.e8[:, 1, :], k.e8[:, 0, :]))
            do(V.tensor_scalar(k.e8[:, 2, :], k.e8[:, 1, :], float(P), None, ALU.mult))
            do(V.tensor_tensor(e3[3], e3[2], bcast(k.e8[:, 2, :], 2, NT), ALU.add))
            for c in range(top):
                cols = slice(c * NT, (c + 1) * NT)
                do(V.tensor_tensor(r3[4], sel[c], k.rt[3][:, :].rearrange("p (e t) -> p t e", e=NE), ALU.mult))
                do(V.tensor_reduce(k.posf[:, cols], r3[4], AX.X, ALU.add))
            do(V.tensor_copy(k.pos[:, 0:NP], k.posf[:, 0:NP]))
            do(V.tensor_single_scalar(k.hi_int[:, 0:NP], k.pos[:, 0:NP].bitcast(I32), 7, ALU.arith_shift_right))
            do(V.tensor_copy(k.hi[:, 0:NP], k.hi_int[:, 0:NP]))
            do(V.scalar_tensor_tensor(k.lo[:, 0:NP], k.hi[:, 0:NP], -float(P), k.posf[:, 0:NP], ALU.mult, ALU.add))
            do(V.tensor_scalar(k.erow[:, 0:slots], k.iota[:, 0:slots], k.e8[:, 1, 1:2], None, ALU.is_ge))
            for e in range(2, NE):
                do(V.scalar_tensor_tensor(k.erow[:, 0:slots], k.iota[:, 0:slots], k.e8[:, 1, e:e + 1],
                                          k.erow[:, 0:slots], ALU.is_ge, ALU.add))
            do(V.tensor_copy(k.slot_expert[:, 0:slots], k.erow[:, 0:slots]))
            if alone:
                with dve.Fori(0, NB // 2) as i:
                    for r in range(2):
                        place_vector(k, dve, i * 2 + r, r, slots)
                place_end(k, dve, NB, slots)
            k.route_steps = do.n

        @block.scalar
        def _(act):
            if top == 2:
                act.wait_ge(weights.sem, weights.at(1))
                nc.scalar.activation(k.small[:, 0:NT], k.small[:, 0:NT], ACT.Exp).then_inc(expd.sem, 1)

        @block.tensor
        def _(pe):
            pe.wait_ge(marks.sem, marks.at(1))
            nc.tensor.matmul(ps_rank, k.before[:, :], k.marks[:, :], start=True, stop=True)
            nc.tensor.matmul(ps_cnt, k.ones_bf[:, :], k.marks[:, :], start=True, stop=True).then_inc(counted.sem, 1)
            if alone:
                open_table(k, slots)
                with pe.Fori(0, NB // 2) as i:
                    for r in range(2):
                        place_tensor(k, pe, i * 2 + r, r, slots)

    own.close(k.route_steps)
    marks.close(1)
    counted.close(1)
    if top == 2:
        weights.close(1)
        expd.close(1)
    if alone:
        close_places(k, NB)


def place_counters(k):
    k.onehot, k.placed, k.place_own = (k.counter(f"place_{n}") for n in ("onehot_ready", "done", "step"))


def close_places(k, batches):
    k.onehot.close(batches)
    k.placed.close(batches)
    k.place_own.close(2)


def place_vector(k, dve, n, r, slots):
    V = k.nc.vector
    dve.wait_ge(k.placed.sem, k.placed.at(n - 1))
    for j in range(GRP):
        t = n * GRP + j
        V.tensor_scalar(k.oh_lane[:, r, j, :], k.iota_bf[:, 0:P], k.lo[:, ds(t, 1)], None, ALU.is_equal)
        V.tensor_scalar(k.oh_slot[:, r, j, 0:slots], k.iota_bf[:, 0:slots], k.hi[:, ds(t, 1)],
                        k.lane[:, 0:1], ALU.is_equal, ALU.mult)
        ins = V.tensor_scalar(k.oh_slot[:, r, j, slots:2 * slots], k.iota_bf[:, 0:slots], k.hi[:, ds(t, 1)],
                              k.tile_of[:, ds(t, 1)], ALU.is_equal, ALU.mult)
    ins.then_inc(k.onehot.sem, 1)


def place_end(k, dve, batches, slots):
    V, table, own = k.nc.vector, k.ps[:, 6, 0:2 * slots], k.place_own
    dve.wait_ge(k.placed.sem, k.placed.at(batches))
    V.tensor_copy(k.erow[:, 0:slots], table[:, 0:slots]).then_inc(own.sem, 1)
    dve.wait_ge(own.sem, own.at(1))
    V.scalar_tensor_tensor(k.slot_token[:, 0:slots], table[:, slots:2 * slots], float(P), k.erow[:, 0:slots],
                           ALU.mult, ALU.add).then_inc(own.sem, 1)
    dve.wait_ge(own.sem, own.at(2))


def open_table(k, slots):
    k.nc.tensor.matmul(k.ps[:, 6, 0:2 * slots], k.ones_bf[:, :], k.zeros_bf[:, 0:2 * slots], start=True,
                       stop=False, skip_group_check=True)


def place_tensor(k, pe, n, r, slots):
    pe.wait_ge(k.onehot.sem, k.onehot.at(n + 1))
    for j in range(GRP):
        ins = k.nc.tensor.matmul(k.ps[:, 6, 0:2 * slots], k.oh_lane[:, r, j, :], k.oh_slot[:, r, j, 0:2 * slots],
                                 start=False, stop=False, skip_group_check=True)
    ins.then_inc(k.placed.sem, 1)


def shared(k, slots):
    nc = k.nc
    place_counters(k)
    up, acted, ready, down_done, added = (k.counter(f"shared_{n}") for n in ("up", "acted", "inner_ready", "down", "added"))
    w12, w3 = k.w12[:, NE, :], k.w3[:, NE]
    h1, h2, py = k.ps[:, 0:2, :], k.ps[:, 2:4, :], k.ps[:, 4:6, :]
    NU = NG * FB

    k.start()
    with nc.Block() as block:
        @block.tensor
        def _(pe):
            def up_block(g, b):
                u, r = g * FB + b, b % 2
                pe.wait_ge(ready.sem, ready.at(u - 1))
                nc.tensor.matmul(h1[:, r, :], w12[:, b * P:(b + 1) * P], k.xnT[:, ds(g * GRP * P, GRP * P)],
                                 start=True, stop=True)
                nc.tensor.matmul(h2[:, r, :], w12[:, FF + b * P:FF + (b + 1) * P],
                                 k.xnT[:, ds(g * GRP * P, GRP * P)], start=True, stop=True).then_inc(up.sem, 1)

            def down_group(g, r):
                pe.wait_ge(ready.sem, ready.at((g + 1) * FB))
                pe.wait_ge(added.sem, added.at(g - 1))
                for j in range(GRP):
                    for b in range(FB):
                        ins = nc.tensor.matmul(py[:, r, j * P:(j + 1) * P], k.inner[:, r, b, j * P:(j + 1) * P],
                                               w3[:, b, :], start=(b == 0), stop=(b == FB - 1))
                ins.then_inc(down_done.sem, 1)

            def up_group(g, r, i):
                for b in range(FB):
                    up_block(g, b)

            def down(g, r, i):
                place_tensor(k, pe, g, r, slots)
                down_group(g, r)

            open_table(k, slots)
            in_turn(pe, NG, up_group, down)

        @block.scalar
        def _(act):
            with act.Fori(0, NG) as g:
                for b in range(FB):
                    u = g * FB + b
                    act.wait_ge(up.sem, up.at(u + 1))
                    act.wait_ge(ready.sem, ready.at(u - 1))
                    nc.scalar.activation(k.gl[:, b % 2, :], h1[:, b % 2, :], ACT.Gelu).then_inc(acted.sem, 1)

        @block.vector
        def _(dve):
            def inner(g, r):
                dve.wait_ge(down_done.sem, down_done.at(g - 1))
                for b in range(FB):
                    u = g * FB + b
                    dve.wait_ge(acted.sem, acted.at(u + 1))
                    nc.vector.tensor_tensor(k.inner[:, r, b, :], k.gl[:, b % 2, :], h2[:, b % 2, :],
                                            ALU.mult).then_inc(ready.sem, 1)

            def add(g, r):
                dve.wait_ge(down_done.sem, down_done.at(g + 1))
                xg = k.x[:, ds(g * GRP * D, GRP * D)]
                nc.vector.scalar_tensor_tensor(xg, py[:, r, :], 0.5, xg, ALU.mult, ALU.add).then_inc(added.sem, 1)

            def ahead(g, r, i):
                inner(g, r)
                place_vector(k, dve, g, r, slots)

            in_turn(dve, NG, ahead, lambda g, r, i: add(g, r))
            place_end(k, dve, NG, slots)
            dve.wait_ge(added.sem, added.at(NG))

    for s in (up, acted, ready):
        s.close(NU)
    down_done.close(NG)
    close_places(k, NG)
    added.close(NG)


def experts(k, top, slots):
    nc = k.nc
    RING, LAG = 4, 4
    gathered = [k.counter(f"slot_gathered{r}", 16, lead=0) for r in range(RING)]
    stored = [k.counter(f"slot_stored{r}", 16) for r in range(RING)]
    index_ready, weights_ready, transposed, gT_ready, up_done, act_done, inner_ready, down_done, y_ready = (
        k.counter(f"slot_{n}") for n in ("index_ready", "weights_ready", "transposed", "gT_ready", "up_done",
                                         "act_done", "inner_ready", "down_done", "y_ready"))
    biased = k.counter("slot_biased")
    ps_t, h1, h2, py = k.ps[:, 0:2, 0:P], k.ps[:, 2:4, :], k.ps[:, 4:6, :], k.ps[:, 6:8, 0:D]
    wide = 2 * FF if top == 1 else FF
    w_up = k.w12[:, :, :].rearrange("p e n -> p (e n)") if top == 1 else k.w1[:, :, :].rearrange("p e n -> p (e n)")
    w_dn = (k.w3 if top == 1 else k.w2)[:, :, :, :].rearrange("p e b d -> p (e b d)")
    y_rows = k.y_rows.rearrange("(s p) d -> s p d", p=P)

    def expert_of(eng, s):
        return eng.value_load(k.slot_expert[0:1, ds(s, 1)], min_val=0, max_val=NE - 1)

    k.start()
    with nc.Block() as block:
        @block.gpsimd
        def _(pool):
            def step(at):
                if at(0):
                    s, q, _ = at(0)
                    pool.wait_ge(transposed.sem, transposed.at(s - 3))
                    k.settle(pool)
                    nc.gpsimd.tensor_copy(k.index[:, q:q + 1], k.slot_token[:, ds(s, 1)]).then_inc(index_ready.sem, 1)
                    pool.wait_ge(index_ready.sem, index_ready.at(s + 1))
                    k.settle(pool)
                    nc.gpsimd.indirect_dma_start(k.rows_in[:, q, :], None, k.xn_rows[:, :],
                                                 bass.IndirectOffsetOnAxis(ap=k.index[:, q:q + 1], axis=0)
                                                 ).then_inc(gathered[q].sem, 16)
            rounds(pool, slots, LAG, RING, step)

        @block.tensor
        def _(pe):
            def turn(s, q, n):
                pe.wait_ge(gathered[q].sem, gathered[q].at(n + 1))
                pe.wait_ge(gT_ready.sem, gT_ready.at(s - 1))
                nc.tensor.transpose(ps_t[:, q % 2, :], k.rows_in[:, q, :], k.ident[:, :]).then_inc(transposed.sem, 1)

            def up(s, q, n):
                r = q % 2
                pe.wait_ge(gT_ready.sem, gT_ready.at(s + 1))
                pe.wait_ge(weights_ready.sem, weights_ready.at(s + 1))
                if top == 1:
                    pe.wait_ge(inner_ready.sem, inner_ready.at(s - 1))
                else:
                    pe.wait_ge(biased.sem, biased.at(s - 1))
                for b in range(FB):
                    ins = nc.tensor.matmul(h1[:, r, b * P:(b + 1) * P], k.w_slot[:, r, b * P:(b + 1) * P],
                                           k.gT[:, r, :], start=True, stop=True)
                if top == 1:
                    for b in range(FB):
                        ins = nc.tensor.matmul(h2[:, r, b * P:(b + 1) * P], k.w_slot[:, r, FF + b * P:FF + (b + 1) * P],
                                               k.gT[:, r, :], start=True, stop=True)
                ins.then_inc(up_done.sem, 1)

            def down(s, q, n):
                e = expert_of(pe, s)
                pe.wait_ge(inner_ready.sem, inner_ready.at(s + 1))
                pe.wait_ge(y_ready.sem, y_ready.at(s - 1))
                for b in range(FB):
                    ins = nc.tensor.matmul(py[:, q % 2, :], k.inner_slot[:, q, b * P:(b + 1) * P],
                                           w_dn[:, ds(e * (FB * D) + b * D, D)], start=(b == 0), stop=(b == FB - 1))
                ins.then_inc(down_done.sem, 1)

            def step(at):
                for stage, behind in ((turn, 0), (up, 1), (down, 3)):
                    if at(behind):
                        stage(*at(behind))
            rounds(pe, slots, LAG, RING, step)

        @block.scalar
        def _(act):
            def weights(s, q, n):
                e = expert_of(act, s)
                act.wait_ge(up_done.sem, up_done.at(s - 1))
                nc.scalar.copy(k.w_slot[:, q % 2, 0:wide], w_up[:, ds(e * wide, wide)]).then_inc(weights_ready.sem, 1)

            def rows(s, q, n):
                act.wait_ge(transposed.sem, transposed.at(s + 1))
                act.wait_ge(up_done.sem, up_done.at(s - 1))
                nc.scalar.copy(k.gT[:, q % 2, :], ps_t[:, q % 2, :]).then_inc(gT_ready.sem, 1)

            def gelu(s, q, n):
                act.wait_ge(up_done.sem, up_done.at(s + 1))
                act.wait_ge(inner_ready.sem, inner_ready.at(s - 1))
                nc.scalar.activation(k.gl[:, q % 2, :], h1[:, q % 2, :], ACT.Gelu).then_inc(act_done.sem, 1)

            def gelu_or_tanh(s, q, n):
                e = expert_of(act, s)
                act.wait_ge(biased.sem, biased.at(s + 1))
                act.wait_ge(down_done.sem, down_done.at(s - 3))
                with act.If(e % 2 == 0):
                    nc.scalar.activation(k.inner_slot[:, q, :], k.hb[:, q, :], ACT.Gelu).then_inc(act_done.sem, 1)
                with act.Else():
                    nc.scalar.activation(k.inner_slot[:, q, :], k.hb[:, q, :], ACT.Tanh, scale=0.5).then_inc(act_done.sem, 1)

            def step(at):
                stages = ((rows, 0), (gelu, 1)) if top == 1 else ((weights, 0), (rows, 0), (gelu_or_tanh, 1))
                for stage, behind in stages:
                    if at(behind):
                        stage(*at(behind))
            nc.scalar.activation(k.spare[:, 1:2], k.zero[:, 0:1], ACT.Gelu)
            rounds(act, slots, LAG, RING, step)

        @block.vector
        def _(dve):
            V = nc.vector

            def weights(s, q, n):
                e = expert_of(dve, s)
                dve.wait_ge(up_done.sem, up_done.at(s - 1))
                V.tensor_copy(k.w_slot[:, q % 2, 0:wide], w_up[:, ds(e * wide, wide)]).then_inc(weights_ready.sem, 1)

            def gated(s, q, n):
                dve.wait_ge(act_done.sem, act_done.at(s + 1))
                dve.wait_ge(down_done.sem, down_done.at(s - 3))
                V.tensor_tensor(k.inner_slot[:, q, :], k.gl[:, q % 2, :], h2[:, q % 2, :], ALU.mult
                                ).then_inc(inner_ready.sem, 1)

            def bias(s, q, n):
                e = expert_of(dve, s)
                dve.wait_ge(up_done.sem, up_done.at(s + 1))
                V.tensor_tensor(k.hb[:, q, :].rearrange("p (b t) -> p b t", b=FB),
                                h1[:, q % 2, :].rearrange("p (b t) -> p b t", b=FB),
                                bcast(k.b1[:, ds(e * FB, FB)], 2, P), ALU.add).then_inc(biased.sem, 1)

            def silu(s, q, n):
                e = expert_of(dve, s)
                dve.wait_ge(act_done.sem, act_done.at(s + 1))
                dve.wait_ge(inner_ready.sem, inner_ready.at(s))
                with dve.If(e % 2 == 0):
                    dve.sem_inc(inner_ready.sem, 1)
                with dve.Else():
                    V.scalar_tensor_tensor(k.inner_slot[:, q, :], k.inner_slot[:, q, :], 1.0, k.hb[:, q, :],
                                           ALU.add, ALU.mult).then_inc(inner_ready.sem, 1)

            def output(s, q, n):
                if top == 2:
                    e = expert_of(dve, s)
                dve.wait_ge(down_done.sem, down_done.at(s + 1))
                dve.wait_ge(stored[q].sem, stored[q].at(n))
                if top == 1:
                    V.tensor_copy(k.y[:, q, :], py[:, q % 2, :]).then_inc(y_ready.sem, 1)
                else:
                    V.tensor_tensor(k.y[:, q, :], py[:, q % 2, :], k.b2[:, ds(e * D, D)], ALU.add
                                    ).then_inc(y_ready.sem, 1)

            def step(at):
                stages = ((weights, 0), (gated, 2), (output, 4)) if top == 1 else ((bias, 1), (silu, 2), (output, 4))
                for stage, behind in stages:
                    if at(behind):
                        stage(*at(behind))
            rounds(dve, slots, LAG, RING, step)

        @block.sync
        def _(sp):
            def step(at):
                if at(4):
                    s, q, n = at(4)
                    sp.wait_ge(y_ready.sem, y_ready.at(s + 1))
                    sp.dma_start(y_rows[ds(s, 1)].rearrange("s p d -> (s p) d"), k.y[:, q, :]).then_inc(stored[q].sem, 16)
            rounds(sp, slots, LAG, RING, step)
            for q in range(RING):
                sp.wait_ge(stored[q].sem, stored[q].at((slots - q + RING - 1) // RING))

    for s in (index_ready, weights_ready, transposed, gT_ready, up_done, act_done, inner_ready, down_done, y_ready):
        s.close(slots)
    if top == 2:
        biased.close(slots)
    for q in range(RING):
        gathered[q].close((slots - q + RING - 1) // RING)
        stored[q].close((slots - q + RING - 1) // RING)
    k.pending = (top, slots)


def attend(k, w):
    nc = k.nc
    QB = SEQ // P
    SCALE = float(QK) ** -0.5
    w_turned, w_ready = k.counter("attn_w_turned"), k.counter("attn_w_ready")
    projected, qk_ready = k.counter("attn_projected"), k.counter("attn_qk_ready")
    v_in = k.counter("attn_v_in", 16)
    scored, masked, maxed, expd, turned, pt_ready, mixed, added = (
        k.counter(f"attn_{n}") for n in ("scored", "masked", "max_ready", "exp_done", "probs_turned",
                                        "probsT_ready", "mixed", "added"))
    own = k.counter("attn_vector_step")
    with ExitStack() as stack:
        S = k.scope(stack)
        wqk, wT, bqk = S("wqk", [QK, 2, D]), S("wT", [P, 2, QK]), S("bqk", [QK, 2])
        qT, kT = S("qT", [QK, SEQ]), S("kT", [QK, SEQ])
        v = S("v", [P, QB, D])
        probs, pT = S("probs", [P, 2, SEQ]), S("pT", [P, 2, SEQ])
        keep, fill = S("keep", [P, P]), S("fill", [P, P])
        top, nmax, total, inv = (S(n, [P, 2]) for n in ("top", "nmax", "total", "inv"))
        loads = [(wqk[:, 0, :], w["L1_attn_w_q"]), (wqk[:, 1, :], w["L1_attn_w_k"]),
                 (bqk[:, 0:1], w["L1_attn_b_q"].unsqueeze(1)), (bqk[:, 1:2], w["L1_attn_b_k"].unsqueeze(1))]
        prepare(k, S, None, 0, loads)
        xn_h = k.xn_rows.rearrange("(b t p) d -> p b t d", p=P, b=BATCH)
        ps_s = [k.ps[:, 2 * r:2 * r + 2, :].rearrange("p b n -> p (b n)") for r in range(2)]
        ps_t = k.ps[:, 4:6, :].rearrange("p b n -> p (b n)")
        ps_o, ps_q = k.ps[:, 6:8, 0:D], k.ps[:, 7, :]
        k.start()
        with nc.Block() as block:
            @block.gpsimd
            def _(pool):
                nc.gpsimd.affine_select(out=keep[:, :], in_=k.ones[:, :], compare_op=ALU.is_ge, fill=0.0, base=0,
                                        pattern=[[-1, P]], channel_multiplier=1).then_inc(w_turned.sem, 1)
                pool.wait_ge(w_turned.sem, w_turned.at(1))
                nc.gpsimd.tensor_scalar(fill[:, :], keep[:, :], -1.0, 10000.0 / SCALE, ALU.add, ALU.mult
                                        ).then_inc(w_turned.sem, 1)

            @block.sync
            def _(sp):
                with sp.Fori(0, BATCH) as b:
                    sp.wait_ge(mixed.sem, mixed.at(b * QB))
                    sp.dma_start(v[:, :, :], xn_h[:, ds(b, 1)].rearrange("p b t d -> p (b t) d")).then_inc(v_in.sem, 16)

            @block.tensor
            def _(pe):
                for i in range(2):
                    ins = nc.tensor.transpose(ps_q[:, i * QK:(i + 1) * QK], wqk[:, i, :], k.ident[0:QK, 0:QK])
                ins.then_inc(w_ready.sem, 1)
                pe.wait_ge(w_ready.sem, w_ready.at(2))

                def score(b, q):
                    n, r = b * QB + q, q % 2
                    pe.wait_ge(expd.sem, expd.at(n - 1))
                    for c in range(0, (q + 1) * P, 512):
                        width = min(512, (q + 1) * P - c)
                        ins = nc.tensor.matmul(ps_s[r][:, c:c + width], qT[:, q * P:(q + 1) * P], kT[:, c:c + width],
                                               start=True, stop=True)
                    ins.then_inc(scored.sem, 1)

                def mix(b, q):
                    n, r = b * QB + q, q % 2
                    pe.wait_ge(expd.sem, expd.at(n + 1))
                    pe.wait_ge(pt_ready.sem, pt_ready.at(n))
                    for c in range(q + 1):
                        ins = nc.tensor.transpose(ps_t[:, c * P:(c + 1) * P], probs[:, r, c * P:(c + 1) * P], k.ident[:, :])
                    ins.then_inc(turned.sem, 1)
                    pe.wait_ge(pt_ready.sem, pt_ready.at(n + 1))
                    pe.wait_ge(added.sem, added.at(n - 1))
                    for c in range(q + 1):
                        ins = nc.tensor.matmul(ps_o[:, r, :], pT[:, r, c * P:(c + 1) * P], v[:, c, :],
                                               start=(c == 0), stop=(c == q))
                    ins.then_inc(mixed.sem, 1)

                with pe.Fori(0, BATCH) as b:
                    pe.wait_ge(added.sem, added.at(b * QB))
                    for i in range(4):
                        m = b * 4 + i
                        pe.wait_ge(qk_ready.sem, qk_ready.at(m))
                        k.settle(pe)
                        nc.tensor.matmul(ps_q[0:QK, :], wT[:, i // 2, :], k.xnT[:, ds(b * SEQ + (i % 2) * 512, 512)],
                                         start=True, stop=True).then_inc(projected.sem, 1)
                    pe.wait_ge(qk_ready.sem, qk_ready.at(b * 4 + 4))
                    pe.wait_ge(v_in.sem, v_in.at(b + 1))
                    score(b, 0)
                    for q in range(1, QB):
                        score(b, q)
                        mix(b, q - 1)
                    mix(b, QB - 1)

            @block.scalar
            def _(act):
                act.wait_ge(w_ready.sem, w_ready.at(1))
                nc.scalar.copy(wT[:, :, :].rearrange("p a n -> p (a n)"), ps_q[:, 0:2 * QK]).then_inc(w_ready.sem, 1)
                with act.Fori(0, BATCH) as b:
                    for i in range(4):
                        m = b * 4 + i
                        act.wait_ge(projected.sem, projected.at(m + 1))
                        dst = (qT, kT)[i // 2]
                        nc.scalar.activation(dst[:, (i % 2) * 512:(i % 2) * 512 + 512], ps_q[0:QK, :], ACT.Identity,
                                             bias=bqk[:, i // 2:i // 2 + 1]).then_inc(qk_ready.sem, 1)
                    for q in range(QB):
                        n, r, width = b * QB + q, q % 2, (q + 1) * P
                        act.wait_ge(maxed.sem, maxed.at(n + 1))
                        act.wait_ge(turned.sem, turned.at(n - 1))
                        act.wait_ge(added.sem, added.at(n - 1))
                        nc.scalar.activation(probs[:, r, 0:width], ps_s[r][:, 0:width], ACT.Exp, scale=SCALE,
                                             bias=nmax[:, r:r + 1], accum_out=total[:, r:r + 1]).then_inc(expd.sem, 1)
                        act.wait_ge(turned.sem, turned.at(n + 1))
                        act.wait_ge(mixed.sem, mixed.at(n - 1))
                        nc.scalar.copy(pT[:, r, 0:width], ps_t[:, 0:width]).then_inc(pt_ready.sem, 1)

            @block.vector
            def _(dve):
                V = nc.vector
                dve.wait_ge(w_turned.sem, w_turned.at(2))

                def maximum(b, q):
                    n, r = b * QB + q, q % 2
                    last = ps_s[r][:, q * P:(q + 1) * P]
                    dve.wait_ge(scored.sem, scored.at(n + 1))
                    V.tensor_tensor(last, last, keep[:, :], ALU.mult).then_inc(own.sem, 1)
                    dve.wait_ge(own.sem, own.at(n * 3 + 1))
                    V.tensor_tensor(last, last, fill[:, :], ALU.add).then_inc(own.sem, 1)
                    dve.wait_ge(own.sem, own.at(n * 3 + 2))
                    V.tensor_reduce(top[:, r:r + 1], ps_s[r][:, 0:(q + 1) * P], AX.X, ALU.max).then_inc(own.sem, 1)
                    dve.wait_ge(own.sem, own.at(n * 3 + 3))
                    dve.wait_ge(expd.sem, expd.at(n - 1))
                    V.tensor_scalar(nmax[:, r:r + 1], top[:, r:r + 1], -SCALE, None, ALU.mult).then_inc(maxed.sem, 1)

                def add(b, q):
                    n, r = b * QB + q, q % 2
                    dve.wait_ge(mixed.sem, mixed.at(n + 1))
                    V.reciprocal(inv[:, r:r + 1], total[:, r:r + 1]).then_inc(masked.sem, 1)
                    dve.wait_ge(masked.sem, masked.at(n + 1))
                    xt = k.x[:, ds(n * D, D)]
                    V.scalar_tensor_tensor(xt, ps_o[:, r, :], inv[:, r:r + 1], xt, ALU.mult, ALU.add
                                           ).then_inc(added.sem, 1)

                with dve.Fori(0, BATCH) as b:
                    maximum(b, 0)
                    for q in range(1, QB):
                        maximum(b, q)
                        add(b, q - 1)
                    add(b, QB - 1)
        n = BATCH * QB
        for s in (scored, masked, maxed, expd, turned, pt_ready, mixed, added):
            s.close(n)
        own.close(3 * n)
        w_turned.close(2)
        w_ready.close(2)
        projected.close(4 * BATCH)
        qk_ready.close(4 * BATCH)
        v_in.close(BATCH)


def mamba(k, w):
    nc = k.nc
    with ExitStack() as stack:
        S = k.scope(stack)
        m = Weights()
        m.win, m.wout, m.nw = S("win", [P, ME, ZW + CW + MH]), S("wout", [P, ME, 2, D]), S("nw", [P, ME * 2])
        m.cw, m.cb = S("cw", [P, ME * 4, TAPS]), S("cb", [P, ME * 4])
        m.dtb, m.aneg, m.dsk = (S(n, [P, MEH]) for n in ("dtb", "aneg", "dsk"))
        m.diagD = S("diagD", [P, MEH, P])
        m.tri, m.identb = S("tri", [P, P]), S("identb", [P, P], BF16)
        m.future = S("future", [P, MH, P], BF16)
        m.pickA, m.pickQ = S("pickA", [P, MEH, P], BF16), S("pickQ", [P, ME, MH * P], BF16)
        m.keep = S("keepg", [P, NG])
        m.rout = S("rout", [P, NT * ME])
        m.wst, m.ea, m.cd = (S(n, [P, NT * MEH]) for n in ("wst", "ea", "cd"))
        m.parts = S("parts", [P, NT, P], BF16)
        in_w = w["L0_attn_in_w"]
        loads = [
            (m.win[:, :, :], in_w.rearrange("e d n -> d e n")),
            (m.wout[:, :].rearrange("p e b d -> p (e b) d"), w["L0_attn_out_w"].rearrange("e (b p) d -> p (e b) d", p=P)),
            (m.nw[:, :], w["L0_attn_norm_w"].rearrange("e (b p) -> p (e b)", p=P)),
            (m.cw[:, :, :], w["L0_attn_conv_w"].rearrange("e (b p) k -> p (e b) k", p=P)),
            (m.cb[:, :], w["L0_attn_conv_b"].rearrange("e (b p) -> p (e b)", p=P)),
            (m.dtb[:, :], w["L0_attn_dt_bias"].rearrange("e h -> (e h)").unsqueeze(0).to_broadcast([P, MEH])),
            (m.aneg[:, :], w["L0_attn_A_log"].rearrange("e h -> (e h)").unsqueeze(0).to_broadcast([P, MEH])),
            (m.dsk[:, :], w["L0_attn_D_skip"].rearrange("e h -> (e h)").unsqueeze(0).to_broadcast([P, MEH])),
        ]
        prepare(k, S, k.mw[:, :], NM, loads)
        with ExitStack() as inner:
            mamba_scalars(k, m, k.scope(inner))
        with ExitStack() as inner:
            mamba_groups(k, m, k.scope(inner))


class Weights:
    pass


def mamba_scalars(k, m, S):
    nc = k.nc
    N = NT * MEH
    v, av, u, dt, q, z0 = (S(n, [P, N]) for n in ("v", "av", "u", "dt", "q", "z0"))
    mx, sm = S("mx", [P, NT]), S("sm", [P, NT])
    consts, own, to_act, acted, a_ready, summed = (
        k.counter(f"scalars_{n}") for n in ("constants", "vector_step", "to_scalar", "scalar_step", "a_ready", "summed"))
    lg = k.logits[:, 0:NT * NM].rearrange("p (t n) -> p t n", n=NM)
    by_head = lambda t: t[:, :].rearrange("p (t n) -> p t n", n=MEH)
    ps_acs, ps_tot = k.ps[:, 0, :], k.ps[:, 1, :]

    k.start()
    with nc.Block() as block:
        @block.gpsimd
        def _(pool):
            G = nc.gpsimd
            do = Chain(pool, consts)
            do(G.affine_select(out=m.tri[:, :], in_=k.ones[:, :], compare_op=ALU.is_ge, fill=0.0, base=0,
                               pattern=[[1, P]], channel_multiplier=-1))
            do(G.tensor_copy(m.identb[:, :], k.ident[:, :]))
            do(G.memset(m.future[:, :, :], 0.0))
            do(G.affine_select(out=m.future[:, :, :], in_=m.future[:, :, :], compare_op=ALU.is_ge, fill=-1e30,
                               base=0, pattern=[[0, MH], [1, P]], channel_multiplier=-1))
            do(G.memset(m.pickA[:, :, :], 0.0))
            do(G.memset(m.pickQ[:, :, :], 0.0))
            for part in range(3):
                do(G.affine_select(out=m.pickA[:, :, :], in_=m.pickA[:, :, :], compare_op=ALU.not_equal, fill=1.0,
                                   base=-MEH * part, pattern=[[-1, MEH], [0, P]], channel_multiplier=1))
                pq = m.pickQ[:, :, :].rearrange("p e (h l) -> p e h l", h=MH)
                do(G.affine_select(out=pq, in_=pq, compare_op=ALU.not_equal, fill=1.0, base=-MEH * (3 + part),
                                   pattern=[[-MH, ME], [-1, MH], [0, P]], channel_multiplier=1))
            do(G.memset(m.keep[:, :], 1.0))
            do(G.memset(m.keep[:, :].rearrange("p (b g) -> p b g", b=BATCH)[:, :, 0:1], 0.0))

        @block.vector
        def _(dve):
            V = nc.vector
            do = Chain(dve, own)

            def on_scalar(step):
                dve.sem_inc(to_act.sem, 1)
                dve.wait_ge(acted.sem, acted.at(step))

            rout = m.rout[:, :].rearrange("p (t e) -> p t e", e=ME)
            do(V.memset(m.parts[:, :, :], 0.0))
            do(V.tensor_reduce(mx[:, :], lg[:, :, 0:ME], AX.X, ALU.max))
            do(V.tensor_tensor(rout, lg[:, :, 0:ME], bcast(mx[:, :], 2, ME), ALU.subtract))
            do(V.tensor_tensor(by_head(v), lg[:, :, ME:NM], bcast(m.dtb[:, :], 1, NT), ALU.add))
            do(V.scalar_tensor_tensor(av[:, :], v[:, :], -1.0, v[:, :], ALU.mult, ALU.max))
            on_scalar(3)
            do(V.tensor_reduce(sm[:, :], rout, AX.X, ALU.add))
            do(V.reciprocal(sm[:, :], sm[:, :]))
            do(V.tensor_tensor(rout, rout, bcast(sm[:, :], 2, ME), ALU.mult))
            do(V.tensor_scalar(av[:, :], u[:, :], 1.0, None, ALU.add))
            on_scalar(4)
            do(V.tensor_scalar(av[:, :], av[:, :], -1.0, None, ALU.add))
            do(V.tensor_scalar(z0[:, :], av[:, :], 0.0, None, ALU.is_equal))
            do(V.tensor_add(av[:, :], av[:, :], z0[:, :]))
            do(V.reciprocal(av[:, :], av[:, :]))
            do(V.tensor_mul(dt[:, :], dt[:, :], av[:, :]))
            do(V.tensor_add(dt[:, :], dt[:, :], z0[:, :]))
            do(V.tensor_mul(dt[:, :], dt[:, :], u[:, :]))
            do(V.scalar_tensor_tensor(dt[:, :], v[:, :], 0.0, dt[:, :], ALU.max, ALU.add))
            do(V.tensor_scalar(u[:, :], dt[:, :], 1e-19, None, ALU.max))
            V.scalar_tensor_tensor(by_head(v), by_head(dt), -1.0, bcast(m.aneg[:, :], 1, NT), ALU.mult, ALU.mult
                                   ).then_inc(a_ready.sem, 1)
            on_scalar(5)
            dve.wait_ge(summed.sem, summed.at(1))
            acs = dt
            do(V.tensor_copy(acs[:, :], ps_acs))
            do(V.tensor_sub(q[:, :], q[:, :], acs[:, :]))
            do(V.tensor_tensor(av[:, :], q[:, :], ps_tot, ALU.add))
            on_scalar(8)
            for t in (m.ea, m.cd):
                first = t[:, :].rearrange("p (b c n) -> p b c n", b=BATCH, n=MEH)[:, :, 0, :]
                do(V.memset(first, 0.0))
            for src, first in ((acs, 0), (q, 3)):
                for part in range(3):
                    out = m.parts[:, :, (first + part) * MEH:(first + part + 1) * MEH]
                    do(V.tensor_copy(out, by_head(src)))
                    if part < 2:
                        do(V.tensor_tensor(by_head(src), by_head(src), out, ALU.subtract))
            for e in range(ME):
                for b in range(2):
                    do(V.tensor_scalar(m.wout[:, e, b, :], m.wout[:, e, b, :], m.nw[:, e * 2 + b:e * 2 + b + 1],
                                       None, ALU.mult))
            for n in range(MEH):
                do(V.tensor_scalar(m.diagD[:, n, :], k.ident[:, :], m.dsk[:, n:n + 1], None, ALU.mult))
            k.scalar_steps = do.n
            dve.wait_ge(consts.sem, consts.at(14))

        @block.scalar
        def _(act):
            do = Chain(act, acted)
            act.wait_ge(to_act.sem, to_act.at(1))
            do(nc.scalar.activation(m.rout[:, :], m.rout[:, :], ACT.Exp))
            do(nc.scalar.activation(u[:, :], av[:, :], ACT.Exp, scale=-1.0))
            do(nc.scalar.activation(m.aneg[:, :], m.aneg[:, :], ACT.Exp))
            act.wait_ge(to_act.sem, to_act.at(2))
            do(nc.scalar.activation(dt[:, :], av[:, :], ACT.Ln))
            act.wait_ge(to_act.sem, to_act.at(3))
            do(nc.scalar.activation(q[:, :], u[:, :], ACT.Ln))
            act.wait_ge(to_act.sem, to_act.at(4))
            do(nc.scalar.activation(m.wst[:, :], av[:, :], ACT.Exp))
            do(nc.scalar.activation(m.ea[:, :], dt[:, :], ACT.Exp))
            do(nc.scalar.activation(m.cd[:, :], ps_tot, ACT.Exp))

        @block.tensor
        def _(pe):
            pe.wait_ge(consts.sem, consts.at(1))
            pe.wait_ge(a_ready.sem, a_ready.at(1))
            nc.tensor.matmul(ps_acs, m.tri[:, :], v[:, :], start=True, stop=True)
            nc.tensor.matmul(ps_tot, k.ones[:, :], v[:, :], start=True, stop=True).then_inc(summed.sem, 1)
    own.close(k.scalar_steps)
    consts.close(14)
    to_act.close(4)
    acted.close(8)
    a_ready.close(1)
    summed.close(1)


def mamba_groups(k, m, S):
    nc = k.nc
    NU = GRP * ME
    NB = CW // P
    GT = GRP * P
    xc = S("xc", [P, GT])
    xb, cv, tails = S("xb", [P, 2, TAPS - 1 + GT]), S("cv", [P, 2, GT]), S("tails", [P, ME * NB, TAPS - 1])
    xbc, sz = S("xbc", [P, ME, NB, GT]), S("sz", [P, ME, GRP, ZW])
    rows = S("rows", [P, GRP, P], BF16)
    state, carried = S("state", [P, ME, ZW]), S("carried", [P, 2, ZW])
    XB, L, M, Xw = S("XB", [P, 2, ZW + P]), S("L", [P, 2, MH * P]), S("M", [P, 2, MH * P]), S("Xw", [P, 2, ZW])
    t1, t2, y2, yT, sq = S("t1", [P, ZW]), S("t2", [P, ZW]), S("y2", [P, 2, ZW]), S("yT", [P, 2, ZW]), S("sq", [P, ZW])
    ss, rs, gain = S("ss", [P, 2]), S("rs", [P, 2]), S("gain", [P, 2])

    names = ("xc", "rows_turned", "rows", "proj", "copied", "conv", "conv_silu", "z", "z_silu", "tail")
    a = {n: k.counter(f"group_{n}") for n in names}
    own = k.counter("group_vector_step")
    names = ("x_turned", "cb", "exponent", "XB", "L", "M", "Xw", "y", "s", "carried", "state", "y2", "squared",
             "yT_turned", "yT", "out", "gain", "added")
    b = {n: k.counter(f"unit_{n}") for n in names}
    yown, gown, init = k.counter("unit_y_step"), k.counter("unit_gain_step"), k.counter("group_init")

    bankX, bankL, bankCB, bankY, bankS, bankYT, bankO = (k.ps[:, i, :] for i in range(7))

    def inc(ins, sig):
        ins.then_inc(sig.sem, 1)

    def wait(eng, sig, n):
        eng.wait_ge(sig.sem, sig.at(n))

    k.start()
    with nc.Block() as block:
        @block.tensor
        def _(pe):
            def project(g):
                wait(pe, b["added"], g * NU)
                wait(pe, a["xc"], g + 1)
                for j in range(GRP):
                    ins = nc.tensor.matmul(k.ps[:, 7, j * P:(j + 1) * P], m.parts[:, ds(g * GRP + j, 1), :].rearrange("p a n -> p (a n)"),
                                           m.identb[:, :], start=True, stop=True)
                inc(ins, a["rows_turned"])
                for e in range(ME):
                    for blk in range(NB):
                        i = (g * ME + e) * NB + blk
                        wait(pe, a["copied"], i - 3)
                        inc(nc.tensor.matmul(k.ps[:, blk, :], m.win[:, e, ZW + blk * P:ZW + (blk + 1) * P], xc[:, :],
                                             start=True, stop=True), a["proj"])
                    if e == 0:
                        wait(pe, a["rows"], g + 1)
                    wait(pe, a["z_silu"], g * ME + e)
                    for j in range(GRP):
                        ins = nc.tensor.matmul(k.ps[:, 4 + j, 0:ZW], xc[:, j * P:(j + 1) * P], m.win[:, e, 0:ZW],
                                               start=True, stop=True)
                    inc(ins, a["z"])

            def open_unit(g, u):
                j, e = u // ME, u % ME
                n = g * NU + u
                cols = slice(j * P, (j + 1) * P)
                if u < ME:
                    wait(pe, a["conv_silu"], (g * ME + ME) * NB)
                    wait(pe, a["z_silu"], (g + 1) * ME)
                wait(pe, b["XB"], n)
                for blk in range(3):
                    ins = nc.tensor.transpose(bankX[:, blk * P:(blk + 1) * P], xbc[:, e, blk, cols], k.ident[:, :])
                inc(ins, b["x_turned"])
                wait(pe, b["L"], n)
                nc.tensor.matmul(bankL, m.identb[:, :], m.future[:, :, :].rearrange("p h l -> p (h l)"),
                                 start=True, stop=False, skip_group_check=True)
                nc.tensor.matmul(bankL, rows[:, j, :], m.pickQ[:, e, :], start=False, stop=False, skip_group_check=True)
                for h in range(MH):
                    ins = nc.tensor.matmul(bankL[:, h * P:(h + 1) * P], m.pickA[:, e * MH + h, :], rows[:, j, :],
                                           start=False, stop=(h == MH - 1), skip_group_check=True)
                inc(ins, b["exponent"])
                wait(pe, b["M"], n)
                inc(nc.tensor.matmul(bankCB[:, 0:P], xbc[:, e, 2, cols], xbc[:, e, 3, cols], start=True, stop=True), b["cb"])

            def mix_unit(g, u):
                j, e = u // ME, u % ME
                n = g * NU + u
                r = u % 2
                wait(pe, b["M"], n + 1)
                wait(pe, b["XB"], n + 1)
                wait(pe, b["y2"], n)
                for h in range(MH):
                    cols = slice(h * HD, (h + 1) * HD)
                    nc.tensor.matmul(bankY[:, cols], M[:, r, h * P:(h + 1) * P], XB[:, r, cols], start=True, stop=False)
                    nc.tensor.matmul(bankY[:, cols], m.diagD[:, e * MH + h, :], XB[:, r, cols], start=False, stop=True)
                wait(pe, b["state"], n - 3)
                inc(nc.tensor.matmul(bankY[:, ZW:2 * ZW], xbc[:, e, 3, j * P:(j + 1) * P], state[:, e, :],
                                     start=True, stop=True), b["y"])
                wait(pe, b["Xw"], n + 1)
                wait(pe, b["state"], n)
                inc(nc.tensor.matmul(bankS[:, 0:ZW], XB[:, r, ZW:ZW + P], Xw[:, r, :], start=True, stop=True), b["s"])

            def turn_unit(g, u):
                n, r = g * NU + u, u % 2
                wait(pe, b["y2"], n + 1)
                wait(pe, b["yT"], n)
                for blk in range(2):
                    ins = nc.tensor.transpose(bankYT[:, blk * P:(blk + 1) * P], y2[:, r, blk * P:(blk + 1) * P], k.ident[:, :])
                inc(ins, b["yT_turned"])

            def out_unit(g, u):
                n, r, e = g * NU + u, u % 2, u % ME
                wait(pe, b["yT"], n + 1)
                wait(pe, b["added"], n)
                for blk in range(2):
                    ins = nc.tensor.matmul(bankO[:, 0:D], yT[:, r, blk * P:(blk + 1) * P], m.wout[:, e, blk, :],
                                           start=(blk == 0), stop=(blk == 1))
                inc(ins, b["out"])

            wait(pe, init, 1)
            with pe.Fori(0, NG) as g:
                project(g)
                open_unit(g, 0)
                for u in range(NU + 1):
                    if u + 1 < NU:
                        open_unit(g, u + 1)
                    if u >= 1:
                        turn_unit(g, u - 1)
                    if u < NU:
                        mix_unit(g, u)
                    if u >= 1:
                        out_unit(g, u - 1)

        @block.scalar
        def _(act):
            def copy(i, blk):
                wait(act, a["proj"], i + 1)
                wait(act, a["conv"], i - 1)
                inc(nc.scalar.copy(xb[:, blk % 2, TAPS - 1:TAPS - 1 + GT], k.ps[:, blk, :]), a["copied"])

            def silu(i, e, blk):
                wait(act, a["conv"], i + 1)
                inc(nc.scalar.activation(xbc[:, e, blk, :], cv[:, blk % 2, :], ACT.Silu,
                                         bias=m.cb[:, e * NB + blk:e * NB + blk + 1]), a["conv_silu"])

            def open_unit(g, u):
                n, r = g * NU + u, u % 2
                wait(act, b["x_turned"], n + 1)
                wait(act, b["s"], n - 1)
                inc(nc.scalar.copy(XB[:, r, :], bankX[:, 0:ZW + P]), b["XB"])
                wait(act, b["exponent"], n + 1)
                wait(act, b["M"], n - 1)
                inc(nc.scalar.activation(L[:, r, :], bankL, ACT.Exp), b["L"])

            def close_unit(g, u):
                n, r = g * NU + u, u % 2
                wait(act, b["yT_turned"], n + 1)
                wait(act, b["out"], n - 1)
                inc(nc.scalar.copy(yT[:, r, :], bankYT[:, 0:ZW]), b["yT"])
                wait(act, b["gain"], n - 1)
                wait(act, b["squared"], n)
                inc(nc.scalar.activation(sq[:, :], y2[:, r, :], ACT.Square, scale=float(ZW) ** -0.5,
                                         accum_out=ss[:, r:r + 1]), b["squared"])

            with act.Fori(0, NG) as g:
                wait(act, a["z"], g * ME)
                wait(act, b["out"], g * NU)
                inc(nc.scalar.copy(xc[:, :], k.xnT[:, ds(g * GT, GT)]), a["xc"])
                wait(act, a["rows_turned"], g + 1)
                inc(nc.scalar.copy(rows[:, :, :].rearrange("p j n -> p (j n)"), k.ps[:, 7, :]), a["rows"])
                for e in range(ME):
                    i = (g * ME + e) * NB
                    copy(i, 0)
                    for blk in range(1, NB):
                        copy(i + blk, blk)
                        silu(i + blk - 1, e, blk - 1)
                    wait(act, a["z"], g * ME + e + 1)
                    inc(nc.scalar.activation(sz[:, e, :, :], k.ps[:, 4:8, 0:ZW], ACT.Silu), a["z_silu"])
                    silu(i + NB - 1, e, NB - 1)
                open_unit(g, 0)
                for u in range(NU + 1):
                    if u + 1 < NU:
                        open_unit(g, u + 1)
                    if u >= 1:
                        close_unit(g, u - 1)

        @block.vector
        def _(dve):
            V = nc.vector

            def convolve(g, e, blk):
                i = (g * ME + e) * NB + blk
                r, c = blk % 2, e * NB + blk
                k5 = i * 5
                wait(dve, own, k5)
                inc(V.tensor_scalar(xb[:, r, 0:TAPS - 1], tails[:, c, :], m.keep[:, ds(g, 1)], None, ALU.mult), own)
                wait(dve, a["copied"], i + 1)
                wait(dve, own, k5 + 1)
                wait(dve, a["conv_silu"], i - 1)
                inc(V.tensor_scalar(cv[:, r, :], xb[:, r, 0:GT], m.cw[:, c, 0:1], None, ALU.mult), own)
                for tap in range(1, TAPS):
                    wait(dve, own, k5 + 1 + tap)
                    ins = V.scalar_tensor_tensor(cv[:, r, :], xb[:, r, tap:tap + GT], m.cw[:, c, tap:tap + 1],
                                                 cv[:, r, :], ALU.mult, ALU.add)
                    if tap < TAPS - 1:
                        inc(ins, own)
                inc(V.tensor_copy(tails[:, c, :], xb[:, r, GT:GT + TAPS - 1]), own)
                wait(dve, own, k5 + 5)
                inc(V.tensor_copy(k.spare[:, 0:1], k.zero[:, 0:1]), a["conv"])

            def matrices(g, u):
                n, r = g * NU + u, u % 2
                wait(dve, b["L"], n + 1)
                wait(dve, b["cb"], n + 1)
                wait(dve, b["y"], n - 1)
                inc(V.tensor_tensor(M[:, r, :].rearrange("p (h l) -> p h l", h=MH), L[:, r, :].rearrange(
                    "p (h l) -> p h l", h=MH), bcast(bankCB[:, 0:P], 1, MH), ALU.mult), b["M"])

            def gated(g, u):
                j, e = u // ME, u % ME
                n, r = g * NU + u, u % 2
                heads = lambda t: t.rearrange("p (h d) -> p h d", h=MH)
                wait(dve, b["y"], n + 1)
                wait(dve, b["y2"], n)
                inc(V.tensor_tensor(heads(t1[:, :]), heads(bankY[:, ZW:2 * ZW]),
                                    bcast(m.ea[:, ds((g * GRP + j) * MEH + e * MH, MH)], 2, HD), ALU.mult), yown)
                wait(dve, yown, n * 2 + 1)
                inc(V.tensor_tensor(t2[:, :], t1[:, :], bankY[:, 0:ZW], ALU.add), yown)
                wait(dve, yown, n * 2 + 2)
                wait(dve, b["squared"], n - 1)
                wait(dve, b["yT_turned"], n - 1)
                inc(V.tensor_tensor(y2[:, r, :], t2[:, :], sz[:, e, j, :], ALU.mult), b["y2"])
                wait(dve, b["s"], n + 1)
                wait(dve, b["carried"], n + 1)
                inc(V.tensor_tensor(state[:, e, :], bankS[:, 0:ZW], carried[:, r, :], ALU.add), b["state"])

            def add(g, u):
                j = u // ME
                n, r = g * NU + u, u % 2
                wait(dve, b["out"], n + 1)
                wait(dve, b["gain"], n + 1)
                wait(dve, b["added"], n)
                xt = k.x[:, ds((g * GRP + j) * D, D)]
                inc(V.scalar_tensor_tensor(xt, bankO[:, 0:D], gain[:, r:r + 1], xt, ALU.mult, ALU.add), b["added"])

            V.memset(tails[:, :, :], 0.0)
            inc(V.memset(state[:, :, :], 0.0), init)
            wait(dve, init, 1)
            with dve.Fori(0, NG) as g:
                for e in range(ME):
                    for blk in range(NB):
                        convolve(g, e, blk)
                matrices(g, 0)
                for u in range(NU + 1):
                    if u + 1 < NU:
                        matrices(g, u + 1)
                    if u < NU:
                        gated(g, u)
                    if u >= 1:
                        add(g, u - 1)

        @block.gpsimd
        def _(pool):
            G = nc.gpsimd
            heads = lambda t: t.rearrange("p (h d) -> p h d", h=MH)

            def weigh(g, u):
                j, e = u // ME, u % ME
                n, r = g * NU + u, u % 2
                wait(pool, b["XB"], n + 1)
                wait(pool, b["s"], n - 1)
                k.settle(pool)
                inc(G.tensor_tensor(heads(Xw[:, r, :]), heads(XB[:, r, 0:ZW]),
                                    bcast(m.wst[:, ds((g * GRP + j) * MEH + e * MH, MH)], 2, HD), ALU.mult), b["Xw"])

            def carry(g, u):
                j, e = u // ME, u % ME
                n, r = g * NU + u, u % 2
                wait(pool, b["state"], n - 1)
                k.settle(pool)
                inc(G.tensor_tensor(heads(carried[:, r, :]), heads(state[:, e, :]),
                                    bcast(m.cd[:, ds((g * GRP + j) * MEH + e * MH, MH)], 2, HD), ALU.mult), b["carried"])

            def normalise(g, u):
                j, e = u // ME, u % ME
                n, r = g * NU + u, u % 2
                wait(pool, b["squared"], n + 1)
                wait(pool, b["added"], n - 1)
                inc(G.tensor_tensor(rs[:, r:r + 1], ss[:, r:r + 1], k.eps[:, 0:1], ALU.add), gown)
                wait(pool, gown, n * 2 + 1)
                inc(G.tensor_tensor(rs[:, r:r + 1], rs[:, r:r + 1], k.minus_half[:, 0:1], ALU.pow), gown)
                wait(pool, gown, n * 2 + 2)
                k.settle(pool)
                inc(G.tensor_tensor(gain[:, r:r + 1], rs[:, r:r + 1], m.rout[:, ds((g * GRP + j) * ME + e, 1)],
                                    ALU.mult), b["gain"])

            wait(pool, init, 1)
            with pool.Fori(0, NG) as g:
                weigh(g, 0)
                for u in range(NU + 1):
                    if u < NU:
                        carry(g, u)
                    if u + 1 < NU:
                        weigh(g, u + 1)
                    if u >= 1:
                        normalise(g, u - 1)

    for n in ("xc", "rows_turned", "rows"):
        a[n].close(NG)
    for n in ("proj", "copied", "conv", "conv_silu"):
        a[n].close(NG * ME * NB)
    for n in ("z", "z_silu"):
        a[n].close(NG * ME)
    own.close(NG * ME * NB * 5)
    for s in b.values():
        s.close(NG * NU)
    yown.close(NG * NU * 2)
    gown.close(NG * NU * 2)
    init.close(1)

def setup(k, w):
    nc = k.nc
    k.counter("settled")
    loads, made, own = k.counter("setup_loads", 16), k.counter("setup_made"), k.counter("setup_step")
    S = k.sb
    k.x, k.xnT = S("x", [P, NT * D]), S("xnT", [P, TOK])
    k.xn4, k.xt4 = S("xn4", [P, 2, GRP, D]), S("xt4", [P, 2, GRP * P])
    k.stat, k.mv, k.rstd = S("stat", [P, 2, GRP, 6]), S("mv", [P, 2, GRP, 2]), S("rstd", [P, 2, GRP])
    k.logits = S("logits", [P, NT * NM])
    k.ident, k.ones, k.zero = S("ident", [P, P]), S("ones", [P, P]), S("zero", [P, 1])
    k.ones_bf, k.zeros_bf, k.before = S("ones_bf", [P, P], BF16), S("zeros_bf", [P, 2 * SLOTS2], BF16), S("before", [P, P], BF16)
    k.iota, k.lane, k.tile_of = S("iota", [P, P]), S("lane", [P, 1]), S("tile_of", [P, 2 * NT])
    k.falling, k.carry, k.minus_half = S("falling", [P, NE]), S("carry", [P, NE * NT]), S("minus_half", [P, GRP])
    k.mw = S("mw", [P, NM])
    k.spare, k.eps = S("spare", [P, 4]), S("eps", [P, GRP])
    k.rt = [S(f"rt{i}", [P, NE * NT]) for i in range(5)]
    k.best, k.small, k.gate = S("best", [P, 2, NT]), S("small", [P, 2 * NT]), S("gate", [P, 2, NT])
    k.marks = S("marks", [P, NE * NT], BF16)
    k.n_int, k.e8 = S("n_int", [P, NE], I32), S("e8", [P, 3, NE])
    k.posf, k.pos, k.hi_int = S("posf", [P, 2 * NT]), S("pos", [P, 2 * NT], U32), S("hi_int", [P, 2 * NT], I32)
    k.hi, k.lo, k.erow = S("hi", [P, 2 * NT]), S("lo", [P, 2 * NT]), S("erow", [P, SLOTS2])
    k.slot_expert, k.slot_token = S("slot_expert", [P, SLOTS2], I32), S("slot_token", [P, SLOTS2], U32)
    k.oh_lane, k.oh_slot = S("oh_lane", [P, 2, GRP, P], BF16), S("oh_slot", [P, 2, GRP, 2 * SLOTS2], BF16)
    k.iota_bf = S("iota_bf", [P, P], BF16)
    k.wg0, k.wg1, k.bg = S("wg0", [P, NE]), S("wg1", [P, NE]), S("bg", [P, NE])
    k.index = S("index", [P, 4 * GRP], U32)
    k.ps = k.ctx.enter_context(nc.psum_tensor("ps", [P, 8, 512], F32))
    k.xn_rows = nc.dram_tensor("xn_rows", [TOK, D], F32, kind="Internal").ap()
    k.y_rows = nc.dram_tensor("y_rows", [SLOTS2 * P, D], F32, kind="Internal").ap()

    copies = [
        (k.x[:, :].rearrange("p (t d) -> p t d", t=NT), w["L0_attn_x"].rearrange("b (t p) d -> p (b t) d", p=P)),
        (k.wg0[:, :], w["L0_ffn_Wg"]),
        (k.wg1[:, :], w["L1_ffn_Wg"]),
        (k.bg[:, :], w["L1_ffn_bg"].unsqueeze(0).to_broadcast([P, NE])),
        (k.mw[:, 0:ME], w["L0_attn_router_w"]),
        (k.mw[:, ME:NM].rearrange("p (e h) -> p e h", e=ME), w["L0_attn_in_w"].rearrange("e d n -> d e n")[:, :, ZW + CW:]),
    ]

    k.start()
    with nc.Block() as block:
        @block.sync
        def _(sp):
            for dst, src in copies:
                sp.dma_start(dst, src, allow_slow_non_contiguous=True).then_inc(loads.sem, 16)
            sp.wait_ge(loads.sem, loads.at(len(copies)))

        @block.gpsimd
        def _(pool):
            G = nc.gpsimd
            do = Chain(pool, made)
            do(G.memset(k.ones[:, :], 1.0))
            do(G.affine_select(out=k.ident[:, :], in_=k.ones[:, :], compare_op=ALU.is_equal, fill=0.0, base=0,
                               pattern=[[1, P]], channel_multiplier=-1))
            do(G.affine_select(out=k.before[:, :], in_=k.ones[:, :], compare_op=ALU.is_gt, fill=0.0, base=0,
                               pattern=[[1, P]], channel_multiplier=-1))
            do(G.memset(k.zero[:, :], 0.0))
            do(G.memset(k.minus_half[:, :], -0.5))
            do(G.memset(k.eps[:, :], EPS))
            do(G.iota(k.iota[:, :], pattern=[[1, P]], base=0, channel_multiplier=0, allow_small_or_imprecise_dtypes=True))
            do(G.tensor_copy(k.iota_bf[:, :], k.iota[:, :]))
            do(G.iota(k.lane[:, :], pattern=[[1, 1]], base=0, channel_multiplier=1, allow_small_or_imprecise_dtypes=True))
            do(G.iota(k.tile_of[:, :], pattern=[[0, 2], [1, NT]], base=0, channel_multiplier=0, allow_small_or_imprecise_dtypes=True))
            do(G.iota(k.falling[:, :], pattern=[[-1, NE]], base=NE, channel_multiplier=0, allow_small_or_imprecise_dtypes=True))

        @block.vector
        def _(dve):
            V = nc.vector
            do = Chain(dve, own)
            do(V.memset(k.ones_bf[:, :], 1.0))
            do(V.memset(k.zeros_bf[:, :], 0.0))
            do(V.memset(k.carry[:, :], 1.0))
            do(V.memset(k.carry[:, :].rearrange("p (e t) -> p e t", e=NE)[:, :, 0:1], 0.0))


def store(k, S, out):
    nc = k.nc
    top, slots = k.pending
    NR = GRP * top
    index_ready, added, k.first_added = (k.counter(f"back_{n}") for n in ("index_ready", "added", "first_added"))
    fetched = [k.counter(f"back_fetched{n}", 16, lead=0) for n in range(2 * NR)]
    back = S("back", [P, 2 * NR, D]) if top else None
    out_stored = k.counter("output_stored", 16)
    by_group = out.rearrange("b t d -> (b t) d").rearrange("(g j p) d -> p g j d", p=P, j=GRP)
    nothing = lambda g, r, i: None
    k.start()
    with nc.Block() as block:
        @block.gpsimd
        def _(pool):
            in_turn(pool, NG, lambda g, r, i: fetch_back(k, pool, g, r, top, slots, back, index_ready, fetched, added),
                    nothing)

        @block.vector
        def _(dve):
            in_turn(dve, NG, lambda g, r, i: take_back(k, dve, g, r, i, top, back, fetched, added), nothing)

        @block.sync
        def _(sp):
            for g in range(NG):
                if top:
                    sp.wait_ge(added.sem, added.at(g + 1))
                sp.dma_start(by_group[:, g], k.x[:, g * GRP * D:(g + 1) * GRP * D].rearrange("p (j d) -> p j d", j=GRP)
                             ).then_inc(out_stored.sem, 16)
            sp.wait_ge(out_stored.sem, out_stored.at(NG))


SLOTS1 = (TOK + NE * (P - 1)) // P
SLOTS2 = (2 * TOK + NE * (P - 1)) // P


def macaron(nc, w, out):
    with ExitStack() as ctx:
        k = Bench(nc, ctx)
        setup(k, w)
        for stage in STAGES:
            {"ffn0": ffn0, "ffn1": ffn1, "attn": attend, "mamba": mamba}[stage](k, w)
        with ExitStack() as stack:
            store(k, k.scope(stack), out)


def ffn0(k, w):
    with ExitStack() as stack:
        S = k.scope(stack)
        k.w12, k.w3 = S("w12", [P, NE + 1, 2 * FF]), S("w3", [P, NE + 1, FB, D])
        k.gl, k.inner = S("gl", [P, 2, GRP * P]), S("inner", [P, 2, FB, GRP * P])
        k.rows_in, k.gT, k.w_slot = S("rows_in", [P, 4, D]), S("gT", [P, 2, P]), S("w_slot", [P, 2, 2 * FF])
        k.inner_slot, k.y = S("inner_slot", [P, 4, FF]), S("y", [P, 4, D])
        loads = [
            (k.w12[:, NE, 0:FF], w["L0_ffn_w1s"]),
            (k.w12[:, NE, FF:2 * FF], w["L0_ffn_w2s"]),
            (k.w3[:, NE], w["L0_ffn_w3s"].rearrange("(b p) d -> p b d", p=P)),
            (k.w12[:, 0:NE, 0:FF], w["L0_ffn_W1"].rearrange("e d f -> d e f")),
            (k.w12[:, 0:NE, FF:2 * FF], w["L0_ffn_W2"].rearrange("e d f -> d e f")),
            (k.w3[:, 0:NE].rearrange("p e b d -> p (e b) d"), w["L0_ffn_W3"].rearrange("e (b p) d -> p (e b) d", p=P)),
        ]
        prepare(k, S, k.wg0[:, :], NE, loads)
        route(k, 1, SLOTS1, False)
        shared(k, SLOTS1)
        experts(k, 1, SLOTS1)


def ffn1(k, w):
    nc = k.nc
    done = k.counter("router_biased")
    with ExitStack() as stack:
        S = k.scope(stack)
        k.w1, k.w2 = S("w1", [P, NE, FF]), S("w2", [P, NE, FB, D])
        k.b1, k.b2 = S("b1", [P, NE * FB]), S("b2", [P, NE * D])
        k.rows_in, k.gT, k.w_slot = S("rows_in", [P, 4, D]), S("gT", [P, 2, P]), S("w_slot", [P, 2, FF])
        k.inner_slot, k.hb, k.y = S("inner_slot", [P, 4, FF]), S("hb", [P, 4, FF]), S("y", [P, 4, D])
        loads = [
            (k.w1[:, :, :], w["L1_ffn_W1"].rearrange("e d f -> d e f")),
            (k.b2[:, :], w["L1_ffn_b2"].rearrange("e d -> (e d)").unsqueeze(0).to_broadcast([P, NE * D])),
            (k.w2[:, :].rearrange("p e b d -> p (e b) d"), w["L1_ffn_W2"].rearrange("e (b p) d -> p (e b) d", p=P)),
            (k.b1[:, :], w["L1_ffn_b1"].rearrange("e (b p) -> p (e b)", p=P)),
        ]
        prepare(k, S, k.wg1[:, :], NE, loads)
        k.start()
        with nc.Block() as block:
            @block.vector
            def _(dve):
                l3 = k.logits[:, 0:NT * NE].rearrange("p (t e) -> p t e", e=NE)
                nc.vector.tensor_tensor(l3, l3, bcast(k.bg[:, :], 1, NT), ALU.add).then_inc(done.sem, 1)
                for e in range(1, NE, 2):
                    nc.vector.tensor_scalar(k.w2[:, e], k.w2[:, e], 0.5, None, ALU.mult).then_inc(done.sem, 1)
                dve.wait_ge(done.sem, done.at(1 + NE // 2))
        done.close(1 + NE // 2)
        route(k, 2, SLOTS2, True)
        experts(k, 2, SLOTS2)


_INS = ['L0_attn_x', 'L0_attn_router_w', 'L0_attn_in_w', 'L0_attn_conv_w', 'L0_attn_conv_b', 'L0_attn_dt_bias',
        'L0_attn_A_log', 'L0_attn_D_skip', 'L0_attn_norm_w', 'L0_attn_out_w', 'L0_ffn_w1s', 'L0_ffn_w2s', 'L0_ffn_w3s',
        'L0_ffn_W1', 'L0_ffn_W2', 'L0_ffn_W3', 'L0_ffn_Wg', 'L1_attn_w_q', 'L1_attn_b_q', 'L1_attn_w_k', 'L1_attn_b_k',
        'L1_ffn_W1', 'L1_ffn_b1', 'L1_ffn_W2', 'L1_ffn_b2', 'L1_ffn_Wg', 'L1_ffn_bg']


def kernel(**inputs):
    import numpy as _np
    import concourse.bacc as _bacc
    from concourse import mybir as _mybir
    from concourse.bass_utils import run_bass_kernel_spmd as _run

    nc = _bacc.Bacc("TRN2", target_bir_lowering=False, num_devices=1)
    arrays, w = {}, {}
    for name in _INS:
        a = _np.ascontiguousarray(inputs[name])
        arrays[f"in_{name}"] = a
        w[name] = nc.dram_tensor(f"in_{name}", a.shape, _mybir.dt.from_np(a.dtype), kind="ExternalInput").ap()
    out = nc.dram_tensor("out_x", (BATCH, SEQ, D), _mybir.dt.float32, kind="ExternalOutput").ap()
    macaron(nc, w, out)
    r = _run(nc, [arrays], core_ids=[0])
    return r.results[0]["out_x"]
```

```python
import numpy as np
import concourse.bass as bass
from concourse import mybir
from contextlib import ExitStack

F32 = mybir.dt.float32
BF16 = mybir.dt.bfloat16
I32 = mybir.dt.int32
U32 = mybir.dt.uint32
ALU = mybir.AluOpType
ACT = mybir.ActivationFunctionType
AX = mybir.AxisListType
ds = bass.ds

STAGES = ("ffn0", "mamba", "ffn0", "ffn1", "attn", "ffn1")

P = 128
D = 128
BATCH, SEQ = 4, 1024
TOK = BATCH * SEQ
NT = TOK // P
GRP = 4
NG = NT // GRP
NE = 8
FF = 512
FB = FF // P
EPS = 1e-5
ME, MH = 4, 4
ZW, CW = 256, 512
HD = ZW // MH
MEH = ME * MH
NM = ME + MEH
TAPS = 4
QK = 16
LEAD = 4


class Signal:

    def __init__(self, nc, ctx, name, unit=1, lead=LEAD):
        self.sem = ctx.enter_context(nc.semaphore(name))
        self.unit = unit
        self.base = self.lead = lead * unit

    def at(self, n):
        return n * self.unit + self.base

    def close(self, total):
        self.base += total * self.unit


class Bench:

    def __init__(self, nc, ctx):
        self.nc, self.ctx, self.counters, self.new, self.stages = nc, ctx, {}, [], 0
        self.pending = (0, 0)

    def sb(self, name, shape, dt=F32):
        return self.ctx.enter_context(self.nc.sbuf_tensor(name, shape, dt))

    def scope(self, stack):
        self.stages += 1
        tag = self.stages
        return lambda name, shape, dt=F32: stack.enter_context(self.nc.sbuf_tensor(f"{name}_{tag}", shape, dt))

    def counter(self, name, unit=1, lead=LEAD):
        if name not in self.counters:
            self.counters[name] = Signal(self.nc, self.ctx, name, unit, lead)
            self.new.append(self.counters[name])
        return self.counters[name]

    def settle(self, eng):
        eng.sem_inc(self.counters["settled"].sem, 1)

    def start(self):
        if self.new:
            with self.nc.Block() as block:
                @block.sync
                def _(sp):
                    for s in self.new:
                        if s.lead:
                            sp.sem_inc(s.sem, s.lead)
            self.new = []


def bcast(ap, axis, n):
    shape = list(ap.shape)
    return ap.unsqueeze(axis).to_broadcast(shape[:axis] + [n] + shape[axis:])


class Chain:

    def __init__(self, eng, signal, start=0):
        self.eng, self.count, self.n = eng, signal, start

    def __call__(self, ins):
        self.n += 1
        ins.then_inc(self.count.sem, 1)
        self.eng.wait_ge(self.count.sem, self.count.at(self.n))


def in_turn(eng, n, ahead, behind):
    ahead(0, 0, 0)
    with eng.Fori(0, n // 2 - 1) as i:
        ahead(i * 2 + 1, 1, i)
        behind(i * 2, 0, i)
        ahead(i * 2 + 2, 0, i + 1)
        behind(i * 2 + 1, 1, i)
    ahead(n - 1, 1, n // 2 - 1)
    behind(n - 2, 0, n // 2 - 1)
    behind(n - 1, 1, n // 2 - 1)


def rounds(eng, n, lag, ring, step):
    def fixed(t):
        return lambda behind: (t - behind, (t - behind) % ring, (t - behind) // ring) if 0 <= t - behind < n else None

    full = (n - lag) // ring
    for t in range(lag):
        step(fixed(t))
    with eng.Fori(0, full) as i:
        for q in range(ring):
            step(lambda behind: (i * ring + (lag + q - behind), (lag + q - behind) % ring,
                                 i + (lag + q - behind) // ring))
    for t in range(lag + full * ring, n + lag):
        step(fixed(t))


def weave(eng, groups, units, ahead, behind, step):
    def fixed(t):
        return lambda d: divmod(t + d, units) if 0 <= t + d < groups * units else None

    for t in range(-ahead, behind):
        step(fixed(t))
    with eng.Fori(0, groups - 1) as g:
        for u in range(behind, units + behind):
            step(lambda d: (g + (u + d) // units, (u + d) % units))
    for t in range((groups - 1) * units + behind, groups * units + behind):
        step(fixed(t))


def prepare(k, S, router, nr, loads):
    nc = k.nc
    top, slots, x = k.pending[0], k.pending[1], k.x
    k.pending = (0, 0)
    weights_in = k.counter("weights_in", 16)
    var_ready, rstd_ready, xn_ready = (k.counter(n) for n in ("prep_var_ready", "prep_rstd_ready", "prep_xn_ready"))
    own, pool_own = k.counter("prep_vector_step"), k.counter("prep_pool_step")
    transposed, xt_copied, routed, logits_kept = (
        k.counter(n) for n in ("prep_transposed", "prep_xt_copied", "prep_routed", "prep_logits_kept"))
    stored = [k.counter(f"prep_stored{r}", 16) for r in range(2)]
    index_ready, added, k.first_added = (k.counter(f"back_{n}") for n in ("index_ready", "added", "first_added"))
    NR = GRP * top
    fetched = [k.counter(f"back_fetched{n}", 16, lead=0) for n in range(2 * NR)]
    xn4, xt4, xnT, stat, mv, rstd = k.xn4, k.xt4, k.xnT, k.stat, k.mv, k.rstd
    back = S("back", [P, 2 * NR, D]) if top else None
    rows = k.xn_rows.rearrange("(g j p) d -> p g j d", p=P, j=GRP)
    ps_t, ps_r = k.ps[:, 0:2, :], k.ps[:, 2:4, :]

    k.start()
    with nc.Block() as block:
        @block.vector
        def _(dve):
            V = nc.vector

            def statistics(g, r, i):
                take_back(k, dve, g, r, i, top, back, fetched, added)
                for j in range(GRP):
                    ins = V.bn_stats(stat[:, r, j, :], x[:, ds((g * GRP + j) * D, D)])
                ins.then_inc(own.sem, 1)
                dve.wait_ge(own.sem, own.at(g + 1))
                k.settle(dve)
                for j in range(GRP):
                    ins = V.bn_aggr(mv[:, r, j, :], stat[:, r, j, :])
                ins.then_inc(var_ready.sem, 1)

            def normalise(g, r, i):
                dve.wait_ge(rstd_ready.sem, rstd_ready.at(g + 1))
                dve.wait_ge(transposed.sem, transposed.at(g - 1))
                dve.wait_ge(stored[r].sem, stored[r].at(i))
                for j in range(GRP):
                    ins = V.tensor_scalar(xn4[:, r, j, :], x[:, ds((g * GRP + j) * D, D)],
                                          mv[:, r, j, 0:1], rstd[:, r, j:j + 1], ALU.subtract, ALU.mult)
                ins.then_inc(xn_ready.sem, 1)

            in_turn(dve, NG, statistics, normalise)

        @block.gpsimd
        def _(pool):
            def fetch(g, r, i):
                fetch_back(k, pool, g, r, top, slots, back, index_ready, fetched, added)

            def root(g, r, i):
                pool.wait_ge(var_ready.sem, var_ready.at(g + 1))
                pool.wait_ge(xn_ready.sem, xn_ready.at(g - 1))
                nc.gpsimd.tensor_tensor(rstd[:, r, :], mv[:, r, :, 1], k.eps[:, 0:GRP], ALU.add).then_inc(pool_own.sem, 1)
                pool.wait_ge(pool_own.sem, pool_own.at(g + 1))
                nc.gpsimd.tensor_tensor(rstd[:, r, :], rstd[:, r, :], k.minus_half[:, 0:GRP],
                                        ALU.pow).then_inc(rstd_ready.sem, 1)

            in_turn(pool, NG, fetch, root)

        @block.sync
        def _(sp):
            for dst, src in loads:
                sp.dma_start(dst, src, allow_slow_non_contiguous=True).then_inc(weights_in.sem, 16)
            with sp.Fori(0, NG // 2) as i:
                for r in range(2):
                    g = i * 2 + r
                    sp.wait_ge(xn_ready.sem, xn_ready.at(g + 1))
                    sp.wait_ge(stored[r].sem, stored[r].at(i))
                    sp.dma_start(rows[:, ds(g, 1)].rearrange("p g j d -> p (g j) d"), xn4[:, r, :, :]).then_inc(stored[r].sem, 16)
            for r in range(2):
                sp.wait_ge(stored[r].sem, stored[r].at(NG // 2))
            sp.wait_ge(weights_in.sem, weights_in.at(len(loads)))

        @block.tensor
        def _(pe):
            def transpose(g, r, i):
                pe.wait_ge(xn_ready.sem, xn_ready.at(g + 1))
                pe.wait_ge(xt_copied.sem, xt_copied.at(g - 1))
                for j in range(GRP):
                    ins = nc.tensor.transpose(ps_t[:, r, j * P:(j + 1) * P], xn4[:, r, j, :], k.ident[:, :])
                ins.then_inc(transposed.sem, 1)

            def score(g, r, i):
                if nr:
                    pe.wait_ge(xt_copied.sem, xt_copied.at(g + 1))
                    pe.wait_ge(logits_kept.sem, logits_kept.at(g - 1))
                    for j in range(GRP):
                        ins = nc.tensor.matmul(ps_r[:, r, j * nr:(j + 1) * nr], xt4[:, r, j * P:(j + 1) * P],
                                               router, start=True, stop=True)
                    ins.then_inc(routed.sem, 1)

            in_turn(pe, NG, transpose, score)

        @block.scalar
        def _(act):
            def copy(g, r, i):
                act.wait_ge(transposed.sem, transposed.at(g + 1))
                if nr:
                    act.wait_ge(routed.sem, routed.at(g - 1))
                    nc.scalar.copy(xt4[:, r, :], ps_t[:, r, :])
                nc.scalar.copy(xnT[:, ds(g * GRP * P, GRP * P)], ps_t[:, r, :]).then_inc(xt_copied.sem, 1)

            def keep(g, r, i):
                if nr:
                    act.wait_ge(routed.sem, routed.at(g + 1))
                    nc.scalar.copy(k.logits[:, ds(g * GRP * nr, GRP * nr)], ps_r[:, r, 0:GRP * nr]
                                   ).then_inc(logits_kept.sem, 1)

            in_turn(act, NG, copy, keep)

    weights_in.close(len(loads))
    for s in (var_ready, rstd_ready, xn_ready, own, pool_own, transposed, xt_copied):
        s.close(NG)
    if nr:
        routed.close(NG)
        logits_kept.close(NG)
    for s in stored:
        s.close(NG // 2)
    close_back(k, top, index_ready, fetched, added)


def fetch_back(k, pool, g, r, top, slots, back, index_ready, fetched, added):
    if not top:
        return
    NR = GRP * top
    pool.wait_ge(added.sem, added.at(g - 1))
    k.settle(pool)
    for c in range(top):
        ins = k.nc.gpsimd.tensor_copy(k.index[:, r * NR + c * GRP:r * NR + (c + 1) * GRP],
                                      k.pos[:, ds(g * GRP + c * NT, GRP)])
    ins.then_inc(index_ready.sem, 1)
    pool.wait_ge(index_ready.sem, index_ready.at(g + 1))
    k.settle(pool)
    for n in range(r * NR, (r + 1) * NR):
        k.nc.gpsimd.indirect_dma_start(back[:, n, :], None, k.y_rows[0:slots * P, :],
                                       bass.IndirectOffsetOnAxis(ap=k.index[:, n:n + 1], axis=0)
                                       ).then_inc(fetched[n].sem, 16)


def take_back(k, dve, g, r, i, top, back, fetched, added):
    if not top:
        return
    NR = GRP * top
    V = k.nc.vector
    for n in range(r * NR, r * NR + GRP):
        dve.wait_ge(fetched[n].sem, fetched[n].at(i + 1))
    if top == 1:
        xg = k.x[:, ds(g * GRP * D, GRP * D)]
        V.scalar_tensor_tensor(xg, back[:, r * NR:(r + 1) * NR, :].rearrange("p j d -> p (j d)"), 0.5, xg,
                               ALU.mult, ALU.add).then_inc(added.sem, 1)
        dve.wait_ge(added.sem, added.at(g + 1))
        k.settle(dve)
        return
    for c in range(top):
        for j in range(GRP):
            n = r * NR + c * GRP + j
            if c:
                dve.wait_ge(fetched[n].sem, fetched[n].at(i + 1))
            xt = k.x[:, ds((g * GRP + j) * D, D)]
            ins = V.scalar_tensor_tensor(xt, back[:, n, :], k.gate[:, c, ds(g * GRP + j, 1)], xt, ALU.mult, ALU.add)
        if c == 0:
            ins.then_inc(k.first_added.sem, 1)
            dve.wait_ge(k.first_added.sem, k.first_added.at(g + 1))
    ins.then_inc(added.sem, 1)
    dve.wait_ge(added.sem, added.at(g + 1))
    k.settle(dve)


def close_back(k, top, index_ready, fetched, added):
    if top == 2:
        k.first_added.close(NG)
    if top:
        index_ready.close(NG)
        added.close(NG)
        for s in fetched:
            s.close(NG // 2)


def route(k, top, slots, alone):
    nc = k.nc
    own = k.counter("route_vector_step")
    marks, counted = k.counter("route_marks_ready"), k.counter("route_counted")
    weights, expd = k.counter("route_difference_ready"), k.counter("route_exp_done")
    place_counters(k)
    NB = top * NG
    L3 = k.logits[:, 0:NT * NE].rearrange("p (t e) -> p t e", e=NE)
    r3 = [k.rt[i][:, :].rearrange("p (t e) -> p t e", e=NE) for i in range(5)]
    e3 = [k.rt[i][:, :].rearrange("p (e t) -> p e t", e=NE) for i in range(5)]
    NP = top * NT
    ps_rank, ps_cnt = k.ps[:, 0, 0:NE * NT], k.ps[:, 1, 0:NE * NT]
    V = nc.vector

    k.start()
    with nc.Block() as block:
        @block.vector
        def _(dve):
            do = Chain(dve, own)
            logit, eq, sel = L3, r3[4], [r3[0], r3[1]]
            for c in range(top):
                do(V.tensor_reduce(k.best[:, c, :], logit, AX.X, ALU.max))
                do(V.tensor_tensor(eq, logit, bcast(k.best[:, c, :], 2, NE), ALU.is_equal))
                do(V.tensor_tensor(eq, eq, bcast(k.falling[:, :], 1, NT), ALU.mult))
                do(V.tensor_reduce(k.small[:, 0:NT], eq, AX.X, ALU.max))
                do(V.tensor_tensor(sel[c], eq, bcast(k.small[:, 0:NT], 2, NE), ALU.is_equal))
                if c + 1 < top:
                    do(V.scalar_tensor_tensor(r3[3], sel[c], -1e30, L3, ALU.mult, ALU.add))
                    logit = r3[3]
            if top == 2:
                V.tensor_sub(k.small[:, 0:NT], k.best[:, 1, :], k.best[:, 0, :]).then_inc(weights.sem, 1)
                dve.wait_ge(expd.sem, expd.at(1))
                do(V.tensor_scalar(k.small[:, NT:2 * NT], k.small[:, 0:NT], 1.0, None, ALU.add))
                do(V.reciprocal(k.gate[:, 0, :], k.small[:, NT:2 * NT]))
                do(V.tensor_scalar(k.gate[:, 0, :], k.gate[:, 0, :], 0.5, None, ALU.mult))
                do(V.tensor_mul(k.gate[:, 1, :], k.small[:, 0:NT], k.gate[:, 0, :]))
                do(V.tensor_add(r3[4], sel[0], sel[1]))
                V.tensor_copy(k.marks[:, :].rearrange("p (e t) -> p t e", e=NE), r3[4]).then_inc(marks.sem, 1)
            else:
                V.tensor_copy(k.marks[:, :].rearrange("p (e t) -> p t e", e=NE), sel[0]).then_inc(marks.sem, 1)
            dve.wait_ge(counted.sem, counted.at(1))
            cnt, incl = k.rt[2], k.rt[3]
            do(V.tensor_copy(cnt[:, :], ps_cnt))
            do(V.tensor_tensor_scan(incl[:, :], k.carry[:, :], cnt[:, :], 0.0, ALU.mult, ALU.add))
            do(V.tensor_sub(cnt[:, :], incl[:, :], cnt[:, :]))
            do(V.tensor_tensor(cnt[:, :], cnt[:, :], ps_rank, ALU.add))
            do(V.tensor_scalar(k.n_int[:, :], e3[3][:, :, NT - 1], float(P - 1), None, ALU.add))
            do(V.tensor_single_scalar(k.n_int[:, :], k.n_int[:, :], 7, ALU.arith_shift_right))
            do(V.tensor_copy(k.e8[:, 0, :], k.n_int[:, :]))
            do(V.tensor_tensor_scan(k.e8[:, 1, :], k.ones[:, 0:NE], k.e8[:, 0, :], 0.0, ALU.mult, ALU.add))
            do(V.tensor_sub(k.e8[:, 1, :], k.e8[:, 1, :], k.e8[:, 0, :]))
            do(V.tensor_scalar(k.e8[:, 2, :], k.e8[:, 1, :], float(P), None, ALU.mult))
            do(V.tensor_tensor(e3[3], e3[2], bcast(k.e8[:, 2, :], 2, NT), ALU.add))
            for c in range(top):
                cols = slice(c * NT, (c + 1) * NT)
                do(V.tensor_tensor(r3[4], sel[c], k.rt[3][:, :].rearrange("p (e t) -> p t e", e=NE), ALU.mult))
                do(V.tensor_reduce(k.posf[:, cols], r3[4], AX.X, ALU.add))
            do(V.tensor_copy(k.pos[:, 0:NP], k.posf[:, 0:NP]))
            do(V.tensor_single_scalar(k.hi_int[:, 0:NP], k.pos[:, 0:NP].bitcast(I32), 7, ALU.arith_shift_right))
            do(V.tensor_copy(k.hi[:, 0:NP], k.hi_int[:, 0:NP]))
            do(V.scalar_tensor_tensor(k.lo[:, 0:NP], k.hi[:, 0:NP], -float(P), k.posf[:, 0:NP], ALU.mult, ALU.add))
            do(V.tensor_scalar(k.erow[:, 0:slots], k.iota[:, 0:slots], k.e8[:, 1, 1:2], None, ALU.is_ge))
            for e in range(2, NE):
                do(V.scalar_tensor_tensor(k.erow[:, 0:slots], k.iota[:, 0:slots], k.e8[:, 1, e:e + 1],
                                          k.erow[:, 0:slots], ALU.is_ge, ALU.add))
            do(V.tensor_copy(k.slot_expert[:, 0:slots], k.erow[:, 0:slots]))
            if alone:
                with dve.Fori(0, NB // 2) as i:
                    for r in range(2):
                        place_vector(k, dve, i * 2 + r, r, slots)
                place_end(k, dve, NB, slots)
            k.route_steps = do.n

        @block.scalar
        def _(act):
            if top == 2:
                act.wait_ge(weights.sem, weights.at(1))
                nc.scalar.activation(k.small[:, 0:NT], k.small[:, 0:NT], ACT.Exp).then_inc(expd.sem, 1)

        @block.tensor
        def _(pe):
            pe.wait_ge(marks.sem, marks.at(1))
            nc.tensor.matmul(ps_rank, k.before[:, :], k.marks[:, :], start=True, stop=True)
            nc.tensor.matmul(ps_cnt, k.ones_bf[:, :], k.marks[:, :], start=True, stop=True).then_inc(counted.sem, 1)
            if alone:
                open_table(k, slots)
                with pe.Fori(0, NB // 2) as i:
                    for r in range(2):
                        place_tensor(k, pe, i * 2 + r, r, slots)

    own.close(k.route_steps)
    marks.close(1)
    counted.close(1)
    if top == 2:
        weights.close(1)
        expd.close(1)
    if alone:
        close_places(k, NB)


def place_counters(k):
    k.onehot, k.placed, k.place_own = (k.counter(f"place_{n}") for n in ("onehot_ready", "done", "step"))


def close_places(k, batches):
    k.onehot.close(batches)
    k.placed.close(batches)
    k.place_own.close(2)


def place_vector(k, dve, n, r, slots):
    V = k.nc.vector
    dve.wait_ge(k.placed.sem, k.placed.at(n - 1))
    for j in range(GRP):
        t = n * GRP + j
        V.tensor_scalar(k.oh_lane[:, r, j, :], k.iota_bf[:, 0:P], k.lo[:, ds(t, 1)], None, ALU.is_equal)
        V.tensor_scalar(k.oh_slot[:, r, j, 0:slots], k.iota_bf[:, 0:slots], k.hi[:, ds(t, 1)],
                        k.lane[:, 0:1], ALU.is_equal, ALU.mult)
        ins = V.tensor_scalar(k.oh_slot[:, r, j, slots:2 * slots], k.iota_bf[:, 0:slots], k.hi[:, ds(t, 1)],
                              k.tile_of[:, ds(t, 1)], ALU.is_equal, ALU.mult)
    ins.then_inc(k.onehot.sem, 1)


def place_end(k, dve, batches, slots):
    V, table, own = k.nc.vector, k.ps[:, 6, 0:2 * slots], k.place_own
    dve.wait_ge(k.placed.sem, k.placed.at(batches))
    V.tensor_copy(k.erow[:, 0:slots], table[:, 0:slots]).then_inc(own.sem, 1)
    dve.wait_ge(own.sem, own.at(1))
    V.scalar_tensor_tensor(k.slot_token[:, 0:slots], table[:, slots:2 * slots], float(P), k.erow[:, 0:slots],
                           ALU.mult, ALU.add).then_inc(own.sem, 1)
    dve.wait_ge(own.sem, own.at(2))


def open_table(k, slots):
    k.nc.tensor.matmul(k.ps[:, 6, 0:2 * slots], k.ones_bf[:, :], k.zeros_bf[:, 0:2 * slots], start=True,
                       stop=False, skip_group_check=True)


def place_tensor(k, pe, n, r, slots):
    pe.wait_ge(k.onehot.sem, k.onehot.at(n + 1))
    for j in range(GRP):
        ins = k.nc.tensor.matmul(k.ps[:, 6, 0:2 * slots], k.oh_lane[:, r, j, :], k.oh_slot[:, r, j, 0:2 * slots],
                                 start=False, stop=False, skip_group_check=True)
    ins.then_inc(k.placed.sem, 1)


def shared(k, slots):
    nc = k.nc
    place_counters(k)
    up, acted, ready, down_done, added = (k.counter(f"shared_{n}") for n in ("up", "acted", "inner_ready", "down", "added"))
    w12, w3 = k.w12[:, NE, :], k.w3[:, NE]
    h1, h2, py = k.ps[:, 0:2, :], k.ps[:, 2:4, :], k.ps[:, 4:6, :]
    NU = NG * FB

    k.start()
    with nc.Block() as block:
        @block.tensor
        def _(pe):
            def up_block(g, b):
                u, r = g * FB + b, b % 2
                pe.wait_ge(ready.sem, ready.at(u - 1))
                nc.tensor.matmul(h1[:, r, :], w12[:, b * P:(b + 1) * P], k.xnT[:, ds(g * GRP * P, GRP * P)],
                                 start=True, stop=True)
                nc.tensor.matmul(h2[:, r, :], w12[:, FF + b * P:FF + (b + 1) * P],
                                 k.xnT[:, ds(g * GRP * P, GRP * P)], start=True, stop=True).then_inc(up.sem, 1)

            def down_group(g, r):
                pe.wait_ge(ready.sem, ready.at((g + 1) * FB))
                pe.wait_ge(added.sem, added.at(g - 1))
                for j in range(GRP):
                    for b in range(FB):
                        ins = nc.tensor.matmul(py[:, r, j * P:(j + 1) * P], k.inner[:, r, b, j * P:(j + 1) * P],
                                               w3[:, b, :], start=(b == 0), stop=(b == FB - 1))
                ins.then_inc(down_done.sem, 1)

            def up_group(g, r, i):
                for b in range(FB):
                    up_block(g, b)

            def down(g, r, i):
                place_tensor(k, pe, g, r, slots)
                down_group(g, r)

            open_table(k, slots)
            in_turn(pe, NG, up_group, down)

        @block.scalar
        def _(act):
            with act.Fori(0, NG) as g:
                for b in range(FB):
                    u = g * FB + b
                    act.wait_ge(up.sem, up.at(u + 1))
                    act.wait_ge(ready.sem, ready.at(u - 1))
                    nc.scalar.activation(k.gl[:, b % 2, :], h1[:, b % 2, :], ACT.Gelu).then_inc(acted.sem, 1)

        @block.vector
        def _(dve):
            def inner(g, r):
                dve.wait_ge(down_done.sem, down_done.at(g - 1))
                for b in range(FB):
                    u = g * FB + b
                    dve.wait_ge(acted.sem, acted.at(u + 1))
                    nc.vector.tensor_tensor(k.inner[:, r, b, :], k.gl[:, b % 2, :], h2[:, b % 2, :],
                                            ALU.mult).then_inc(ready.sem, 1)

            def add(g, r):
                dve.wait_ge(down_done.sem, down_done.at(g + 1))
                xg = k.x[:, ds(g * GRP * D, GRP * D)]
                nc.vector.scalar_tensor_tensor(xg, py[:, r, :], 0.5, xg, ALU.mult, ALU.add).then_inc(added.sem, 1)

            def ahead(g, r, i):
                inner(g, r)
                place_vector(k, dve, g, r, slots)

            in_turn(dve, NG, ahead, lambda g, r, i: add(g, r))
            place_end(k, dve, NG, slots)
            dve.wait_ge(added.sem, added.at(NG))

    for s in (up, acted, ready):
        s.close(NU)
    down_done.close(NG)
    close_places(k, NG)
    added.close(NG)


def experts(k, top, slots):
    nc = k.nc
    RING, LAG = 4, 4
    gathered = [k.counter(f"slot_gathered{r}", 16, lead=0) for r in range(RING)]
    stored = [k.counter(f"slot_stored{r}", 16) for r in range(RING)]
    index_ready, weights_ready, transposed, gT_ready, up_done, act_done, inner_ready, down_done, y_ready = (
        k.counter(f"slot_{n}") for n in ("index_ready", "weights_ready", "transposed", "gT_ready", "up_done",
                                         "act_done", "inner_ready", "down_done", "y_ready"))
    biased = k.counter("slot_biased")
    ps_t, h1, h2, py = k.ps[:, 0:2, 0:P], k.ps[:, 2:4, :], k.ps[:, 4:6, :], k.ps[:, 6:8, 0:D]
    wide = 2 * FF if top == 1 else FF
    w_up = k.w12[:, :, :].rearrange("p e n -> p (e n)") if top == 1 else k.w1[:, :, :].rearrange("p e n -> p (e n)")
    w_dn = (k.w3 if top == 1 else k.w2)[:, :, :, :].rearrange("p e b d -> p (e b d)")
    y_rows = k.y_rows.rearrange("(s p) d -> s p d", p=P)

    def expert_of(eng, s):
        return eng.value_load(k.slot_expert[0:1, ds(s, 1)], min_val=0, max_val=NE - 1)

    k.start()
    with nc.Block() as block:
        @block.gpsimd
        def _(pool):
            def step(at):
                if at(0):
                    s, q, _ = at(0)
                    pool.wait_ge(transposed.sem, transposed.at(s - 3))
                    k.settle(pool)
                    nc.gpsimd.tensor_copy(k.index[:, q:q + 1], k.slot_token[:, ds(s, 1)]).then_inc(index_ready.sem, 1)
                    pool.wait_ge(index_ready.sem, index_ready.at(s + 1))
                    k.settle(pool)
                    nc.gpsimd.indirect_dma_start(k.rows_in[:, q, :], None, k.xn_rows[:, :],
                                                 bass.IndirectOffsetOnAxis(ap=k.index[:, q:q + 1], axis=0)
                                                 ).then_inc(gathered[q].sem, 16)
            rounds(pool, slots, LAG, RING, step)

        @block.tensor
        def _(pe):
            def turn(s, q, n):
                pe.wait_ge(gathered[q].sem, gathered[q].at(n + 1))
                pe.wait_ge(gT_ready.sem, gT_ready.at(s - 1))
                nc.tensor.transpose(ps_t[:, q % 2, :], k.rows_in[:, q, :], k.ident[:, :]).then_inc(transposed.sem, 1)

            def up(s, q, n):
                r = q % 2
                pe.wait_ge(gT_ready.sem, gT_ready.at(s + 1))
                pe.wait_ge(weights_ready.sem, weights_ready.at(s + 1))
                if top == 1:
                    pe.wait_ge(inner_ready.sem, inner_ready.at(s - 1))
                else:
                    pe.wait_ge(biased.sem, biased.at(s - 1))
                for b in range(FB):
                    ins = nc.tensor.matmul(h1[:, r, b * P:(b + 1) * P], k.w_slot[:, r, b * P:(b + 1) * P],
                                           k.gT[:, r, :], start=True, stop=True)
                if top == 1:
                    for b in range(FB):
                        ins = nc.tensor.matmul(h2[:, r, b * P:(b + 1) * P], k.w_slot[:, r, FF + b * P:FF + (b + 1) * P],
                                               k.gT[:, r, :], start=True, stop=True)
                ins.then_inc(up_done.sem, 1)

            def down(s, q, n):
                e = expert_of(pe, s)
                pe.wait_ge(inner_ready.sem, inner_ready.at(s + 1))
                pe.wait_ge(y_ready.sem, y_ready.at(s - 1))
                for b in range(FB):
                    ins = nc.tensor.matmul(py[:, q % 2, :], k.inner_slot[:, q, b * P:(b + 1) * P],
                                           w_dn[:, ds(e * (FB * D) + b * D, D)], start=(b == 0), stop=(b == FB - 1))
                ins.then_inc(down_done.sem, 1)

            def step(at):
                for stage, behind in ((turn, 0), (up, 1), (down, 3)):
                    if at(behind):
                        stage(*at(behind))
            rounds(pe, slots, LAG, RING, step)

        @block.scalar
        def _(act):
            def weights(s, q, n):
                e = expert_of(act, s)
                act.wait_ge(up_done.sem, up_done.at(s - 1))
                nc.scalar.copy(k.w_slot[:, q % 2, 0:wide], w_up[:, ds(e * wide, wide)]).then_inc(weights_ready.sem, 1)

            def rows(s, q, n):
                act.wait_ge(transposed.sem, transposed.at(s + 1))
                act.wait_ge(up_done.sem, up_done.at(s - 1))
                nc.scalar.copy(k.gT[:, q % 2, :], ps_t[:, q % 2, :]).then_inc(gT_ready.sem, 1)

            def gelu(s, q, n):
                act.wait_ge(up_done.sem, up_done.at(s + 1))
                act.wait_ge(inner_ready.sem, inner_ready.at(s - 1))
                nc.scalar.activation(k.gl[:, q % 2, :], h1[:, q % 2, :], ACT.Gelu).then_inc(act_done.sem, 1)

            def gelu_or_tanh(s, q, n):
                e = expert_of(act, s)
                act.wait_ge(biased.sem, biased.at(s + 1))
                act.wait_ge(down_done.sem, down_done.at(s - 3))
                with act.If(e % 2 == 0):
                    nc.scalar.activation(k.inner_slot[:, q, :], k.hb[:, q, :], ACT.Gelu).then_inc(act_done.sem, 1)
                with act.Else():
                    nc.scalar.activation(k.inner_slot[:, q, :], k.hb[:, q, :], ACT.Tanh, scale=0.5).then_inc(act_done.sem, 1)

            def step(at):
                stages = ((rows, 0), (gelu, 1)) if top == 1 else ((weights, 0), (rows, 0), (gelu_or_tanh, 1))
                for stage, behind in stages:
                    if at(behind):
                        stage(*at(behind))
            nc.scalar.activation(k.spare[:, 1:2], k.zero[:, 0:1], ACT.Gelu)
            rounds(act, slots, LAG, RING, step)

        @block.vector
        def _(dve):
            V = nc.vector

            def weights(s, q, n):
                e = expert_of(dve, s)
                dve.wait_ge(up_done.sem, up_done.at(s - 1))
                V.tensor_copy(k.w_slot[:, q % 2, 0:wide], w_up[:, ds(e * wide, wide)]).then_inc(weights_ready.sem, 1)

            def gated(s, q, n):
                dve.wait_ge(act_done.sem, act_done.at(s + 1))
                dve.wait_ge(down_done.sem, down_done.at(s - 3))
                V.tensor_tensor(k.inner_slot[:, q, :], k.gl[:, q % 2, :], h2[:, q % 2, :], ALU.mult
                                ).then_inc(inner_ready.sem, 1)

            def bias(s, q, n):
                e = expert_of(dve, s)
                dve.wait_ge(up_done.sem, up_done.at(s + 1))
                V.tensor_tensor(k.hb[:, q, :].rearrange("p (b t) -> p b t", b=FB),
                                h1[:, q % 2, :].rearrange("p (b t) -> p b t", b=FB),
                                bcast(k.b1[:, ds(e * FB, FB)], 2, P), ALU.add).then_inc(biased.sem, 1)

            def silu(s, q, n):
                e = expert_of(dve, s)
                dve.wait_ge(act_done.sem, act_done.at(s + 1))
                dve.wait_ge(inner_ready.sem, inner_ready.at(s))
                with dve.If(e % 2 == 0):
                    dve.sem_inc(inner_ready.sem, 1)
                with dve.Else():
                    V.scalar_tensor_tensor(k.inner_slot[:, q, :], k.inner_slot[:, q, :], 1.0, k.hb[:, q, :],
                                           ALU.add, ALU.mult).then_inc(inner_ready.sem, 1)

            def output(s, q, n):
                if top == 2:
                    e = expert_of(dve, s)
                dve.wait_ge(down_done.sem, down_done.at(s + 1))
                dve.wait_ge(stored[q].sem, stored[q].at(n))
                if top == 1:
                    V.tensor_copy(k.y[:, q, :], py[:, q % 2, :]).then_inc(y_ready.sem, 1)
                else:
                    V.tensor_tensor(k.y[:, q, :], py[:, q % 2, :], k.b2[:, ds(e * D, D)], ALU.add
                                    ).then_inc(y_ready.sem, 1)

            def step(at):
                stages = ((weights, 0), (gated, 2), (output, 4)) if top == 1 else ((bias, 1), (silu, 2), (output, 4))
                for stage, behind in stages:
                    if at(behind):
                        stage(*at(behind))
            rounds(dve, slots, LAG, RING, step)

        @block.sync
        def _(sp):
            def step(at):
                if at(4):
                    s, q, n = at(4)
                    sp.wait_ge(y_ready.sem, y_ready.at(s + 1))
                    sp.dma_start(y_rows[ds(s, 1)].rearrange("s p d -> (s p) d"), k.y[:, q, :]).then_inc(stored[q].sem, 16)
            rounds(sp, slots, LAG, RING, step)
            for q in range(RING):
                sp.wait_ge(stored[q].sem, stored[q].at((slots - q + RING - 1) // RING))

    for s in (index_ready, weights_ready, transposed, gT_ready, up_done, act_done, inner_ready, down_done, y_ready):
        s.close(slots)
    if top == 2:
        biased.close(slots)
    for q in range(RING):
        gathered[q].close((slots - q + RING - 1) // RING)
        stored[q].close((slots - q + RING - 1) // RING)
    k.pending = (top, slots)


def attend(k, w):
    nc = k.nc
    QB = SEQ // P
    SCALE = float(QK) ** -0.5
    w_turned, w_ready = k.counter("attn_w_turned"), k.counter("attn_w_ready")
    projected, qk_ready = k.counter("attn_projected"), k.counter("attn_qk_ready")
    v_in, q_ready = k.counter("attn_v_in", 16), k.counter("attn_queries_ready")
    scored, masked, maxed, expd, turned, pt_ready, mixed, added = (
        k.counter(f"attn_{n}") for n in ("scored", "masked", "max_ready", "exp_done", "probs_turned",
                                        "probsT_ready", "mixed", "added"))
    own = k.counter("attn_vector_step")
    with ExitStack() as stack:
        S = k.scope(stack)
        wqk, wT, bqk = S("wqk", [QK, 2, D]), S("wT", [P, 2, QK]), S("bqk", [QK, 2])
        qT, kT = S("qT", [QK, TOK]), S("kT", [QK, TOK])
        q_in = S("q_in", [QK, 2, P])
        v = S("v", [P, NT, D])
        probs, pT = S("probs", [P, 2, SEQ]), S("pT", [P, 2, SEQ])
        keep, fill = S("keep", [P, P]), S("fill", [P, P])
        top, nmax, total, inv = (S(n, [P, 2]) for n in ("top", "nmax", "total", "inv"))
        loads = [(wqk[:, 0, :], w["L1_attn_w_q"]), (wqk[:, 1, :], w["L1_attn_w_k"]),
                 (bqk[:, 0:1], w["L1_attn_b_q"].unsqueeze(1)), (bqk[:, 1:2], w["L1_attn_b_k"].unsqueeze(1))]
        prepare(k, S, None, 0, loads)
        ps_s = [k.ps[:, 2 * r:2 * r + 2, :].rearrange("p b n -> p (b n)") for r in range(2)]
        ps_t = k.ps[:, 4:6, :].rearrange("p b n -> p (b n)")
        ps_o = k.ps[:, 6:8, 0:D]
        ps_q = k.ps[:, 6:8, :]

        k.start()
        with nc.Block() as block:
            @block.gpsimd
            def _(pool):
                nc.gpsimd.affine_select(out=keep[:, :], in_=k.ones[:, :], compare_op=ALU.is_ge, fill=0.0, base=0,
                                        pattern=[[-1, P]], channel_multiplier=1).then_inc(w_turned.sem, 1)
                pool.wait_ge(w_turned.sem, w_turned.at(1))
                nc.gpsimd.tensor_scalar(fill[:, :], keep[:, :], -1.0, 10000.0 / SCALE, ALU.add, ALU.mult
                                        ).then_inc(w_turned.sem, 1)

            @block.sync
            def _(sp):
                sp.dma_start(v[:, :, :], k.xn_rows.rearrange("(t p) d -> p t d", p=P)).then_inc(v_in.sem, 16)
                sp.wait_ge(v_in.sem, v_in.at(1))

            @block.tensor
            def _(pe):
                for i in range(2):
                    ins = nc.tensor.transpose(ps_t[:, i * QK:(i + 1) * QK], wqk[:, i, :], k.ident[0:QK, 0:QK])
                ins.then_inc(w_ready.sem, 1)
                pe.wait_ge(w_ready.sem, w_ready.at(2))
                with pe.Fori(0, NG) as g:
                    for i in range(2):
                        pe.wait_ge(qk_ready.sem, qk_ready.at(g * 2 + i - 1))
                        k.settle(pe)
                        nc.tensor.matmul(ps_q[0:QK, i, :], wT[:, i, :], k.xnT[:, ds(g * GRP * P, GRP * P)],
                                         start=True, stop=True).then_inc(projected.sem, 1)

            @block.scalar
            def _(act):
                act.wait_ge(w_ready.sem, w_ready.at(1))
                nc.scalar.copy(wT[:, :, :].rearrange("p a n -> p (a n)"), ps_t[:, 0:2 * QK]).then_inc(w_ready.sem, 1)
                with act.Fori(0, NG) as g:
                    for i, dst in enumerate((qT, kT)):
                        act.wait_ge(projected.sem, projected.at(g * 2 + i + 1))
                        nc.scalar.activation(dst[:, ds(g * GRP * P, GRP * P)], ps_q[0:QK, i, :], ACT.Identity,
                                             bias=bqk[:, i:i + 1]).then_inc(qk_ready.sem, 1)

        k.start()
        with nc.Block() as block:
            @block.gpsimd
            def _(pool):
                def queries(b, q):
                    n, r = b * QB + q, q % 2
                    pool.wait_ge(scored.sem, scored.at(n - 1))
                    k.settle(pool)
                    nc.gpsimd.tensor_copy(q_in[:, r, :], qT[:, ds(n * P, P)]).then_inc(q_ready.sem, 1)

                def step(at):
                    if at(1):
                        queries(*at(1))
                weave(pool, BATCH, QB, 1, 2, step)

            @block.tensor
            def _(pe):
                def score(b, q):
                    n, r = b * QB + q, q % 2
                    pe.wait_ge(q_ready.sem, q_ready.at(n + 1))
                    pe.wait_ge(expd.sem, expd.at(n - 1))
                    k.settle(pe)
                    for c in range(0, (q + 1) * P, 512):
                        width = min(512, (q + 1) * P - c)
                        ins = nc.tensor.matmul(ps_s[r][:, c:c + width], q_in[:, r, :], kT[:, ds(b * SEQ + c, width)],
                                               start=True, stop=True)
                    ins.then_inc(scored.sem, 1)

                def turn(b, q):
                    n, r = b * QB + q, q % 2
                    pe.wait_ge(expd.sem, expd.at(n + 1))
                    pe.wait_ge(pt_ready.sem, pt_ready.at(n))
                    for c in range(q + 1):
                        ins = nc.tensor.transpose(ps_t[:, c * P:(c + 1) * P], probs[:, r, c * P:(c + 1) * P], k.ident[:, :])
                    ins.then_inc(turned.sem, 1)

                def mix(b, q):
                    n, r = b * QB + q, q % 2
                    pe.wait_ge(pt_ready.sem, pt_ready.at(n + 1))
                    pe.wait_ge(added.sem, added.at(n - 1))
                    for c in range(q + 1):
                        ins = nc.tensor.matmul(ps_o[:, r, :], pT[:, r, c * P:(c + 1) * P],
                                               v[:, ds(b * QB + c, 1), :].rearrange("p a d -> p (a d)"),
                                               start=(c == 0), stop=(c == q))
                    ins.then_inc(mixed.sem, 1)

                def step(at):
                    for stage, d in ((score, 0), (mix, -2), (turn, -1)):
                        if at(d):
                            stage(*at(d))
                weave(pe, BATCH, QB, 1, 2, step)

            @block.scalar
            def _(act):
                def exponential(b, q):
                    n, r, width = b * QB + q, q % 2, (q + 1) * P
                    act.wait_ge(maxed.sem, maxed.at(n + 1))
                    act.wait_ge(turned.sem, turned.at(n - 1))
                    act.wait_ge(added.sem, added.at(n - 1))
                    nc.scalar.activation(probs[:, r, 0:width], ps_s[r][:, 0:width], ACT.Exp, scale=SCALE,
                                         bias=nmax[:, r:r + 1], accum_out=total[:, r:r + 1]).then_inc(expd.sem, 1)

                def copy(b, q):
                    n, r, width = b * QB + q, q % 2, (q + 1) * P
                    act.wait_ge(turned.sem, turned.at(n + 1))
                    act.wait_ge(mixed.sem, mixed.at(n - 1))
                    nc.scalar.copy(pT[:, r, 0:width], ps_t[:, 0:width]).then_inc(pt_ready.sem, 1)

                def step(at):
                    for stage, d in ((exponential, 0), (copy, -1)):
                        if at(d):
                            stage(*at(d))
                weave(act, BATCH, QB, 1, 2, step)

            @block.vector
            def _(dve):
                V = nc.vector

                def maximum(b, q):
                    n, r = b * QB + q, q % 2
                    last = ps_s[r][:, q * P:(q + 1) * P]
                    dve.wait_ge(scored.sem, scored.at(n + 1))
                    V.tensor_tensor(last, last, keep[:, :], ALU.mult).then_inc(own.sem, 1)
                    dve.wait_ge(own.sem, own.at(n * 3 + 1))
                    V.tensor_tensor(last, last, fill[:, :], ALU.add).then_inc(own.sem, 1)
                    dve.wait_ge(own.sem, own.at(n * 3 + 2))
                    V.tensor_reduce(top[:, r:r + 1], ps_s[r][:, 0:(q + 1) * P], AX.X, ALU.max).then_inc(own.sem, 1)
                    dve.wait_ge(own.sem, own.at(n * 3 + 3))
                    dve.wait_ge(expd.sem, expd.at(n - 1))
                    V.tensor_scalar(nmax[:, r:r + 1], top[:, r:r + 1], -SCALE, None, ALU.mult).then_inc(maxed.sem, 1)

                def add(b, q):
                    n, r = b * QB + q, q % 2
                    dve.wait_ge(mixed.sem, mixed.at(n + 1))
                    V.reciprocal(inv[:, r:r + 1], total[:, r:r + 1]).then_inc(masked.sem, 1)
                    dve.wait_ge(masked.sem, masked.at(n + 1))
                    xt = k.x[:, ds(n * D, D)]
                    V.scalar_tensor_tensor(xt, ps_o[:, r, :], inv[:, r:r + 1], xt, ALU.mult, ALU.add
                                           ).then_inc(added.sem, 1)

                def step(at):
                    for stage, d in ((maximum, 0), (add, -2)):
                        if at(d):
                            stage(*at(d))
                weave(dve, BATCH, QB, 1, 2, step)
        n = BATCH * QB
        for s in (scored, masked, maxed, expd, turned, pt_ready, mixed, added, q_ready):
            s.close(n)
        own.close(3 * n)
        w_turned.close(2)
        w_ready.close(2)
        projected.close(2 * NG)
        qk_ready.close(2 * NG)
        v_in.close(1)


def mamba(k, w):
    nc = k.nc
    with ExitStack() as stack:
        S = k.scope(stack)
        m = Weights()
        m.win, m.wout, m.nw = S("win", [P, ME, ZW + CW + MH]), S("wout", [P, ME, 2, D]), S("nw", [P, ME * 2])
        m.cw, m.cb = S("cw", [P, ME * 4, TAPS]), S("cb", [P, ME * 4])
        m.dtb, m.aneg, m.dsk = (S(n, [P, MEH]) for n in ("dtb", "aneg", "dsk"))
        m.diagD = S("diagD", [P, MEH, P])
        m.tri, m.identb = S("tri", [P, P]), S("identb", [P, P], BF16)
        m.future = S("future", [P, MH, P], BF16)
        m.pickA, m.pickQ = S("pickA", [P, MEH, P], BF16), S("pickQ", [P, ME, MH * P], BF16)
        m.keep = S("keepg", [P, NG])
        m.rout = S("rout", [P, NT * ME])
        m.wst, m.ea, m.cd = (S(n, [P, NT * MEH]) for n in ("wst", "ea", "cd"))
        m.rows = S("rows", [P, NT * P], BF16)
        in_w = w["L0_attn_in_w"]
        loads = [
            (m.win[:, :, :], in_w.rearrange("e d n -> d e n")),
            (m.wout[:, :].rearrange("p e b d -> p (e b) d"), w["L0_attn_out_w"].rearrange("e (b p) d -> p (e b) d", p=P)),
            (m.nw[:, :], w["L0_attn_norm_w"].rearrange("e (b p) -> p (e b)", p=P)),
            (m.cw[:, :, :], w["L0_attn_conv_w"].rearrange("e (b p) k -> p (e b) k", p=P)),
            (m.cb[:, :], w["L0_attn_conv_b"].rearrange("e (b p) -> p (e b)", p=P)),
            (m.dtb[:, :], w["L0_attn_dt_bias"].rearrange("e h -> (e h)").unsqueeze(0).to_broadcast([P, MEH])),
            (m.aneg[:, :], w["L0_attn_A_log"].rearrange("e h -> (e h)").unsqueeze(0).to_broadcast([P, MEH])),
            (m.dsk[:, :], w["L0_attn_D_skip"].rearrange("e h -> (e h)").unsqueeze(0).to_broadcast([P, MEH])),
        ]
        prepare(k, S, k.mw[:, :], NM, loads)
        with ExitStack() as inner:
            mamba_scalars(k, m, k.scope(inner))
        with ExitStack() as inner:
            mamba_groups(k, m, k.scope(inner))


class Weights:
    pass


def mamba_scalars(k, m, S):
    nc = k.nc
    N = NT * MEH
    v, av, u, dt, q, z0 = (S(n, [P, N]) for n in ("v", "av", "u", "dt", "q", "z0"))
    mx, sm, parts = S("mx", [P, NT]), S("sm", [P, NT]), S("parts", [P, NT, P], BF16)
    parts_ready, rows_turned, rows_copied = (k.counter(f"scalars_{n}") for n in ("parts_ready", "rows_turned", "rows_copied"))
    consts, own, to_act, acted, a_ready, summed = (
        k.counter(f"scalars_{n}") for n in ("constants", "vector_step", "to_scalar", "scalar_step", "a_ready", "summed"))
    lg = k.logits[:, 0:NT * NM].rearrange("p (t n) -> p t n", n=NM)
    by_head = lambda t: t[:, :].rearrange("p (t n) -> p t n", n=MEH)
    ps_acs, ps_tot = k.ps[:, 0, :], k.ps[:, 1, :]

    k.start()
    with nc.Block() as block:
        @block.gpsimd
        def _(pool):
            G = nc.gpsimd
            do = Chain(pool, consts)
            do(G.affine_select(out=m.tri[:, :], in_=k.ones[:, :], compare_op=ALU.is_ge, fill=0.0, base=0,
                               pattern=[[1, P]], channel_multiplier=-1))
            do(G.tensor_copy(m.identb[:, :], k.ident[:, :]))
            do(G.memset(m.future[:, :, :], 0.0))
            do(G.affine_select(out=m.future[:, :, :], in_=m.future[:, :, :], compare_op=ALU.is_ge, fill=-1e30,
                               base=0, pattern=[[0, MH], [1, P]], channel_multiplier=-1))
            do(G.memset(m.pickA[:, :, :], 0.0))
            do(G.memset(m.pickQ[:, :, :], 0.0))
            for part in range(3):
                do(G.affine_select(out=m.pickA[:, :, :], in_=m.pickA[:, :, :], compare_op=ALU.not_equal, fill=1.0,
                                   base=-MEH * part, pattern=[[-1, MEH], [0, P]], channel_multiplier=1))
                pq = m.pickQ[:, :, :].rearrange("p e (h l) -> p e h l", h=MH)
                do(G.affine_select(out=pq, in_=pq, compare_op=ALU.not_equal, fill=1.0, base=-MEH * (3 + part),
                                   pattern=[[-MH, ME], [-1, MH], [0, P]], channel_multiplier=1))
            do(G.memset(m.keep[:, :], 1.0))
            do(G.memset(m.keep[:, :].rearrange("p (b g) -> p b g", b=BATCH)[:, :, 0:1], 0.0))

        @block.vector
        def _(dve):
            V = nc.vector
            do = Chain(dve, own)

            def on_scalar(step):
                dve.sem_inc(to_act.sem, 1)
                dve.wait_ge(acted.sem, acted.at(step))

            rout = m.rout[:, :].rearrange("p (t e) -> p t e", e=ME)
            do(V.memset(parts[:, :, :], 0.0))
            do(V.tensor_reduce(mx[:, :], lg[:, :, 0:ME], AX.X, ALU.max))
            do(V.tensor_tensor(rout, lg[:, :, 0:ME], bcast(mx[:, :], 2, ME), ALU.subtract))
            do(V.tensor_tensor(by_head(v), lg[:, :, ME:NM], bcast(m.dtb[:, :], 1, NT), ALU.add))
            do(V.scalar_tensor_tensor(av[:, :], v[:, :], -1.0, v[:, :], ALU.mult, ALU.max))
            on_scalar(3)
            do(V.tensor_reduce(sm[:, :], rout, AX.X, ALU.add))
            do(V.reciprocal(sm[:, :], sm[:, :]))
            do(V.tensor_tensor(rout, rout, bcast(sm[:, :], 2, ME), ALU.mult))
            do(V.tensor_scalar(av[:, :], u[:, :], 1.0, None, ALU.add))
            on_scalar(4)
            do(V.tensor_scalar(av[:, :], av[:, :], -1.0, None, ALU.add))
            do(V.tensor_scalar(z0[:, :], av[:, :], 0.0, None, ALU.is_equal))
            do(V.tensor_add(av[:, :], av[:, :], z0[:, :]))
            do(V.reciprocal(av[:, :], av[:, :]))
            do(V.tensor_mul(dt[:, :], dt[:, :], av[:, :]))
            do(V.tensor_add(dt[:, :], dt[:, :], z0[:, :]))
            do(V.tensor_mul(dt[:, :], dt[:, :], u[:, :]))
            do(V.scalar_tensor_tensor(dt[:, :], v[:, :], 0.0, dt[:, :], ALU.max, ALU.add))
            do(V.tensor_scalar(u[:, :], dt[:, :], 1e-19, None, ALU.max))
            V.scalar_tensor_tensor(by_head(v), by_head(dt), -1.0, bcast(m.aneg[:, :], 1, NT), ALU.mult, ALU.mult
                                   ).then_inc(a_ready.sem, 1)
            on_scalar(5)
            dve.wait_ge(summed.sem, summed.at(1))
            acs = dt
            do(V.tensor_copy(acs[:, :], ps_acs))
            do(V.tensor_sub(q[:, :], q[:, :], acs[:, :]))
            do(V.tensor_tensor(av[:, :], q[:, :], ps_tot, ALU.add))
            on_scalar(8)
            for t in (m.ea, m.cd):
                first = t[:, :].rearrange("p (b c n) -> p b c n", b=BATCH, n=MEH)[:, :, 0, :]
                do(V.memset(first, 0.0))
            for src, first in ((acs, 0), (q, 3)):
                for part in range(3):
                    out = parts[:, :, (first + part) * MEH:(first + part + 1) * MEH]
                    do(V.tensor_copy(out, by_head(src)))
                    if part < 2:
                        do(V.tensor_tensor(by_head(src), by_head(src), out, ALU.subtract))
            dve.sem_inc(parts_ready.sem, 1)
            do(V.tensor_scalar(m.cw[:, :, :], m.cw[:, :, :], 0.5, None, ALU.mult))
            do(V.tensor_scalar(m.cb[:, :], m.cb[:, :], 0.5, None, ALU.mult))
            do(V.tensor_scalar(m.rout[:, :], m.rout[:, :], 0.5, None, ALU.mult))
            for e in range(ME):
                for b in range(2):
                    do(V.tensor_scalar(m.wout[:, e, b, :], m.wout[:, e, b, :], m.nw[:, e * 2 + b:e * 2 + b + 1],
                                       None, ALU.mult))
            for n in range(MEH):
                do(V.tensor_scalar(m.diagD[:, n, :], k.ident[:, :], m.dsk[:, n:n + 1], None, ALU.mult))
            k.scalar_steps = do.n
            dve.wait_ge(consts.sem, consts.at(14))

        @block.scalar
        def _(act):
            do = Chain(act, acted)
            act.wait_ge(to_act.sem, to_act.at(1))
            do(nc.scalar.activation(m.rout[:, :], m.rout[:, :], ACT.Exp))
            do(nc.scalar.activation(u[:, :], av[:, :], ACT.Exp, scale=-1.0))
            do(nc.scalar.activation(m.aneg[:, :], m.aneg[:, :], ACT.Exp))
            act.wait_ge(to_act.sem, to_act.at(2))
            do(nc.scalar.activation(dt[:, :], av[:, :], ACT.Ln))
            act.wait_ge(to_act.sem, to_act.at(3))
            do(nc.scalar.activation(q[:, :], u[:, :], ACT.Ln))
            act.wait_ge(to_act.sem, to_act.at(4))
            do(nc.scalar.activation(m.wst[:, :], av[:, :], ACT.Exp))
            do(nc.scalar.activation(m.ea[:, :], dt[:, :], ACT.Exp))
            do(nc.scalar.activation(m.cd[:, :], ps_tot, ACT.Exp))
            with act.Fori(0, NG // 2) as i:
                for r in range(2):
                    g = i * 2 + r
                    act.wait_ge(rows_turned.sem, rows_turned.at(g + 1))
                    nc.scalar.copy(m.rows[:, ds(g * GRP * P, GRP * P)], k.ps[:, 2 + r, :]).then_inc(rows_copied.sem, 1)
            act.wait_ge(rows_copied.sem, rows_copied.at(NG))

        @block.tensor
        def _(pe):
            pe.wait_ge(consts.sem, consts.at(1))
            pe.wait_ge(a_ready.sem, a_ready.at(1))
            nc.tensor.matmul(ps_acs, m.tri[:, :], v[:, :], start=True, stop=True)
            nc.tensor.matmul(ps_tot, k.ones[:, :], v[:, :], start=True, stop=True).then_inc(summed.sem, 1)
            pe.wait_ge(consts.sem, consts.at(2))
            pe.wait_ge(parts_ready.sem, parts_ready.at(1))
            with pe.Fori(0, NG // 2) as i:
                for r in range(2):
                    g = i * 2 + r
                    pe.wait_ge(rows_copied.sem, rows_copied.at(g - 1))
                    k.settle(pe)
                    for j in range(GRP):
                        ins = nc.tensor.matmul(k.ps[:, 2 + r, j * P:(j + 1) * P],
                                               parts[:, ds(g * GRP + j, 1), :].rearrange("p a n -> p (a n)"),
                                               m.identb[:, :], start=True, stop=True)
                    ins.then_inc(rows_turned.sem, 1)
    parts_ready.close(1)
    rows_turned.close(NG)
    rows_copied.close(NG)
    own.close(k.scalar_steps)
    consts.close(14)
    to_act.close(4)
    acted.close(8)
    a_ready.close(1)
    summed.close(1)


def mamba_groups(k, m, S):
    nc = k.nc
    NU = GRP * ME
    NB = CW // P
    GT = GRP * P
    AHEAD = 7
    xc = S("xc", [P, GT])
    xb, cv, tails = S("xb", [P, 2, TAPS - 1 + GT]), S("cv", [P, 4, GT]), S("tails", [P, ME * NB, TAPS - 1])
    th = S("th", [P, 2, GT])
    xbc, sz = S("xbc", [P, ME, NB, GT]), S("sz", [P, ME, GRP, ZW])
    state, carried = S("state", [P, ME, ZW]), S("carried", [P, 2, ZW])
    XB, L, M, Xw = S("XB", [P, 2, ZW + P]), S("L", [P, 2, MH * P]), S("M", [P, 2, MH * P]), S("Xw", [P, 2, ZW])
    t1, t2, y2, yT, sq = S("t1", [P, ZW]), S("t2", [P, ZW]), S("y2", [P, 2, ZW]), S("yT", [P, 2, ZW]), S("sq", [P, ZW])
    ss, rs, gain = S("ss", [P, 2]), S("rs", [P, 2]), S("gain", [P, 2])

    names = ("proj", "copied", "conv", "tanh", "half_silu", "silu", "z", "z_tanh", "z_gate")
    a = {n: k.counter(f"piece_{n}") for n in names}
    own, xc_ready = k.counter("piece_vector_step"), k.counter("group_xc_ready")
    names = ("x_turned", "cb", "exponent", "XB", "L", "M", "Xw", "y", "s", "carried", "state", "y2", "squared",
             "yT_turned", "yT", "out", "gain", "added")
    b = {n: k.counter(f"unit_{n}") for n in names}
    yown, gown, init = k.counter("unit_y_step"), k.counter("unit_gain_step"), k.counter("group_init")

    bankX, bankL, bankCB, bankY, bankS, bankYT, bankP, bankZ = (k.ps[:, i, :] for i in range(8))
    bankO = bankYT[:, ZW:ZW + D]
    heads = lambda t: t.rearrange("p (h d) -> p h d", h=MH)

    def inc(ins, sig):
        ins.then_inc(sig.sem, 1)

    def wait(eng, sig, n):
        eng.wait_ge(sig.sem, sig.at(n))

    k.start()
    with nc.Block() as block:
        @block.tensor
        def _(pe):
            def project(g, u):
                e, blk = u // GRP, u % GRP
                n = g * NU + u
                wait(pe, a["copied"], n)
                inc(nc.tensor.matmul(bankP, m.win[:, e, ZW + blk * P:ZW + (blk + 1) * P], k.xnT[:, ds(g * GT, GT)],
                                     start=True, stop=True), a["proj"])
                if u == 0:
                    wait(pe, xc_ready, g + 1)
                wait(pe, a["z_gate"], n)
                inc(nc.tensor.matmul(bankZ[:, 0:ZW], xc[:, blk * P:(blk + 1) * P], m.win[:, e, 0:ZW],
                                     start=True, stop=True), a["z"])

            def open_unit(g, u):
                e, j = u // GRP, u % GRP
                n = g * NU + u
                cols = slice(j * P, (j + 1) * P)
                if j == 0:
                    wait(pe, a["silu"], n + NB)
                wait(pe, b["XB"], n)
                for blk in range(3):
                    ins = nc.tensor.transpose(bankX[:, blk * P:(blk + 1) * P], xbc[:, e, blk, cols], k.ident[:, :])
                inc(ins, b["x_turned"])
                wait(pe, b["L"], n)
                k.settle(pe)
                rows = m.rows[:, ds((g * GRP + j) * P, P)]
                nc.tensor.matmul(bankL, m.identb[:, :], m.future[:, :, :].rearrange("p h l -> p (h l)"),
                                 start=True, stop=False, skip_group_check=True)
                nc.tensor.matmul(bankL, rows, m.pickQ[:, e, :], start=False, stop=False, skip_group_check=True)
                for h in range(MH):
                    ins = nc.tensor.matmul(bankL[:, h * P:(h + 1) * P], m.pickA[:, e * MH + h, :], rows,
                                           start=False, stop=(h == MH - 1), skip_group_check=True)
                inc(ins, b["exponent"])
                wait(pe, b["M"], n)
                inc(nc.tensor.matmul(bankCB[:, 0:P], xbc[:, e, 2, cols], xbc[:, e, 3, cols], start=True, stop=True), b["cb"])

            def mix_unit(g, u):
                e, j = u // GRP, u % GRP
                n, r = g * NU + u, u % 2
                wait(pe, b["M"], n + 1)
                wait(pe, b["XB"], n + 1)
                wait(pe, b["Xw"], n + 1)
                wait(pe, b["state"], n)
                inc(nc.tensor.matmul(bankS[:, 0:ZW], XB[:, r, ZW:ZW + P], Xw[:, r, :], start=True, stop=True), b["s"])
                wait(pe, b["y2"], n)
                for h in range(MH):
                    cols = slice(h * HD, (h + 1) * HD)
                    nc.tensor.matmul(bankY[:, cols], M[:, r, h * P:(h + 1) * P], XB[:, r, cols], start=True, stop=False)
                    nc.tensor.matmul(bankY[:, cols], m.diagD[:, e * MH + h, :], XB[:, r, cols], start=False, stop=True)
                inc(nc.tensor.matmul(bankY[:, ZW:2 * ZW], xbc[:, e, 3, j * P:(j + 1) * P], state[:, e, :],
                                     start=True, stop=True), b["y"])

            def turn_unit(g, u):
                n, r = g * NU + u, u % 2
                wait(pe, b["y2"], n + 1)
                wait(pe, b["added"], n)
                for blk in range(2):
                    ins = nc.tensor.transpose(bankYT[:, blk * P:(blk + 1) * P], y2[:, r, blk * P:(blk + 1) * P], k.ident[:, :])
                inc(ins, b["yT_turned"])

            def out_unit(g, u):
                n, r, e = g * NU + u, u % 2, u // GRP
                wait(pe, b["yT"], n + 1)
                for blk in range(2):
                    ins = nc.tensor.matmul(bankO, yT[:, r, blk * P:(blk + 1) * P], m.wout[:, e, blk, :],
                                           start=(blk == 0), stop=(blk == 1))
                inc(ins, b["out"])

            def step(at):
                for stage, d in ((project, AHEAD), (open_unit, 1), (turn_unit, -1), (mix_unit, 0), (out_unit, -1)):
                    if at(d):
                        stage(*at(d))
            wait(pe, init, 1)
            weave(pe, NG, NU, AHEAD, 1, step)

        @block.scalar
        def _(act):
            A = nc.scalar

            def copy_piece(g, u):
                e, blk, r = u // GRP, u % GRP, u % 2
                n, c = g * NU + u, e * NB + blk
                if u == 0:
                    wait(act, a["z"], n)
                    inc(A.copy(xc[:, :], k.xnT[:, ds(g * GT, GT)]), xc_ready)
                wait(act, a["proj"], n + 1)
                wait(act, a["conv"], n - 1)
                A.copy(xb[:, r, TAPS - 1:TAPS - 1 + GT], bankP)
                wait(act, a["silu"], n - 3)
                inc(A.activation(cv[:, blk, :], bankP, ACT.Identity, scale=m.cw[:, c, TAPS - 1:TAPS],
                                 bias=m.cb[:, c:c + 1]), a["copied"])
                wait(act, a["z"], n + 1)
                inc(A.activation(sz[:, e, blk, :], bankZ[:, 0:ZW], ACT.Tanh, scale=0.5), a["z_tanh"])

            def tanh_piece(g, u):
                n, r, blk = g * NU + u, u % 2, u % GRP
                wait(act, a["conv"], n + 1)
                wait(act, a["silu"], n - 1)
                inc(A.activation(th[:, r, :], cv[:, blk, :], ACT.Tanh), a["tanh"])

            def open_unit(g, u):
                n, r = g * NU + u, u % 2
                wait(act, b["x_turned"], n + 1)
                wait(act, b["y"], n - 1)
                inc(A.copy(XB[:, r, :], bankX[:, 0:ZW + P]), b["XB"])
                wait(act, b["exponent"], n + 1)
                wait(act, b["M"], n - 1)
                inc(A.activation(L[:, r, :], bankL, ACT.Exp), b["L"])

            def close_unit(g, u):
                n, r = g * NU + u, u % 2
                wait(act, b["yT_turned"], n + 1)
                wait(act, b["out"], n - 1)
                inc(A.copy(yT[:, r, :], bankYT[:, 0:ZW]), b["yT"])
                wait(act, b["gain"], n - 1)
                wait(act, b["squared"], n)
                inc(A.activation(sq[:, :], y2[:, r, :], ACT.Square, scale=0.5 * float(ZW) ** -0.5,
                                 accum_out=ss[:, r:r + 1]), b["squared"])

            def step(at):
                for stage, d in ((copy_piece, AHEAD), (open_unit, 1), (close_unit, -1), (tanh_piece, AHEAD - 1)):
                    if at(d):
                        stage(*at(d))
            A.activation(k.spare[:, 1:2], k.zero[:, 0:1], ACT.Exp)
            weave(act, NG, NU, AHEAD, 1, step)

        @block.vector
        def _(dve):
            V = nc.vector

            def convolve(g, u):
                e, blk, r = u // GRP, u % GRP, u % 2
                n, c = g * NU + u, e * NB + blk
                tap = lambda i: V.scalar_tensor_tensor(cv[:, blk, :], xb[:, r, i:i + GT], m.cw[:, c, i:i + 1],
                                                       cv[:, blk, :], ALU.mult, ALU.add)
                wait(dve, own, n * 4)
                inc(V.tensor_scalar(xb[:, r, 0:TAPS - 1], tails[:, c, :], m.keep[:, ds(g, 1)], None, ALU.mult), own)
                wait(dve, a["copied"], n + 1)
                wait(dve, own, n * 4 + 1)
                inc(tap(0), own)
                inc(V.tensor_copy(tails[:, c, :], xb[:, r, GT:GT + TAPS - 1]), own)
                wait(dve, own, n * 4 + 3)
                inc(tap(1), own)
                wait(dve, own, n * 4 + 4)
                inc(tap(2), a["conv"])

            def gate_piece(g, u):
                e, j = u // GRP, u % GRP
                n = g * NU + u
                wait(dve, a["z_tanh"], n + 1)
                inc(V.scalar_tensor_tensor(sz[:, e, j, :], sz[:, e, j, :], 1.0, bankZ[:, 0:ZW], ALU.add, ALU.mult),
                    a["z_gate"])

            def matrices(g, u):
                n, r = g * NU + u, u % 2
                wait(dve, b["L"], n + 1)
                wait(dve, b["cb"], n + 1)
                wait(dve, b["y"], n - 1)
                inc(V.tensor_tensor(heads(M[:, r, :]), heads(L[:, r, :]), bcast(bankCB[:, 0:P], 1, MH), ALU.mult), b["M"])

            def gated(g, u):
                e, j = u // GRP, u % GRP
                n, r = g * NU + u, u % 2
                wait(dve, b["s"], n + 1)
                wait(dve, b["carried"], n + 1)
                wait(dve, b["y"], n + 1)
                inc(V.tensor_tensor(heads(t1[:, :]), heads(bankY[:, ZW:2 * ZW]),
                                    bcast(m.ea[:, ds((g * GRP + j) * MEH + e * MH, MH)], 2, HD), ALU.mult), yown)
                inc(V.tensor_tensor(state[:, e, :], bankS[:, 0:ZW], carried[:, r, :], ALU.add), b["state"])
                wait(dve, yown, n * 2 + 1)
                inc(V.tensor_tensor(t2[:, :], t1[:, :], bankY[:, 0:ZW], ALU.add), yown)
                wait(dve, yown, n * 2 + 2)
                wait(dve, b["squared"], n - 1)
                wait(dve, b["yT_turned"], n - 1)
                inc(V.tensor_tensor(y2[:, r, :], t2[:, :], sz[:, e, j, :], ALU.mult), b["y2"])

            def add(g, u):
                j = u % GRP
                n, r = g * NU + u, u % 2
                wait(dve, b["out"], n + 1)
                wait(dve, b["gain"], n + 1)
                xt = k.x[:, ds((g * GRP + j) * D, D)]
                inc(V.scalar_tensor_tensor(xt, bankO, gain[:, r:r + 1], xt, ALU.mult, ALU.add), b["added"])

            def step(at):
                for stage, d in ((convolve, AHEAD - 1), (gate_piece, AHEAD), (matrices, 1), (gated, 0), (add, -1)):
                    if at(d):
                        stage(*at(d))
            V.memset(tails[:, :, :], 0.0)
            inc(V.memset(state[:, :, :], 0.0), init)
            wait(dve, init, 1)
            weave(dve, NG, NU, AHEAD, 1, step)

        @block.gpsimd
        def _(pool):
            G = nc.gpsimd

            def weigh(g, u):
                e, j = u // GRP, u % GRP
                n, r = g * NU + u, u % 2
                wait(pool, b["XB"], n + 1)
                wait(pool, b["s"], n - 1)
                k.settle(pool)
                inc(G.tensor_tensor(heads(Xw[:, r, :]), heads(XB[:, r, 0:ZW]),
                                    bcast(m.wst[:, ds((g * GRP + j) * MEH + e * MH, MH)], 2, HD), ALU.mult), b["Xw"])

            def carry(g, u):
                e, j = u // GRP, u % GRP
                n, r = g * NU + u, u % 2
                wait(pool, b["state"], n)
                k.settle(pool)
                inc(G.tensor_tensor(heads(carried[:, r, :]), heads(state[:, e, :]),
                                    bcast(m.cd[:, ds((g * GRP + j) * MEH + e * MH, MH)], 2, HD), ALU.mult), b["carried"])

            def normalise(g, u):
                e, j = u // GRP, u % GRP
                n, r = g * NU + u, u % 2
                wait(pool, b["squared"], n + 1)
                wait(pool, b["added"], n - 1)
                inc(G.tensor_tensor(rs[:, r:r + 1], ss[:, r:r + 1], k.eps[:, 0:1], ALU.add), gown)
                wait(pool, gown, n * 2 + 1)
                inc(G.tensor_tensor(rs[:, r:r + 1], rs[:, r:r + 1], k.minus_half[:, 0:1], ALU.pow), gown)
                wait(pool, gown, n * 2 + 2)
                k.settle(pool)
                inc(G.tensor_tensor(gain[:, r:r + 1], rs[:, r:r + 1], m.rout[:, ds((g * GRP + j) * ME + e, 1)],
                                    ALU.mult), b["gain"])

            def silu_piece(g, u):
                e, blk, r = u // GRP, u % GRP, u % 2
                n = g * NU + u
                wait(pool, a["tanh"], n + 1)
                inc(G.tensor_tensor(th[:, r, :], th[:, r, :], cv[:, blk, :], ALU.mult), a["half_silu"])
                wait(pool, a["half_silu"], n + 1)
                inc(G.tensor_tensor(xbc[:, e, blk, :], th[:, r, :], cv[:, blk, :], ALU.add), a["silu"])

            def step(at):
                for stage, d in ((carry, 0), (weigh, 1), (normalise, -1), (silu_piece, AHEAD - 2)):
                    if at(d):
                        stage(*at(d))
            wait(pool, init, 1)
            weave(pool, NG, NU, AHEAD, 1, step)

    for s in a.values():
        s.close(NG * NU)
    own.close(NG * NU * 4)
    xc_ready.close(NG)
    for s in b.values():
        s.close(NG * NU)
    yown.close(NG * NU * 2)
    gown.close(NG * NU * 2)
    init.close(1)


def setup(k, w):
    nc = k.nc
    k.counter("settled")
    loads, made, own = k.counter("setup_loads", 16), k.counter("setup_made"), k.counter("setup_step")
    S = k.sb
    k.x, k.xnT = S("x", [P, NT * D]), S("xnT", [P, TOK])
    k.xn4, k.xt4 = S("xn4", [P, 2, GRP, D]), S("xt4", [P, 2, GRP * P])
    k.stat, k.mv, k.rstd = S("stat", [P, 2, GRP, 6]), S("mv", [P, 2, GRP, 2]), S("rstd", [P, 2, GRP])
    k.logits = S("logits", [P, NT * NM])
    k.ident, k.ones, k.zero = S("ident", [P, P]), S("ones", [P, P]), S("zero", [P, 1])
    k.ones_bf, k.zeros_bf, k.before = S("ones_bf", [P, P], BF16), S("zeros_bf", [P, 2 * SLOTS2], BF16), S("before", [P, P], BF16)
    k.iota, k.lane, k.tile_of = S("iota", [P, P]), S("lane", [P, 1]), S("tile_of", [P, 2 * NT])
    k.falling, k.carry, k.minus_half = S("falling", [P, NE]), S("carry", [P, NE * NT]), S("minus_half", [P, GRP])
    k.mw = S("mw", [P, NM])
    k.spare, k.eps = S("spare", [P, 4]), S("eps", [P, GRP])
    k.rt = [S(f"rt{i}", [P, NE * NT]) for i in range(5)]
    k.best, k.small, k.gate = S("best", [P, 2, NT]), S("small", [P, 2 * NT]), S("gate", [P, 2, NT])
    k.marks = S("marks", [P, NE * NT], BF16)
    k.n_int, k.e8 = S("n_int", [P, NE], I32), S("e8", [P, 3, NE])
    k.posf, k.pos, k.hi_int = S("posf", [P, 2 * NT]), S("pos", [P, 2 * NT], U32), S("hi_int", [P, 2 * NT], I32)
    k.hi, k.lo, k.erow = S("hi", [P, 2 * NT]), S("lo", [P, 2 * NT]), S("erow", [P, SLOTS2])
    k.slot_expert, k.slot_token = S("slot_expert", [P, SLOTS2], I32), S("slot_token", [P, SLOTS2], U32)
    k.oh_lane, k.oh_slot = S("oh_lane", [P, 2, GRP, P], BF16), S("oh_slot", [P, 2, GRP, 2 * SLOTS2], BF16)
    k.iota_bf = S("iota_bf", [P, P], BF16)
    k.wg0, k.wg1, k.bg = S("wg0", [P, NE]), S("wg1", [P, NE]), S("bg", [P, NE])
    k.index = S("index", [P, 4 * GRP], U32)
    k.ps = k.ctx.enter_context(nc.psum_tensor("ps", [P, 8, 512], F32))
    k.xn_rows = nc.dram_tensor("xn_rows", [TOK, D], F32, kind="Internal").ap()
    k.y_rows = nc.dram_tensor("y_rows", [SLOTS2 * P, D], F32, kind="Internal").ap()

    copies = [
        (k.x[:, :].rearrange("p (t d) -> p t d", t=NT), w["L0_attn_x"].rearrange("b (t p) d -> p (b t) d", p=P)),
        (k.wg0[:, :], w["L0_ffn_Wg"]),
        (k.wg1[:, :], w["L1_ffn_Wg"]),
        (k.bg[:, :], w["L1_ffn_bg"].unsqueeze(0).to_broadcast([P, NE])),
        (k.mw[:, 0:ME], w["L0_attn_router_w"]),
        (k.mw[:, ME:NM].rearrange("p (e h) -> p e h", e=ME), w["L0_attn_in_w"].rearrange("e d n -> d e n")[:, :, ZW + CW:]),
    ]

    k.start()
    with nc.Block() as block:
        @block.sync
        def _(sp):
            for dst, src in copies:
                sp.dma_start(dst, src, allow_slow_non_contiguous=True).then_inc(loads.sem, 16)
            sp.wait_ge(loads.sem, loads.at(len(copies)))

        @block.gpsimd
        def _(pool):
            G = nc.gpsimd
            do = Chain(pool, made)
            do(G.memset(k.ones[:, :], 1.0))
            do(G.affine_select(out=k.ident[:, :], in_=k.ones[:, :], compare_op=ALU.is_equal, fill=0.0, base=0,
                               pattern=[[1, P]], channel_multiplier=-1))
            do(G.affine_select(out=k.before[:, :], in_=k.ones[:, :], compare_op=ALU.is_gt, fill=0.0, base=0,
                               pattern=[[1, P]], channel_multiplier=-1))
            do(G.memset(k.zero[:, :], 0.0))
            do(G.memset(k.minus_half[:, :], -0.5))
            do(G.memset(k.eps[:, :], EPS))
            do(G.iota(k.iota[:, :], pattern=[[1, P]], base=0, channel_multiplier=0, allow_small_or_imprecise_dtypes=True))
            do(G.tensor_copy(k.iota_bf[:, :], k.iota[:, :]))
            do(G.iota(k.lane[:, :], pattern=[[1, 1]], base=0, channel_multiplier=1, allow_small_or_imprecise_dtypes=True))
            do(G.iota(k.tile_of[:, :], pattern=[[0, 2], [1, NT]], base=0, channel_multiplier=0, allow_small_or_imprecise_dtypes=True))
            do(G.iota(k.falling[:, :], pattern=[[-1, NE]], base=NE, channel_multiplier=0, allow_small_or_imprecise_dtypes=True))

        @block.vector
        def _(dve):
            V = nc.vector
            do = Chain(dve, own)
            do(V.memset(k.ones_bf[:, :], 1.0))
            do(V.memset(k.zeros_bf[:, :], 0.0))
            do(V.memset(k.carry[:, :], 1.0))
            do(V.memset(k.carry[:, :].rearrange("p (e t) -> p e t", e=NE)[:, :, 0:1], 0.0))


def store(k, S, out):
    nc = k.nc
    top, slots = k.pending
    NR = GRP * top
    index_ready, added, k.first_added = (k.counter(f"back_{n}") for n in ("index_ready", "added", "first_added"))
    fetched = [k.counter(f"back_fetched{n}", 16, lead=0) for n in range(2 * NR)]
    back = S("back", [P, 2 * NR, D]) if top else None
    out_stored = k.counter("output_stored", 16)
    by_group = out.rearrange("b t d -> (b t) d").rearrange("(g j p) d -> p g j d", p=P, j=GRP)
    nothing = lambda g, r, i: None
    k.start()
    with nc.Block() as block:
        @block.gpsimd
        def _(pool):
            in_turn(pool, NG, lambda g, r, i: fetch_back(k, pool, g, r, top, slots, back, index_ready, fetched, added),
                    nothing)

        @block.vector
        def _(dve):
            in_turn(dve, NG, lambda g, r, i: take_back(k, dve, g, r, i, top, back, fetched, added), nothing)

        @block.sync
        def _(sp):
            for g in range(NG):
                if top:
                    sp.wait_ge(added.sem, added.at(g + 1))
                sp.dma_start(by_group[:, g], k.x[:, g * GRP * D:(g + 1) * GRP * D].rearrange("p (j d) -> p j d", j=GRP)
                             ).then_inc(out_stored.sem, 16)
            sp.wait_ge(out_stored.sem, out_stored.at(NG))


SLOTS1 = (TOK + NE * (P - 1)) // P
SLOTS2 = (2 * TOK + NE * (P - 1)) // P


def macaron(nc, w, out):
    with ExitStack() as ctx:
        k = Bench(nc, ctx)
        setup(k, w)
        for stage in STAGES:
            {"ffn0": ffn0, "ffn1": ffn1, "attn": attend, "mamba": mamba}[stage](k, w)
        with ExitStack() as stack:
            store(k, k.scope(stack), out)


def ffn0(k, w):
    with ExitStack() as stack:
        S = k.scope(stack)
        k.w12, k.w3 = S("w12", [P, NE + 1, 2 * FF]), S("w3", [P, NE + 1, FB, D])
        k.gl, k.inner = S("gl", [P, 2, GRP * P]), S("inner", [P, 2, FB, GRP * P])
        k.rows_in, k.gT, k.w_slot = S("rows_in", [P, 4, D]), S("gT", [P, 2, P]), S("w_slot", [P, 2, 2 * FF])
        k.inner_slot, k.y = S("inner_slot", [P, 4, FF]), S("y", [P, 4, D])
        loads = [
            (k.w12[:, NE, 0:FF], w["L0_ffn_w1s"]),
            (k.w12[:, NE, FF:2 * FF], w["L0_ffn_w2s"]),
            (k.w3[:, NE], w["L0_ffn_w3s"].rearrange("(b p) d -> p b d", p=P)),
            (k.w12[:, 0:NE, 0:FF], w["L0_ffn_W1"].rearrange("e d f -> d e f")),
            (k.w12[:, 0:NE, FF:2 * FF], w["L0_ffn_W2"].rearrange("e d f -> d e f")),
            (k.w3[:, 0:NE].rearrange("p e b d -> p (e b) d"), w["L0_ffn_W3"].rearrange("e (b p) d -> p (e b) d", p=P)),
        ]
        prepare(k, S, k.wg0[:, :], NE, loads)
        route(k, 1, SLOTS1, False)
        shared(k, SLOTS1)
        experts(k, 1, SLOTS1)


def ffn1(k, w):
    nc = k.nc
    done = k.counter("router_biased")
    with ExitStack() as stack:
        S = k.scope(stack)
        k.w1, k.w2 = S("w1", [P, NE, FF]), S("w2", [P, NE, FB, D])
        k.b1, k.b2 = S("b1", [P, NE * FB]), S("b2", [P, NE * D])
        k.rows_in, k.gT, k.w_slot = S("rows_in", [P, 4, D]), S("gT", [P, 2, P]), S("w_slot", [P, 2, FF])
        k.inner_slot, k.hb, k.y = S("inner_slot", [P, 4, FF]), S("hb", [P, 4, FF]), S("y", [P, 4, D])
        loads = [
            (k.w1[:, :, :], w["L1_ffn_W1"].rearrange("e d f -> d e f")),
            (k.b2[:, :], w["L1_ffn_b2"].rearrange("e d -> (e d)").unsqueeze(0).to_broadcast([P, NE * D])),
            (k.w2[:, :].rearrange("p e b d -> p (e b) d"), w["L1_ffn_W2"].rearrange("e (b p) d -> p (e b) d", p=P)),
            (k.b1[:, :], w["L1_ffn_b1"].rearrange("e (b p) -> p (e b)", p=P)),
        ]
        prepare(k, S, k.wg1[:, :], NE, loads)
        k.start()
        with nc.Block() as block:
            @block.vector
            def _(dve):
                l3 = k.logits[:, 0:NT * NE].rearrange("p (t e) -> p t e", e=NE)
                nc.vector.tensor_tensor(l3, l3, bcast(k.bg[:, :], 1, NT), ALU.add).then_inc(done.sem, 1)
                for e in range(1, NE, 2):
                    nc.vector.tensor_scalar(k.w2[:, e], k.w2[:, e], 0.5, None, ALU.mult).then_inc(done.sem, 1)
                dve.wait_ge(done.sem, done.at(1 + NE // 2))
        done.close(1 + NE // 2)
        route(k, 2, SLOTS2, True)
        experts(k, 2, SLOTS2)


_INS = ['L0_attn_x', 'L0_attn_router_w', 'L0_attn_in_w', 'L0_attn_conv_w', 'L0_attn_conv_b', 'L0_attn_dt_bias',
        'L0_attn_A_log', 'L0_attn_D_skip', 'L0_attn_norm_w', 'L0_attn_out_w', 'L0_ffn_w1s', 'L0_ffn_w2s', 'L0_ffn_w3s',
        'L0_ffn_W1', 'L0_ffn_W2', 'L0_ffn_W3', 'L0_ffn_Wg', 'L1_attn_w_q', 'L1_attn_b_q', 'L1_attn_w_k', 'L1_attn_b_k',
        'L1_ffn_W1', 'L1_ffn_b1', 'L1_ffn_W2', 'L1_ffn_b2', 'L1_ffn_Wg', 'L1_ffn_bg']


def kernel(**inputs):
    import numpy as _np
    import concourse.bacc as _bacc
    from concourse import mybir as _mybir
    from concourse.bass_utils import run_bass_kernel_spmd as _run

    nc = _bacc.Bacc("TRN2", target_bir_lowering=False, num_devices=1)
    arrays, w = {}, {}
    for name in _INS:
        a = _np.ascontiguousarray(inputs[name])
        arrays[f"in_{name}"] = a
        w[name] = nc.dram_tensor(f"in_{name}", a.shape, _mybir.dt.from_np(a.dtype), kind="ExternalInput").ap()
    out = nc.dram_tensor("out_x", (BATCH, SEQ, D), _mybir.dt.float32, kind="ExternalOutput").ap()
    macaron(nc, w, out)
    r = _run(nc, [arrays], core_ids=[0])
    return r.results[0]["out_x"]
```
